# Optimizing a Trainium2 kernel written in Bass

```python
import numpy as np
import jax
import jax.numpy as jnp

def _softmax(x, axis=-1):
    return jax.nn.softmax(x, axis=axis)

def _gelu(x):
    return jax.nn.gelu(x, approximate=True)

def _silu(x):
    return jax.nn.silu(x)

def _sigmoid(x):
    return jax.nn.sigmoid(x)

def _layernorm(x, axis=-1, eps=1e-05):
    m = jnp.mean(x, axis=axis, keepdims=True)
    v = jnp.var(x, axis=axis, keepdims=True)
    return (x - m) / jnp.sqrt(v + eps)

def _scatter_add(tgt, idx, src, axis=0):
    return tgt.at[idx].add(src)

def _segment_sum(src, seg, n):
    return jax.ops.segment_sum(src, seg, n)
kernel_name = 'mk_flamingo_gated_d1_seqx_r2_573eb0'

def setup_inputs(seed: int=0):
    np.random.seed(seed)
    _w = jnp.asarray

    def _rec_inputs():
        import jax
        import jax.numpy as jnp
        _rk = jax.random.key(seed)
        x = 0.0003765 + 1 * jax.random.normal(jax.random.fold_in(_rk, 1), (16, 512, 1024), jnp.float32)
        _lenS = 512 - jax.random.randint(jax.random.fold_in(_rk, 7), (16,), 0, max(1, 512 // 4) + 1, jnp.int32)
        _lenS2 = 512 - jax.random.randint(jax.random.fold_in(_rk, 8), (16,), 0, max(1, 512 // 4) + 1, jnp.int32)
        _ctx_2048P = jax.random.normal(jax.random.fold_in(_rk, 11), (16, 16, 1024), jnp.float32)
        _ctx_2048c = jax.random.dirichlet(jax.random.fold_in(_rk, 511), 0.3 * jnp.ones((16,), jnp.float32), (16, 512))
        _ctx_2048t = jnp.einsum('bsk,bkd->bsd', _ctx_2048c, _ctx_2048P)
        _ctx_2048t = _ctx_2048t * jax.lax.rsqrt(jnp.mean(jnp.square(_ctx_2048t)) + 1e-12) * 0.953939
        ctx_2048 = -0.000292821 + 1.00034 * (_ctx_2048t + 0.3 * jax.random.normal(jax.random.fold_in(_rk, 611), (16, 512, 1024), jnp.float32))
        _g = jax.random.normal(jax.random.fold_in(_rk, 9001), (2, 1), jnp.float32)
        _g = jnp.sign(_g) * jnp.maximum(jnp.abs(_g), 1.0) + (_g == 0) * 1.0
        g_xattn = _g[0]
        g_ffn = _g[1]
        return (x, ctx_2048, g_xattn, g_ffn)
    x, ctx_2048, g_xattn, g_ffn = _rec_inputs()

    def _L0_xattn_setup():
        import jax, jax.numpy as jnp
        import numpy as np
        key = jax.random.key(seed)
        k1, k2, k3, k4, k5 = jax.random.split(key, 5)
        B, D_MODEL, L = (2, 512, 1024)
        HEAD_DIM = 8
        H = D_MODEL // HEAD_DIM
        return {'k': jax.random.normal(k1, (B, D_MODEL, L), dtype=jnp.float32), 'v': jax.random.normal(k2, (B, D_MODEL, L), dtype=jnp.float32), 'q': jax.random.normal(k3, (B, D_MODEL, L), dtype=jnp.float32), 'ssm_kernel': jax.random.normal(k4, (H, L), dtype=jnp.float32), 'D': jax.random.normal(k5, (H,), dtype=jnp.float32), 'head_dim': HEAD_DIM}
    _L0_xattn_all = _L0_xattn_setup()
    _L0_xattn_in = {k: v for k, v in _L0_xattn_all.items() if k in ('ssm_kernel', 'D')}
    del _L0_xattn_all

    def _L0_ffn_setup():
        import jax, jax.numpy as jnp
        import numpy as np
        TOP_K = 2
        CAPACITY_FACTOR = 1.0

        def _ffn(x, w1, w2):
            h = x @ w1
            x1, x2 = jnp.split(h, 2, axis=-1)
            return x1 * jax.nn.silu(x2) @ w2
        key = jax.random.key(seed)
        ks = jax.random.split(key, 6)
        B, S, D, F, E_r, E_s = (4, 1024, 1024, 512, 7, 1)
        sc_in = 1.0 / np.sqrt(D)
        sc_mid = 1.0 / np.sqrt(F)
        return {'x': jax.random.normal(ks[0], (B, S, D), dtype=jnp.float32), 'gate_w': jax.random.normal(ks[1], (D, E_r), dtype=jnp.float32) * sc_in, 'expert_bias': jnp.zeros((E_r,), dtype=jnp.float32), 'shared_w1': jax.random.normal(ks[2], (E_s, D, 2 * F), dtype=jnp.float32) * sc_in, 'shared_w2': jax.random.normal(ks[3], (E_s, F, D), dtype=jnp.float32) * sc_mid, 'routed_w1': jax.random.normal(ks[4], (E_r, D, 2 * F), dtype=jnp.float32) * sc_in, 'routed_w2': jax.random.normal(ks[5], (E_r, F, D), dtype=jnp.float32) * sc_mid}
    _L0_ffn_all = _L0_ffn_setup()
    _L0_ffn_in = {k: v for k, v in _L0_ffn_all.items() if k in ('gate_w', 'expert_bias', 'shared_w1', 'shared_w2', 'routed_w1', 'routed_w2')}
    del _L0_ffn_all
    return {'x': x, 'ctx_2048': ctx_2048, 'g_xattn': g_xattn, 'g_ffn': g_ffn, 'L0_xattn_ssm_kernel': _L0_xattn_in['ssm_kernel'], 'L0_xattn_D': _L0_xattn_in['D'], 'L0_ffn_gate_w': _L0_ffn_in['gate_w'], 'L0_ffn_expert_bias': _L0_ffn_in['expert_bias'], 'L0_ffn_shared_w1': _L0_ffn_in['shared_w1'], 'L0_ffn_shared_w2': _L0_ffn_in['shared_w2'], 'L0_ffn_routed_w1': _L0_ffn_in['routed_w1'], 'L0_ffn_routed_w2': _L0_ffn_in['routed_w2']}

def reference(x, ctx_2048, g_xattn, g_ffn, L0_xattn_ssm_kernel, L0_xattn_D, L0_ffn_gate_w, L0_ffn_expert_bias, L0_ffn_shared_w1, L0_ffn_shared_w2, L0_ffn_routed_w1, L0_ffn_routed_w2):
    import jax
    import jax.numpy as jnp

    def _L0_xattn_ref(k, v, q, ssm_kernel, D, head_dim):
        import jax, jax.numpy as jnp
        import numpy as np
        B, HD, L = k.shape
        H = HD // head_dim
        fft_size = 2 * L
        k_ = k.reshape(B, H, head_dim, L)
        v_ = v.reshape(B, H, head_dim, L)
        q_ = q.reshape(B, H, head_dim, L)
        kv = jnp.einsum('bhil,bhjl->bijhl', k_, v_)
        kv_f = jnp.fft.rfft(kv, n=fft_size)
        kernel_f = jnp.fft.rfft(ssm_kernel, n=fft_size)
        y = jnp.fft.irfft(kv_f * kernel_f, n=fft_size)[..., :L]
        out = y + kv * D[None, None, None, :, None]
        out = jnp.einsum('bijhl,bhil->bjhl', out, q_)
        out = jnp.transpose(out, (0, 2, 1, 3)).reshape(B, H * head_dim, L)
        return out.astype(k.dtype)

    def _L0_ffn_ref(x, gate_w, expert_bias, shared_w1, shared_w2, routed_w1, routed_w2):
        import jax, jax.numpy as jnp
        import numpy as np
        TOP_K = 2
        CAPACITY_FACTOR = 1.0

        def _ffn(x, w1, w2):
            h = x @ w1
            x1, x2 = jnp.split(h, 2, axis=-1)
            return x1 * jax.nn.silu(x2) @ w2
        B, S, D = x.shape
        E_r = gate_w.shape[1]
        T = B * S
        capacity = max(1, int(CAPACITY_FACTOR * T / E_r))
        flat_x = x.reshape(T, D)
        shared_sum = jax.vmap(_ffn, in_axes=(None, 0, 0))(flat_x, shared_w1, shared_w2).sum(0)
        gate_logits = flat_x @ gate_w + expert_bias
        aff = jax.nn.sigmoid(gate_logits)
        _, topk_idx = jax.lax.top_k(aff, TOP_K)
        mask = (topk_idx[:, :, None] == jnp.arange(E_r)[None, None, :]).any(axis=1)
        score = jnp.where(mask, aff, -1.0).T
        _, sel_idx = jax.lax.top_k(score, capacity)
        kept = jnp.take_along_axis(mask.T, sel_idx, axis=1)
        w = jnp.where(kept, jnp.take_along_axis(aff.T, sel_idx, axis=1), 0.0)
        inp = flat_x[sel_idx]
        out = jax.vmap(_ffn)(inp, routed_w1, routed_w2)
        routed_sum = jnp.zeros_like(flat_x).at[sel_idx].add(out * w[:, :, None])
        return (shared_sum + routed_sum).reshape(B, S, D)
    x = x + jnp.tanh(g_xattn[0]) * _L0_xattn_ref(ctx_2048, ctx_2048, _layernorm(x, axis=-1), L0_xattn_ssm_kernel, L0_xattn_D, 8)
    x = x + jnp.tanh(g_ffn[0]) * _L0_ffn_ref(_layernorm(x, axis=-1), L0_ffn_gate_w, L0_ffn_expert_bias, L0_ffn_shared_w1, L0_ffn_shared_w2, L0_ffn_routed_w1, L0_ffn_routed_w2)
    return x

_drawn_inputs = setup_inputs


def setup_inputs(seed=0):
    import zlib

    import numpy as np

    out = dict(_drawn_inputs(seed))
    spreads = {'L0_ffn_expert_bias': (0.0, 0.8)}
    factors = {'L0_ffn_gate_w': 7.734,
     'L0_ffn_shared_w1': 5.918,
     'L0_ffn_shared_w2': 5.914,
     'L0_ffn_routed_w1': 7.207,
     'L0_ffn_routed_w2': 7.21}
    for name, (base, spread) in spreads.items():
        noise = np.random.default_rng([zlib.crc32(name.encode()), seed]).standard_normal(out[name].shape)
        drawn = base * np.exp(spread * noise) if base else spread * noise
        out[name] = jnp.asarray(drawn.astype(out[name].dtype))
    for name, factor in factors.items():
        out[name] = (out[name] * factor).astype(out[name].dtype)
    return out
```

```python
import math
import numpy as np
import concourse.bass as bass
from concourse import mybir
from contextlib import ExitStack

F32 = mybir.dt.float32
F32R = mybir.dt.float32r
I32 = mybir.dt.int32
ALU = mybir.AluOpType
ACT = mybir.ActivationFunctionType
AX = mybir.AxisListType

P = 128
BANK = 512
HD = 8
PAIRS = HD * (HD + 1) // 2
EPS = 1e-5
LN = slice(0, 2)
PAD = 1152


class Pool:

    def __init__(self, nc, ctx, tag):
        self.nc, self.ctx, self.tag = nc, ctx, tag

    def sb(self, name, shape, dt=F32):
        return self.ctx.enter_context(self.nc.sbuf_tensor(f"{self.tag}_{name}", shape, dt))

    def ps(self, name, shape, dt=F32):
        return self.ctx.enter_context(self.nc.psum_tensor(f"{self.tag}_{name}", shape, dt))

    def sem(self, name):
        return self.ctx.enter_context(self.nc.semaphore(f"{self.tag}_{name}"))


def identity_steps(nc, pool, ident, made):
    nc.gpsimd.memset(ident[:, :], 0.0).then_inc(made, 1)
    pool.wait_ge(made, 1)
    nc.gpsimd.affine_select(out=ident[:, :], in_=ident[:, :], compare_op=ALU.not_equal, fill=1.0,
                            base=0, pattern=[[-1, P]], channel_multiplier=1).then_inc(made, 1)


def prepare_filters(nc, ssm_kernel, D, filt_hi, filt_lo, z_d, out):
    H, L = ssm_kernel.shape
    T = z_d.shape[0] - P
    with ExitStack() as ctx:
        m = Pool(nc, ctx, "fil")
        full = m.sb("full", [H, PAD])
        hi = m.sb("hi", [H, PAD], F32R)
        lo = m.sb("lo", [H, PAD], F32R)
        d = m.sb("d", [H, 1])
        zero = m.sb("zero", [P, L])
        cleared, loaded, tapped, rounded, split, zeroed, stored = (
            m.sem(n) for n in ("cleared", "loaded", "tapped", "rounded", "split", "zeroed", "stored"))
        block = ctx.enter_context(nc.Block())

        @block.sync
        def _(sp):
            sp.wait_ge(cleared, 1)
            sp.dma_start(full[:, P - 1:P - 1 + L], ssm_kernel).then_inc(loaded, 16)
            sp.dma_start(d[:, :], D.rearrange("(h a) -> h a", a=1)).then_inc(loaded, 16)
            sp.wait_ge(zeroed, 1)
            sp.dma_start(z_d[T:T + P, :], zero[:, :]).then_inc(stored, 16)
            sp.dma_start(out[T:T + P, :], zero[:, :]).then_inc(stored, 16)
            sp.wait_ge(split, 1)
            sp.dma_start(filt_hi, hi[:, :].bitcast(F32)).then_inc(stored, 16)
            sp.dma_start(filt_lo, lo[:, :].bitcast(F32)).then_inc(stored, 16)
            sp.wait_ge(stored, 64)

        @block.vector
        def _(dve):
            nc.vector.memset(full[:, :], 0.0).then_inc(cleared, 1)
            nc.vector.memset(zero[:, :], 0.0).then_inc(zeroed, 1)
            dve.wait_ge(loaded, 32)
            nc.vector.tensor_tensor(full[:, P - 1:P], full[:, P - 1:P], d[:, :], ALU.add).then_inc(tapped, 1)
            dve.wait_ge(tapped, 1)
            nc.vector.tensor_copy(hi[:, :], full[:, :]).then_inc(rounded, 1)
            dve.wait_ge(rounded, 1)
            nc.vector.tensor_tensor(lo[:, :], full[:, :], hi[:, :].bitcast(F32), ALU.subtract).then_inc(split, 1)


def gated_conv(nc, x, ctx_rev, g_xattn, gate_w, expert_bias, filt_hi, filt_lo, z_d, zT_d, logit_d, out):
    B, S, L = x.shape
    H = S // HD
    NT = L // P
    G = NT // 2
    E = gate_w.shape[1]
    NB = B // 2
    assert B * HD == P and H % 2 == 0 and H >= 6
    off = [sum(HD - r for r in range(i)) for i in range(HD)]

    x_rows = x.rearrange("b (h j) l -> h b j l", j=HD)
    c_rows = ctx_rev.rearrange("b (h j) l -> h b j l", j=HD)
    z_rows = z_d[0:B * S, :].rearrange("(b h j) l -> h b j l", b=B, j=HD)
    o_rows = out[0:B * S, :].rearrange("(b h j) l -> h b j l", b=B, j=HD)

    def toeplitz(filt):
        return bass.AP(filt.tensor, 0, [[PAD, H], [1, P], [1, L]])

    t_hi, t_lo = toeplitz(filt_hi), toeplitz(filt_lo)

    with ExitStack() as ctx:
        m = Pool(nc, ctx, "att")
        xq = m.sb("xq", [P, L])
        cn = m.sb("cn", [P, L])
        kT = m.sb("kT", [P, NT, B, HD])
        qT = [m.sb(f"qT{u}", [P, NT, B, HD]) for u in range(2)]
        kv = m.sb("kv", [P, G, B, PAIRS])
        kv_hi = [m.sb(f"kv_hi{u}", [P, NT, B, PAIRS], F32R) for u in range(2)]
        kv_lo = [m.sb(f"kv_lo{u}", [P, NT, B, PAIRS], F32R) for u in range(2)]
        tz_hi = [m.sb(f"tz_hi{u}", [P, L], F32R) for u in range(2)]
        tz_lo = [m.sb(f"tz_lo{u}", [P, L], F32R) for u in range(2)]
        y = [m.sb(f"y{u}", [P, NT, B, PAIRS]) for u in range(2)]
        prod = m.sb("prod", [P, G * B, HD, HD])
        oT = m.sb("oT", [P, NT, B * HD])
        x1 = [m.sb(f"x1_{u}", [P, L]) for u in range(2)]
        z = [m.sb(f"z{u}", [P, L]) for u in range(2)]
        zT = m.sb("zT", [P, NT, P])
        ident = m.sb("ident", [P, P])
        gw = m.sb("gw", [P, NT, E])
        bias = m.sb("bias", [P, E])
        g = m.sb("g", [P, 1])
        tg = m.sb("tg", [P, 1])
        st = m.sb("st", [P, 2, 6])
        mv = m.sb("mv", [P, 2])
        rstd = m.sb("rstd", [P, 1])
        st2 = m.sb("st2", [P, 2, 6])
        mv2 = m.sb("mv2", [P, 2])
        rstd2 = m.sb("rstd2", [P, 1])
        eps = m.sb("eps", [P, 1])
        minus_half = m.sb("minus_half", [P, 1])
        logit = m.sb("logit", [P, H, E])

        psY = [m.ps(f"psY{u}", [P, 2, BANK]) for u in range(2)]
        psT = m.ps("psT", [P, NT * P])
        psO = m.ps("psO", [P, L])

        const = m.sem("const")
        made = m.sem("made")
        gate = m.sem("gate")
        passed = m.sem("passed")
        x_in, c_in = m.sem("x_in"), m.sem("c_in")
        tz_in = [m.sem(f"tz_in{u}") for u in range(2)]
        res_in = [m.sem(f"res_in{u}") for u in range(2)]
        z_out = [m.sem(f"z_out{u}") for u in range(2)]
        x1_out = [m.sem(f"x1_out{u}") for u in range(2)]
        zT_out = m.sem("zT_out")
        l_out = m.sem("l_out")
        c_turned = m.sem("c_turned")
        q_turned = m.sem("q_turned")
        z_turned = m.sem("z_turned")
        o_turned = m.sem("o_turned")
        y_done = m.sem("y_done")
        l_done = m.sem("l_done")
        kT_set = m.sem("kT_set")
        qT_set = m.sem("qT_set")
        zT_set = m.sem("zT_set")
        y_set = m.sem("y_set")
        hi_set = m.sem("hi_set")
        kv_set = m.sem("kv_set")
        lo_set = m.sem("lo_set")
        ln1 = m.sem("ln1")
        ln2 = m.sem("ln2")
        root1 = m.sem("root1")
        root2 = m.sem("root2")
        multiplied = m.sem("multiplied")
        summed = m.sem("summed")
        l_set = m.sem("l_set")
        LN1 = 4
        LN2 = 5

        block = ctx.enter_context(nc.Block())

        def keys_of(half):
            return slice((1 - half) * G, (2 - half) * G)

        def wait(eng, sem, value):
            if not (isinstance(value, int) and value <= 0):
                eng.wait_ge(sem, value)

        def steady(eng, step):
            step(0, 0, True, False, False)
            step(1, 1, True, True, False)
            with eng.Fori(1, H // 2 - 1) as pair:
                h = 2 * pair
                step(h, 0, True, True, True)
                step(h + 1, 1, True, True, True)
            step(H - 2, 0, True, True, True)
            step(H - 1, 1, False, True, True)

        @block.sync
        def _(sp):
            sp.dma_start(gw[:, :, :], gate_w.rearrange("(c p) e -> p c e", p=P)).then_inc(const, 16)
            sp.dma_start(bias[:, :], expert_bias.rearrange("(a e) -> a e", a=1).to_broadcast([P, E])).then_inc(const, 16)
            sp.dma_start(g[:, :], g_xattn.rearrange("(a e) -> a e", a=1).to_broadcast([P, 1])).then_inc(const, 16)

            def load_x(h):
                wait(sp, q_turned, h)
                sp.dma_start(xq[:, :], x_rows[h]).then_inc(x_in, 16)

            def load_c(h):
                wait(sp, c_turned, h)
                sp.dma_start(cn[:, :], c_rows[h]).then_inc(c_in, 16)

            def load_filter(h, u):
                wait(sp, y_done, NT * (h - 1))
                sp.dma_start(tz_hi[u][:, :].bitcast(F32), t_hi[h]).then_inc(tz_in[u], 16)
                sp.dma_start(tz_lo[u][:, :].bitcast(F32), t_lo[h]).then_inc(tz_in[u], 16)

            load_c(0)
            load_x(0)
            load_filter(0, 0)
            load_c(1)

            def step(h, u, ahead, back, back2):
                if ahead:
                    load_x(h + 1)
                    load_filter(h + 1, 1 - u)
                if back2:
                    sp.wait_ge(x1_out[u], 8 * (h - u))
                sp.dma_start(x1[u][:, :], x_rows[h]).then_inc(res_in[u], 16)
                if back2:
                    sp.wait_ge(zT_set, h - 1)
                    sp.dma_start(zT_d[h - 2], zT[:, :, :]).then_inc(zT_out, 16)
                if not (isinstance(h, int) and h >= H - 2):
                    load_c(h + 2)
                if back:
                    sp.wait_ge(ln2, LN2 * h - (LN2 - 1))
                    sp.dma_start(o_rows[h - 1], x1[1 - u][:, :]).then_inc(x1_out[1 - u], 16)
                    sp.wait_ge(ln2, LN2 * h)
                    sp.dma_start(z_rows[h - 1], z[1 - u][:, :]).then_inc(z_out[1 - u], 16)

            steady(sp, step)
            sp.wait_ge(ln2, LN2 * H)
            sp.dma_start(o_rows[H - 1], x1[1][:, :]).then_inc(x1_out[1], 16)
            sp.dma_start(z_rows[H - 1], z[1][:, :]).then_inc(z_out[1], 16)
            for h in (H - 2, H - 1):
                sp.wait_ge(zT_set, h + 1)
                sp.dma_start(zT_d[h], zT[:, :, :]).then_inc(zT_out, 16)
            sp.wait_ge(l_set, H)
            sp.dma_start(logit_d, logit[:, :, :]).then_inc(l_out, 16)
            for u in range(2):
                sp.wait_ge(x1_out[u], 8 * H)
                sp.wait_ge(z_out[u], 8 * H)
            sp.wait_ge(zT_out, 16 * H)
            sp.wait_ge(l_out, 16)

        @block.gpsimd
        def _(pool):
            identity_steps(nc, pool, ident, made)
            nc.gpsimd.memset(eps[:, :], EPS).then_inc(made, 1)
            nc.gpsimd.memset(minus_half[:, :], -0.5).then_inc(made, 1)
            pool.wait_ge(made, 4)

            def root(var, r, done, value, sem, n):
                pool.wait_ge(done, value)
                nc.gpsimd.tensor_tensor(r[:, :], var, eps[:, :], ALU.add).then_inc(sem, 1)
                pool.wait_ge(sem, 2 * n + 1)
                nc.gpsimd.tensor_tensor(r[:, :], r[:, :], minus_half[:, :], ALU.pow).then_inc(sem, 1)

            def pairs(h, halves):
                pool.wait_ge(kT_set, h + 1)
                for half in halves:
                    wait(pool, lo_set, 2 * h + half)
                    wait(pool, hi_set, 2 * h + half)
                    ks = kT[:, keys_of(half)].rearrange("p t b i -> p (t b) i")
                    dst = kv[:, :, :, :].rearrange("p t b i -> p (t b) i")
                    for i in range(HD):
                        last = nc.gpsimd.tensor_tensor(dst[:, :, off[i]:off[i] + HD - i], ks[:, :, i:HD],
                                                       ks[:, :, i:i + 1].to_broadcast([P, G * B, HD - i]), ALU.mult)
                    last.then_inc(kv_set, 1)

            pairs(0, [0])
            root(mv[:, 1:2], rstd, ln1, LN1 - 1, root1, 0)
            pairs(0, [1])

            def step(h, u, ahead, back, back2):
                if ahead:
                    pairs(h + 1, [0])
                    root(mv[:, 1:2], rstd, ln1, LN1 * (h + 2) - 1, root1, h + 1)
                    pairs(h + 1, [1])
                if back:
                    root(mv2[:, 1:2], rstd2, ln2, LN2 * h - 1, root2, h - 1)

            steady(pool, step)
            root(mv2[:, 1:2], rstd2, ln2, LN2 * H - 1, root2, H - 1)

        @block.scalar
        def _(act):
            act.wait_ge(const, 48)
            nc.scalar.activation(tg[:, :], g[:, :], ACT.Tanh).then_inc(gate, 1)

            def keys(h):
                act.wait_ge(c_turned, h + 1)
                wait(act, kv_set, 2 * h)
                nc.scalar.activation(kT[:, :, :, :].rearrange("p t b i -> p (t b i)"), psT[:, :], ACT.Copy).then_inc(kT_set, 1)

            def queries(h, u):
                act.wait_ge(q_turned, h + 1)
                wait(act, multiplied, 2 * (h - 1))
                nc.scalar.activation(qT[u][:, :, :, :].rearrange("p t b i -> p (t b i)"), psT[:, :], ACT.Copy).then_inc(qT_set, 1)

            def high(h, u, half):
                act.wait_ge(kv_set, 2 * h + half + 1)
                wait(act, y_done, NT * (h - 1))
                nc.scalar.activation(kv_hi[u][:, keys_of(half)].rearrange("p t b i -> p (t b i)"),
                                     kv[:, :, :, :].rearrange("p t b i -> p (t b i)"), ACT.Copy).then_inc(hi_set, 1)

            def z_turn(h):
                act.wait_ge(z_turned, h + 1)
                wait(act, l_done, h)
                wait(act, zT_out, 16 * h)
                nc.scalar.activation(zT[:, :, :].rearrange("p t n -> p (t n)"), psT[:, :], ACT.Copy).then_inc(zT_set, 1)

            def conv_out(h, u, a):
                act.wait_ge(y_done, NT * h + a + 1)
                if a == 0:
                    wait(act, multiplied, 2 * (h - 1))
                nc.scalar.activation(y[u][:, a].rearrange("p (c b) i -> p c (b i)", c=2),
                                     psY[a % 2][:, :, 0:NB * PAIRS], ACT.Copy).then_inc(y_set, 1)

            keys(0)
            high(0, 0, 0)
            high(0, 0, 1)
            queries(0, 0)

            def step(h, u, ahead, back, back2):
                if ahead:
                    keys(h + 1)
                for a in range(3):
                    conv_out(h, u, a)
                if back2:
                    z_turn(h - 2)
                if ahead:
                    high(h + 1, 1 - u, 0)
                conv_out(h, u, 3)
                if ahead:
                    high(h + 1, 1 - u, 1)
                for a in range(4, NT - 1):
                    conv_out(h, u, a)
                if ahead:
                    queries(h + 1, 1 - u)
                conv_out(h, u, NT - 1)

            steady(act, step)
            z_turn(H - 2)
            z_turn(H - 1)

        @block.vector
        def _(dve):
            def norm(src, stats, mean_var, r, dst, done, base, root):
                for c in range(2):
                    last = nc.vector.bn_stats(stats[:, c, :], src[:, c * (L // 2):(c + 1) * (L // 2)])
                    last.then_inc(done, 1)
                dve.wait_ge(done, base + 2)
                dve.sem_inc(passed, 1)
                nc.vector.bn_aggr(mean_var[:, :], stats[:, :, :].rearrange("p a b -> p (a b)")).then_inc(done, 1)
                dve.wait_ge(*root)
                nc.vector.tensor_scalar(dst[:, :], src[:, :], mean_var[:, 0:1], r[:, 0:1],
                                        ALU.subtract, ALU.mult).then_inc(done, 1)

            def query_norm(h):
                dve.wait_ge(x_in, 16 * (h + 1))
                norm(xq, st, mv, rstd, xq, ln1, LN1 * h, (root1, 2 * h + 2))

            def low(h, u, half):
                dve.wait_ge(hi_set, 2 * h + half + 1)
                nc.vector.tensor_tensor(kv_lo[u][:, keys_of(half)].rearrange("p t b i -> p (t b i)"),
                                        kv[:, :, :, :].rearrange("p t b i -> p (t b i)"),
                                        kv_hi[u][:, keys_of(half)].rearrange("p t b i -> p (t b i)").bitcast(F32),
                                        ALU.subtract).then_inc(lo_set, 1)

            def combine(h, u, half):
                dve.wait_ge(y_set, NT * h + G * (half + 1))
                dve.wait_ge(qT_set, h + 1)
                wait(dve, summed, 2 * h + half)
                ys = y[u][:, half * G:(half + 1) * G].rearrange("p t b i -> p (t b) i")
                qs = qT[u][:, half * G:(half + 1) * G].rearrange("p t b i -> p (t b) i")
                for i in range(HD):
                    n = HD - i
                    last = nc.vector.tensor_tensor(prod[:, :, i:HD, i], ys[:, :, off[i]:off[i] + n],
                                                   qs[:, :, i:i + 1].to_broadcast([P, G * B, n]), ALU.mult)
                    if n > 1:
                        last = nc.vector.tensor_tensor(prod[:, :, i, i + 1:HD], ys[:, :, off[i] + 1:off[i] + n],
                                                       qs[:, :, i + 1:HD], ALU.mult)
                last.then_inc(multiplied, 1)
                dve.wait_ge(multiplied, 2 * h + half + 1)
                wait(dve, o_turned, h)
                nc.vector.tensor_reduce(oT[:, half * G:(half + 1) * G, :].rearrange("p t (b j) -> p (t b) j", j=HD),
                                        prod[:, :, :, :], AX.X, ALU.add).then_inc(summed, 1)

            def residual(h, u, sem_turn):
                dve.wait_ge(o_turned, h + 1)
                dve.wait_ge(res_in[u], sem_turn)
                nc.vector.scalar_tensor_tensor(out=x1[u][:, :], in0=psO[:, :], scalar=tg[:, 0:1], in1=x1[u][:, :],
                                               op0=ALU.mult, op1=ALU.add).then_inc(ln2, 1)
                dve.wait_ge(ln2, LN2 * h + 1)
                if not (isinstance(h, int) and h < 2):
                    dve.wait_ge(z_out[u], sem_turn - 16)
                    dve.wait_ge(z_turned, h - 1)
                norm(x1[u], st2, mv2, rstd2, z[u], ln2, LN2 * h + 1, (root2, 2 * h + 2))

            def logits(h):
                dve.wait_ge(l_done, h + 1)
                nc.vector.tensor_tensor(logit[:, h, :], psO[:, 0:E], bias[:, :], ALU.add).then_inc(l_set, 1)

            query_norm(0)
            low(0, 0, 0)
            low(0, 0, 1)
            dve.wait_ge(gate, 1)
            dve.wait_ge(const, 48)

            def step(h, u, ahead, back, back2):
                if back:
                    combine(h - 1, 1 - u, 0)
                if ahead:
                    query_norm(h + 1)
                if ahead:
                    low(h + 1, 1 - u, 0)
                if back:
                    combine(h - 1, 1 - u, 1)
                if ahead:
                    low(h + 1, 1 - u, 1)
                if back2:
                    logits(h - 2)
                if back:
                    residual(h - 1, 1 - u, 8 * (h + u) if not isinstance(h, int) else 16 * ((h - 1) // 2 + 1))

            steady(dve, step)
            combine(H - 1, 1, 0)
            combine(H - 1, 1, 1)
            logits(H - 2)
            residual(H - 1, 1, 8 * H)
            logits(H - 1)

        @block.tensor
        def _(pe):
            def conv(h, u, tiles, first_use):
                for a in tiles:
                    if a == 0:
                        pe.wait_ge(hi_set, 2 * h + 1)
                        pe.wait_ge(lo_set, 2 * h + 1)
                        pe.wait_ge(tz_in[u], first_use)
                    if a == G:
                        pe.wait_ge(hi_set, 2 * h + 2)
                        pe.wait_ge(lo_set, 2 * h + 2)
                    wait(pe, y_set, NT * h + a - 1)
                    for c in range(a + 1):
                        for half in range(2):
                            acc = psY[a % 2][:, half, 0:NB * PAIRS]
                            d = (a - c) * P
                            hi = kv_hi[u][:, NT - 1 - c, half * NB:(half + 1) * NB, :].rearrange("p b i -> p (b i)")
                            lo = kv_lo[u][:, NT - 1 - c, half * NB:(half + 1) * NB, :].rearrange("p b i -> p (b i)")
                            nc.tensor.matmul(acc, tz_hi[u][:, d:d + P], hi, start=(c == 0), stop=False)
                            nc.tensor.matmul(acc, tz_hi[u][:, d:d + P], lo, start=False, stop=False)
                            last = nc.tensor.matmul(acc, tz_lo[u][:, d:d + P], hi, start=False, stop=(c == a))
                    last.then_inc(y_done, 1)

            def turn_all(dst, src):
                for t in range(NT):
                    last = nc.tensor.transpose(dst[:, t * P:(t + 1) * P], src[:, t * P:(t + 1) * P], ident[:, :])
                return last

            def turn_c(h):
                pe.wait_ge(c_in, 16 * (h + 1))
                wait(pe, qT_set, h)
                turn_all(psT, cn).then_inc(c_turned, 1)

            def turn_q(h):
                pe.wait_ge(ln1, LN1 * (h + 1))
                pe.wait_ge(kT_set, h + 1)
                if not (isinstance(h, int) and h < 3):
                    pe.wait_ge(zT_set, h - 2)
                turn_all(psT, xq).then_inc(q_turned, 1)

            def turn_z(h, zu, k_uses, q_uses):
                pe.wait_ge(ln2, LN2 * (h + 1))
                pe.wait_ge(kT_set, k_uses)
                pe.wait_ge(qT_set, q_uses)
                wait(pe, zT_set, h)
                turn_all(psT, z[zu]).then_inc(z_turned, 1)

            def turn_o(h):
                pe.wait_ge(summed, 2 * (h + 1))
                wait(pe, l_set, h)
                wait(pe, ln2, LN2 * (h - 1) + 1)
                for t in range(NT):
                    last = nc.tensor.transpose(psO[:, t * P:(t + 1) * P], oT[:, t, :], ident[:, :])
                last.then_inc(o_turned, 1)

            def logits(h):
                pe.wait_ge(zT_set, h + 1)
                pe.wait_ge(ln2, LN2 * h + 1)
                wait(pe, l_set, h)
                for t in range(NT):
                    last = nc.tensor.matmul(psO[:, 0:E], zT[:, t, :], gw[:, t, :], start=(t == 0), stop=(t == NT - 1))
                last.then_inc(l_done, 1)

            pe.wait_ge(made, 2)
            pe.wait_ge(const, 48)
            turn_c(0)
            turn_q(0)

            def step(h, u, ahead, back, back2):
                uses = 32 * (h // 2 + 1) if isinstance(h, int) else 16 * (h - u) + 32
                if ahead:
                    turn_c(h + 1)
                conv(h, u, range(0, 3), uses)
                if back2:
                    turn_z(h - 2, u, h + 2 if ahead else h + 1, h + 1)
                conv(h, u, range(3, 5), uses)
                if back2:
                    logits(h - 2)
                conv(h, u, range(5, NT - 1), uses)
                if ahead:
                    turn_q(h + 1)
                if back:
                    turn_o(h - 1)
                conv(h, u, range(NT - 1, NT), uses)

            steady(pe, step)
            turn_z(H - 2, 0, H, H)
            logits(H - 2)
            turn_o(H - 1)
            turn_z(H - 1, 1, H, H)
            logits(H - 1)


def route(nc, logit_d, slot_of, pay, capacity, slots, H):
    E = logit_d.shape[2]
    S = H * HD
    BIG = float(1 << 22)
    with ExitStack() as ctx:
        m = Pool(nc, ctx, "rte")
        raw = m.sb("raw", [P, H, E])
        aff = m.sb("aff", [P, E, H])
        rank = m.sb("rank", [P, E, H])
        cmp = m.sb("cmp", [P, E, H])
        score = m.sb("score", [P, E, H])
        over = m.sb("over", [P, E, H])
        ties = m.sb("ties", [P, E, H])
        scan = [m.sb(f"scan{u}", [P, E, H]) for u in range(2)]
        slot = m.sb("slot", [P, E, H])
        a = m.sb("a", [P, E, H])
        b = m.sb("b", [P, E, H])
        first = m.sb("first", [P, H])
        second = m.sb("second", [P, H])
        none = m.sb("none", [P, H])
        spare = m.sb("spare", [P, H])
        gap = m.sb("gap", [P, H])
        token = m.sb("token", [P, H])
        weight = m.sb("weight", [P, H])
        thr = m.sb("thr", [P, E], I32)
        cand = m.sb("cand", [P, E], I32)
        bit = m.sb("bit", [P, E], I32)
        count = m.sb("count", [P, E])
        keep = m.sb("keep", [P, E])
        base = m.sb("base", [P, E])
        room = m.sb("room", [P, E])
        ones = m.sb("ones", [P, P])
        row = m.sb("row", [P, P])
        col = m.sb("col", [P, P])
        rb = m.sb("rb", [P, P])
        cb = m.sb("cb", [P, P])
        same = m.sb("same", [P, P])
        before = m.sb("before", [P, P])
        under = m.sb("under", [P, P])
        irow = m.sb("irow", [P, P], I32)
        icol = m.sb("icol", [P, P], I32)
        ibat = m.sb("ibat", [P, P], I32)
        itok = m.sb("itok", [P, H], I32)
        iexp = m.sb("iexp", [P, E], I32)
        psC = m.ps("psC", [P, E])
        psR = m.ps("psR", [P, E * H])

        loaded, numbered, negexp, counted, dch, tallied, ranked = (
            m.sem(n) for n in ("loaded", "numbered", "negexp", "counted", "dch", "tallied", "ranked"))
        block = ctx.enter_context(nc.Block())
        TALLIES = 30

        @block.sync
        def _(sp):
            sp.dma_start(raw[:, :, :], logit_d).then_inc(loaded, 16)

        @block.gpsimd
        def _(pool):
            nc.gpsimd.iota(irow[:, :], [[0, P]], base=0, channel_multiplier=1).then_inc(numbered, 1)
            nc.gpsimd.iota(icol[:, :], [[1, P]], base=0, channel_multiplier=0).then_inc(numbered, 1)
            nc.gpsimd.iota(itok[:, :], [[HD, H]], base=0, channel_multiplier=1).then_inc(numbered, 1)
            nc.gpsimd.iota(iexp[:, :], [[slots, E]], base=0, channel_multiplier=0).then_inc(numbered, 1)

        @block.scalar
        def _(act):
            act.wait_ge(loaded, 16)
            nc.scalar.activation(aff[:, :, :], raw[:, :, :].rearrange("p h e -> p e h"), ACT.Exp,
                                 scale=-1.0).then_inc(negexp, 1)

        @block.tensor
        def _(pe):
            with pe.Fori(0, TALLIES) as i:
                pe.wait_ge(counted, i + 1)
                nc.tensor.matmul(psC[:, :], ones[:, :], count[:, :], start=True, stop=True).then_inc(tallied, 1)
            pe.wait_ge(counted, TALLIES + 1)
            nc.tensor.matmul(psC[:, :], ones[:, :], count[:, :], start=True, stop=True).then_inc(tallied, 1)
            for n, what in enumerate((ties, slot)):
                pe.wait_ge(counted, TALLIES + 2 + n)
                flat = what[:, :, :].rearrange("p e h -> p (e h)")
                nc.tensor.matmul(psR[:, :], under[:, :], flat, start=True, stop=False)
                nc.tensor.matmul(psR[:, :], same[:, :], scan[0][:, :, :].rearrange("p e h -> p (e h)"),
                                 start=False, stop=False)
                nc.tensor.matmul(psR[:, :], before[:, :], scan[1][:, :, :].rearrange("p e h -> p (e h)"),
                                 start=False, stop=True).then_inc(ranked, 1)

        @block.vector
        def _(dve):
            done = [0]

            def link(ins):
                done[0] += 1
                ins.then_inc(dch, 1)
                dve.wait_ge(dch, done[0])

            v = nc.vector
            dve.wait_ge(numbered, 4)
            v.memset(ones[:, :], 1.0)
            v.memset(thr[:, :], 0)
            v.memset(bit[:, :], 1 << (TALLIES - 1))
            v.tensor_copy(row[:, :], irow[:, :])
            v.tensor_copy(col[:, :], icol[:, :])
            v.tensor_copy(token[:, :], itok[:, :])
            v.tensor_copy(base[:, :], iexp[:, :])
            v.tensor_scalar(spare[:, :], itok[:, 0:1].to_broadcast([P, H]), float(E * slots), None, ALU.add)
            link(v.tensor_scalar(ibat[:, :], irow[:, :], 3, None, ALU.logical_shift_right))
            link(v.tensor_copy(rb[:, :], ibat[:, :]))
            link(v.tensor_scalar(ibat[:, :], icol[:, :], 3, None, ALU.logical_shift_right))
            link(v.tensor_copy(cb[:, :], ibat[:, :]))
            link(v.scalar_tensor_tensor(out=token[:, :], in0=rb[:, 0:H], scalar=float(S - HD), in1=token[:, :],
                                        op0=ALU.mult, op1=ALU.add))
            v.tensor_tensor(same[:, :], rb[:, :], cb[:, :], ALU.is_equal)
            v.tensor_tensor(before[:, :], rb[:, :], cb[:, :], ALU.is_lt)
            link(v.tensor_tensor(under[:, :], row[:, :], col[:, :], ALU.is_lt))
            link(v.tensor_tensor(under[:, :], under[:, :], same[:, :], ALU.mult))

            dve.wait_ge(negexp, 1)
            link(v.tensor_scalar(aff[:, :, :], aff[:, :, :], 1.0, None, ALU.add))
            link(v.reciprocal(aff[:, :, :], aff[:, :, :]))

            link(v.memset(rank[:, :, :], 0.0))
            for d in range(1, E):
                lower, upper = slice(0, E - d), slice(d, E)
                link(v.tensor_tensor(cmp[:, lower, :], aff[:, lower, :], aff[:, upper, :], ALU.is_ge))
                link(v.tensor_tensor(rank[:, upper, :], rank[:, upper, :], cmp[:, lower, :], ALU.add))
                link(v.scalar_tensor_tensor(out=rank[:, lower, :].rearrange("p e h -> p (e h)"),
                                            in0=rank[:, lower, :].rearrange("p e h -> p (e h)"), scalar=1.0,
                                            in1=cmp[:, lower, :].rearrange("p e h -> p (e h)"),
                                            op0=ALU.add, op1=ALU.subtract))
            link(v.tensor_scalar(rank[:, :, :], rank[:, :, :], 2.0, None, ALU.is_lt))
            link(v.tensor_tensor(score[:, :, :], aff[:, :, :], rank[:, :, :], ALU.mult))
            link(v.scalar_tensor_tensor(out=score[:, :, :], in0=rank[:, :, :], scalar=-1.0, in1=score[:, :, :],
                                        op0=ALU.add, op1=ALU.add))

            linked = done[0]
            STEPS = 6
            with dve.Fori(0, TALLIES) as i:
                def step(ins, n):
                    ins.then_inc(dch, 1)
                    dve.wait_ge(dch, i * STEPS + (linked + n))

                step(v.tensor_tensor(cand[:, :], thr[:, :], bit[:, :], ALU.bitwise_or), 1)
                step(v.tensor_tensor(cmp[:, :, :], score[:, :, :],
                                     cand[:, :].bitcast(F32).unsqueeze(2).to_broadcast([P, E, H]), ALU.is_ge), 2)
                v.tensor_reduce(count[:, :], cmp[:, :, :], AX.X, ALU.add).then_inc(counted, 1)
                step(v.tensor_scalar(bit[:, :], bit[:, :], 1, None, ALU.logical_shift_right), 3)
                dve.wait_ge(tallied, i + 1)
                step(v.scalar_tensor_tensor(out=keep[:, :], in0=psC[:, :], scalar=float(capacity),
                                            in1=cand[:, :].bitcast(F32), op0=ALU.is_ge, op1=ALU.mult), 4)
                step(v.tensor_tensor(keep[:, :], keep[:, :], thr[:, :].bitcast(F32), ALU.max), 5)
                step(v.tensor_copy(thr[:, :].bitcast(F32), keep[:, :]), 6)
            done[0] = linked + STEPS * TALLIES

            limit = thr[:, :].bitcast(F32).unsqueeze(2).to_broadcast([P, E, H])
            v.tensor_tensor(ties[:, :, :], score[:, :, :], limit, ALU.is_equal)
            link(v.tensor_tensor(over[:, :, :], score[:, :, :], limit, ALU.is_gt))
            v.tensor_reduce(count[:, :], over[:, :, :], AX.X, ALU.add).then_inc(counted, 1)
            dve.wait_ge(tallied, TALLIES + 1)
            link(v.tensor_scalar(room[:, :], psC[:, :], -1.0, float(capacity), ALU.mult, ALU.add))

            def earlier(what, n):
                link(v.tensor_copy(scan[0][:, :, :], what[:, :, :]))
                d = 1
                while d < H:
                    link(v.tensor_copy(scan[1][:, :, :], scan[0][:, :, :]))
                    link(v.tensor_tensor(scan[0][:, :, d:H], scan[1][:, :, d:H], scan[1][:, :, 0:H - d], ALU.add))
                    d *= 2
                link(v.tensor_copy(scan[1][:, :, :], scan[0][:, :, H - 1:H].to_broadcast([P, E, H])))
                v.tensor_tensor(scan[0][:, :, :], scan[0][:, :, :], what[:, :, :], ALU.subtract).then_inc(counted, 1)
                dve.wait_ge(ranked, n + 1)

            earlier(ties, 0)
            rows = psR[:, :].rearrange("p (e h) -> p e h", e=E)
            link(v.tensor_tensor(cmp[:, :, :], rows, room[:, :].unsqueeze(2).to_broadcast([P, E, H]), ALU.is_lt))
            link(v.tensor_tensor(cmp[:, :, :], cmp[:, :, :], ties[:, :, :], ALU.mult))
            link(v.tensor_tensor(slot[:, :, :], cmp[:, :, :], over[:, :, :], ALU.add))
            earlier(slot, 1)
            link(v.tensor_tensor(a[:, :, :], rows, base[:, :].unsqueeze(2).to_broadcast([P, E, H]), ALU.add))
            link(v.tensor_scalar(b[:, :, :], a[:, :, :], -BIG, None, ALU.add))
            link(v.tensor_tensor(b[:, :, :], b[:, :, :], slot[:, :, :], ALU.mult))
            link(v.tensor_scalar(b[:, :, :], b[:, :, :], BIG, None, ALU.add))
            link(v.tensor_reduce(first[:, :], b[:, :, :].rearrange("p e h -> p h e"), AX.X, ALU.min))
            link(v.tensor_tensor(cmp[:, :, :], b[:, :, :], first[:, :].unsqueeze(1).to_broadcast([P, E, H]), ALU.is_equal))
            link(v.tensor_tensor(cmp[:, :, :], cmp[:, :, :], aff[:, :, :], ALU.mult))
            link(v.tensor_tensor(cmp[:, :, :], cmp[:, :, :], slot[:, :, :], ALU.mult))
            link(v.tensor_reduce(weight[:, :], cmp[:, :, :].rearrange("p e h -> p h e"), AX.X, ALU.add))
            link(v.tensor_copy(pay[:, :, 0, 1].bitcast(F32), weight[:, :]))
            link(v.tensor_scalar(a[:, :, :], a[:, :, :], 1.0, None, ALU.add))
            link(v.tensor_tensor(a[:, :, :], a[:, :, :], slot[:, :, :], ALU.mult))
            link(v.tensor_reduce(second[:, :], a[:, :, :].rearrange("p e h -> p h e"), AX.X, ALU.max))
            link(v.tensor_tensor(cmp[:, :, :], a[:, :, :], second[:, :].unsqueeze(1).to_broadcast([P, E, H]), ALU.is_equal))
            link(v.tensor_tensor(cmp[:, :, :], cmp[:, :, :], aff[:, :, :], ALU.mult))
            link(v.tensor_tensor(cmp[:, :, :], cmp[:, :, :], slot[:, :, :], ALU.mult))
            link(v.tensor_reduce(weight[:, :], cmp[:, :, :].rearrange("p e h -> p h e"), AX.X, ALU.add))
            link(v.tensor_copy(pay[:, :, 1, 1].bitcast(F32), weight[:, :]))
            link(v.tensor_scalar(second[:, :], second[:, :], -1.0, None, ALU.add))
            link(v.tensor_tensor(none[:, :], second[:, :], first[:, :], ALU.is_le))
            link(v.tensor_tensor(gap[:, :], spare[:, :], second[:, :], ALU.subtract))
            link(v.tensor_tensor(gap[:, :], gap[:, :], none[:, :], ALU.mult))
            link(v.tensor_tensor(second[:, :], second[:, :], gap[:, :], ALU.add))
            link(v.tensor_copy(slot_of[:, :, 1], second[:, :]))
            link(v.tensor_scalar(none[:, :], first[:, :], BIG, None, ALU.is_equal))
            link(v.tensor_tensor(gap[:, :], spare[:, :], first[:, :], ALU.subtract))
            link(v.tensor_tensor(gap[:, :], gap[:, :], none[:, :], ALU.mult))
            link(v.tensor_tensor(first[:, :], first[:, :], gap[:, :], ALU.add))
            link(v.tensor_copy(slot_of[:, :, 0], first[:, :]))
            for n in range(2):
                link(v.tensor_copy(pay[:, :, n, 0], token[:, :]))


def experts(nc, zT_d, z_d, slot_of, pay, list_d, g_ffn, shared_w1, shared_w2, routed_w1, routed_w2, out,
            slots, H):
    D, F2 = shared_w1.shape[1:]
    F = F2 // 2
    E = routed_w1.shape[0]
    C, FC = D // P, F // P
    GE = 5
    M = slots // (2 * GE)
    TILES = E * 2 * GE
    GS = H // 2
    HALF = D // 2
    B = P // HD
    T = B * H * HD
    assert slots == 2 * GE * M and M <= P and HALF <= BANK and GS % 2 == 0 and GS >= 6 and E % 2 == 1

    o_rows = out[0:T, :].rearrange("(b h j) l -> h b j l", b=B, j=HD)

    with ExitStack() as ctx:
        m = Pool(nc, ctx, "moe")
        w1h = m.sb("w1h", [P, C, F2], F32R)
        w1l = m.sb("w1l", [P, C, F2], F32R)
        w2h = m.sb("w2h", [P, FC, D], F32R)
        w2l = m.sb("w2l", [P, FC, D], F32R)
        raw = m.sb("raw", [P, C * F2])
        raw1 = raw[:, :].rearrange("p (c f) -> p c f", c=C)
        raw2 = raw[:, 0:FC * D].rearrange("p (c n) -> p c n", c=FC)
        zin = [m.sb(f"zin{t}", [P, D]) for t in range(2)]
        zh = [m.sb(f"zh{u}", [P, C, 2 * P], F32R) for u in range(2)]
        zl = [m.sb(f"zl{u}", [P, C, 2 * P], F32R) for u in range(2)]
        act_s = [m.sb(f"act_s{j}", [P, 2 * P]) for j in range(2)]
        hid = [m.sb(f"hid{j}", [P, 2 * P]) for j in range(2)]
        hh = [m.sb(f"hh{u}", [P, FC, 2 * P], F32R) for u in range(2)]
        hl = [m.sb(f"hl{u}", [P, FC, 2 * P], F32R) for u in range(2)]
        y = [m.sb(f"y{t}", [P, D]) for t in range(2)]
        ident = m.sb("ident", [P, P])
        g = m.sb("g", [P, 1])
        tg = m.sb("tg", [P, 1])
        lists = m.sb("lists", [M, TILES, 2], I32)
        scale = m.sb("scale", [M, TILES])
        stage_i = [m.sb(f"stage_i{n}", [P, 1], I32) for n in range(2)]
        stage_p = [m.sb(f"stage_p{n}", [P, 2], I32) for n in range(2)]
        get_i = [m.sb(f"get_i{t}", [M, 1], I32) for t in range(2)]
        add_i = [m.sb(f"add_i{t}", [M, 1], I32) for t in range(2)]

        ps1 = [m.ps(f"ps1_{j}", [P, 2, 2 * P]) for j in range(2)]
        ps2 = [m.ps(f"ps2_{t}", [P, 2, BANK]) for t in range(2)]
        psT = m.ps("psT", [P, 2, BANK])

        const = m.sem("const")
        made = m.sem("made")
        gate = m.sem("gate")
        passed = m.sem("passed")
        w1_in, w2_in = m.sem("w1_in"), m.sem("w2_in")
        w1h_set, w1l_set = m.sem("w1h_set"), m.sem("w1l_set")
        w2h_set, w2l_set = m.sem("w2h_set"), m.sem("w2l_set")
        z_in = [m.sem(f"z_in{t}") for t in range(2)]
        z_got = [m.sem(f"z_got{t}") for t in range(2)]
        z_turned = m.sem("z_turned")
        zh_set, zl_set = m.sem("zh_set"), m.sem("zl_set")
        up = m.sem("up")
        silu = m.sem("silu")
        gated = m.sem("gated")
        hh_set, hl_set = m.sem("hh_set"), m.sem("hl_set")
        down = m.sem("down")
        y_set = m.sem("y_set")
        res_in = [m.sem(f"res_in{t}") for t in range(2)]
        stored = [m.sem(f"stored{t}") for t in range(2)]
        list_made = m.sem("list_made")
        list_init = m.sem("list_init")
        staged = m.sem("staged")
        scattered = [m.sem(f"scattered{n}") for n in range(2)]
        list_in = m.sem("list_in")
        scaled = m.sem("scaled")
        got = m.sem("got")
        put = m.sem("put")
        added = m.sem("added")
        y_free = m.sem("y_free")

        block = ctx.enter_context(nc.Block())

        def wait(eng, sem, value):
            if not (isinstance(value, int) and value <= 0):
                eng.wait_ge(sem, value)

        LAST = GS + E * GE

        def schedule(eng, group, after_shared, after):
            group(0, 0, 0, 0, "shared", "shared")
            group(1, 1, 0, 1, "shared", "shared")
            group(2, 0, 0, 2, "shared", "shared")
            with eng.Fori(1, GS // 2 - 1) as p:
                group(2 * p + 1, 1, 0, 3, "shared", "shared")
                group(2 * p + 2, 0, 0, 4, "shared", "shared")
            group(GS - 1, 1, 0, GS - 1, "shared", "routed")
            after_shared()

            def expert(n, k0, u0, last):
                for i in range(GE):
                    group(k0 + i, (u0 + i) % 2, n, i, "routed", None if last and i == GE - 1 else "routed")
                after(n, k0 + GE - 1, (u0 + GE - 1) % 2, last)

            with eng.Fori(0, E // 2) as q:
                expert(2 * q + 1, 2 * GE * q + GS, 0, False)
                expert(2 * q + 2, 2 * GE * q + (GS + GE), 1, False)
            expert(E, GS + GE * (E - 1), 0, True)

        def width(kind):
            return P if kind == "shared" else M

        @block.sync
        def _(sp):
            def load_w1(n, src):
                wait(sp, w2h_set, FC * n)
                wait(sp, w2l_set, FC * n)
                sp.dma_start(raw1, src.rearrange("(c p) f -> p c f", p=P)).then_inc(w1_in, 16)

            def load_w2(n, src):
                sp.wait_ge(w1h_set, C * (n + 1))
                sp.wait_ge(w1l_set, C * (n + 1))
                sp.dma_start(raw2, src.rearrange("(c p) n -> p c n", p=P)).then_inc(w2_in, 16)

            def load_z(k):
                for t in range(2):
                    wait(sp, zh_set, 2 * k + t - 1)
                    wait(sp, zl_set, 2 * k + t - 1)
                    sp.dma_start(zin[t][:, :], zT_d[2 * k + t].rearrange("p c n -> p (c n)")).then_inc(z_in[t], 16)

            def residual(k):
                for t in range(2):
                    wait(sp, stored[t], 16 * k)
                    sp.dma_start(y[t][:, :], o_rows[2 * k + t]).then_inc(res_in[t], 16)

            def store(k):
                for t in range(2):
                    sp.wait_ge(y_set, 4 * k + 2 * t + 2)
                    sp.dma_start(o_rows[2 * k + t], y[t][:, :]).then_inc(stored[t], 16)

            sp.dma_start(g[:, :], g_ffn.rearrange("(a e) -> a e", a=1).to_broadcast([P, 1])).then_inc(const, 16)
            load_w1(0, shared_w1[0])
            load_z(0)
            sp.wait_ge(list_made, 2)
            sp.dma_start(list_d[0:E * slots, :].rearrange("(r q) c -> q r c", q=M), lists[:, :, :]).then_inc(list_init, 16)
            load_w2(0, shared_w2[0])
            load_z(1)
            residual(0)
            load_w1(1, routed_w1[0])
            with sp.Fori(1, GS - 1) as k:
                load_z(k + 1)
                store(k - 1)
                residual(k)
            store(GS - 2)
            residual(GS - 1)
            store(GS - 1)
            for t in range(2):
                sp.wait_ge(stored[t], 16 * GS)
                sp.sem_inc(y_free, 1)
            load_w2(1, routed_w2[0])
            with sp.Fori(2, E + 1) as n:
                load_w1(n, routed_w1[n - 1])
                load_w2(n, routed_w2[n - 1])

        @block.gpsimd
        def _(pool):
            identity_steps(nc, pool, ident, made)
            nc.gpsimd.iota(lists[:, :, 0], [[0, TILES]], base=T, channel_multiplier=1).then_inc(list_made, 1)
            nc.gpsimd.memset(lists[:, :, 1], 0).then_inc(list_made, 1)
            pool.wait_ge(list_init, 16)
            def scatter_column(h):
                for n in range(2):
                    wait(pool, scattered[1 - n], h * 16 + 16 * n)
                    nc.gpsimd.tensor_copy(stage_i[n][:, :], slot_of[:, bass.ds(h, 1), n:n + 1].rearrange("p a b -> p (a b)")).then_inc(staged, 1)
                    nc.gpsimd.tensor_copy(stage_p[n][:, :], pay[:, bass.ds(h, 1), n, :].rearrange("p a b -> p (a b)")).then_inc(staged, 1)
                    pool.wait_ge(staged, h * 4 + (2 * n + 2))
                    pool.sem_inc(passed, 1)
                    nc.gpsimd.indirect_dma_start(list_d, bass.IndirectOffsetOnAxis(stage_i[n][:, 0:1], 0),
                                                 stage_p[n][:, :], None).then_inc(scattered[n], 16)

            scatter_column(0)
            with pool.Fori(1, H) as h:
                scatter_column(h)
            pool.wait_ge(scattered[0], 16 * H)
            pool.wait_ge(scattered[1], 16 * H)
            pool.dma_start(lists[:, :, :], list_d[0:E * slots, :].rearrange("(r q) c -> q r c", q=M)).then_inc(list_in, 16)
            pool.wait_ge(list_in, 16)

            def gather(k):
                r = k - GS
                for t in range(2):
                    pool.wait_ge(zh_set, 2 * k + t - 1)
                    pool.wait_ge(zl_set, 2 * k + t - 1)
                    nc.gpsimd.tensor_copy(get_i[t][:, :], lists[:, bass.ds(2 * r + t, 1), 0]).then_inc(got, 1)
                    pool.wait_ge(got, 2 * r + (t + 1))
                    pool.sem_inc(passed, 1)
                    nc.gpsimd.indirect_dma_start(zin[t][0:M, :], None, z_d,
                                                 bass.IndirectOffsetOnAxis(get_i[t][:, 0:1], 0)).then_inc(z_got[t], 16)

            def scatter(k):
                r = k - GS
                for t in range(2):
                    pool.wait_ge(y_set, 4 * k + (2 * t + 2))
                    nc.gpsimd.tensor_copy(add_i[t][:, :], lists[:, bass.ds(2 * r + t, 1), 0]).then_inc(put, 1)
                    pool.wait_ge(put, 2 * r + (t + 1))
                    pool.sem_inc(passed, 1)
                    nc.gpsimd.indirect_dma_start(out, bass.IndirectOffsetOnAxis(add_i[t][:, 0:1], 0),
                                                 y[t][0:M, :], None, compute_op=ALU.add).then_inc(added, 16)
                    pool.wait_ge(added, 16 * (2 * r + (t + 1)))
                    pool.sem_inc(y_free, 1)

            for k in range(GS, GS + 4):
                gather(k)
                if k == GS + 2:
                    for t in range(2):
                        pool.wait_ge(stored[t], 16 * GS)
                if k == GS + 3:
                    scatter(GS)
            with pool.Fori(GS + 1, LAST - 3) as k:
                gather(k + 3)
                scatter(k)
            for k in range(LAST - 3, LAST):
                scatter(k)

        @block.scalar
        def _(act):
            act.wait_ge(const, 16)
            nc.scalar.activation(tg[:, :], g[:, :], ACT.Tanh).then_inc(gate, 1)

            def w1_high(n):
                act.wait_ge(w1_in, 16 * (n + 1))
                for c in range(C):
                    nc.scalar.activation(w1h[:, c, :], raw1[:, c, :], ACT.Copy).then_inc(w1h_set, 1)

            def w2_high(n, c, k):
                if c == 0:
                    act.wait_ge(w2_in, 16 * (n + 1))
                    wait(act, down, 4 * k)
                nc.scalar.activation(w2h[:, c, :], raw2[:, c, :], ACT.Copy).then_inc(w2h_set, 1)

            def split(k, u, t, kind):
                w = width(kind)
                wait(act, up, FC * (k - 1))
                if kind == "shared":
                    act.wait_ge(z_in[t], 16 * (k + 1))
                    nc.scalar.activation(zh[u][:, :, t * w:(t + 1) * w],
                                         zin[t][:, :].rearrange("p (c n) -> p c n", c=C), ACT.Copy).then_inc(zh_set, 1)
                else:
                    act.wait_ge(z_turned, 2 * (k - GS) + (t + 1))
                    nc.scalar.activation(zh[u][:, :, t * w:(t + 1) * w].rearrange("p (b c) n -> p b c n", b=2),
                                         psT[:, :, 0:C // 2 * w].rearrange("p b (c n) -> p b c n", n=w),
                                         ACT.Copy).then_inc(zh_set, 1)

            def swish(k, j, w):
                act.wait_ge(up, FC * k + (j + 1))
                wait(act, gated, FC * k + (j - 1))
                nc.scalar.activation(act_s[j % 2][:, 0:2 * w], ps1[j % 2][:, 1, 0:2 * w], ACT.Silu).then_inc(silu, 1)

            def high(k, u, j, w):
                act.wait_ge(gated, FC * k + (j + 1))
                wait(act, down, 4 * (k - 1))
                nc.scalar.activation(hh[u][:, j, 0:2 * w], hid[j % 2][:, 0:2 * w], ACT.Copy).then_inc(hh_set, 1)

            def group(k, u, n, i, kind, next_kind):
                w = width(kind)
                swish(k, 0, w)
                if next_kind:
                    split(k + 1, 1 - u, 0, next_kind)
                high(k, u, 0, w)
                first = isinstance(i, int) and i == 0
                if first:
                    w2_high(n, 0, k)
                swish(k, 1, w)
                high(k, u, 1, w)
                if first:
                    w2_high(n, 1, k)
                swish(k, 2, w)
                if next_kind:
                    split(k + 1, 1 - u, 1, next_kind)
                high(k, u, 2, w)
                if first:
                    w2_high(n, 2, k)
                swish(k, 3, w)
                high(k, u, 3, w)
                if first:
                    w2_high(n, 3, k)

            def after_shared():
                act.wait_ge(up, FC * GS)
                w1_high(1)

            def after(n, k, u, last):
                if not last:
                    act.wait_ge(up, FC * (k + 1))
                    w1_high(n + 1)

            w1_high(0)
            split(0, 0, 0, "shared")
            split(0, 0, 1, "shared")
            schedule(act, group, after_shared, after)

        @block.vector
        def _(dve):
            def w1_low(n, c):
                dve.wait_ge(w1h_set, C * n + (c + 1))
                nc.vector.tensor_tensor(w1l[:, c, :], raw1[:, c, :], w1h[:, c, :].bitcast(F32),
                                        ALU.subtract).then_inc(w1l_set, 1)

            def w2_low(n, c):
                dve.wait_ge(w2h_set, FC * n + (c + 1))
                nc.vector.tensor_tensor(w2l[:, c, :], raw2[:, c, :], w2h[:, c, :].bitcast(F32),
                                        ALU.subtract).then_inc(w2l_set, 1)

            def split(k, u, t, kind):
                w = width(kind)
                dve.wait_ge(zh_set, 2 * k + (t + 1))
                if kind == "shared":
                    nc.vector.tensor_tensor(zl[u][:, :, t * w:(t + 1) * w],
                                            zin[t][:, :].rearrange("p (c n) -> p c n", c=C),
                                            zh[u][:, :, t * w:(t + 1) * w].bitcast(F32),
                                            ALU.subtract).then_inc(zl_set, 1)
                else:
                    nc.vector.tensor_tensor(zl[u][:, :, t * w:(t + 1) * w].rearrange("p (b c) n -> p b c n", b=2),
                                            psT[:, :, 0:C // 2 * w].rearrange("p b (c n) -> p b c n", n=w),
                                            zh[u][:, :, t * w:(t + 1) * w].rearrange("p (b c) n -> p b c n", b=2).bitcast(F32),
                                            ALU.subtract).then_inc(zl_set, 1)

            def gate_up(k, j, w):
                dve.wait_ge(silu, FC * k + (j + 1))
                wait(dve, hl_set, FC * k + (j - 1))
                nc.vector.tensor_tensor(hid[j % 2][:, 0:2 * w], ps1[j % 2][:, 0, 0:2 * w],
                                        act_s[j % 2][:, 0:2 * w], ALU.mult).then_inc(gated, 1)

            def low(k, u, j, w):
                dve.wait_ge(hh_set, FC * k + (j + 1))
                nc.vector.tensor_tensor(hl[u][:, j, 0:2 * w], hid[j % 2][:, 0:2 * w],
                                        hh[u][:, j, 0:2 * w].bitcast(F32), ALU.subtract).then_inc(hl_set, 1)

            def result(k, t, half, kind):
                dve.wait_ge(down, 4 * k + (2 * t + half + 1))
                cols = slice(half * HALF, (half + 1) * HALF)
                if kind == "shared":
                    dve.wait_ge(res_in[t], 16 * k + 16)
                    nc.vector.scalar_tensor_tensor(out=y[t][:, cols], in0=ps2[t][:, half, 0:HALF], scalar=tg[:, 0:1],
                                                   in1=y[t][:, cols], op0=ALU.mult, op1=ALU.add).then_inc(y_set, 1)
                else:
                    r = k - GS
                    dve.wait_ge(y_free, 2 * r + (t + 1))
                    nc.vector.tensor_scalar(y[t][0:M, cols], ps2[t][0:M, half, 0:HALF],
                                            scale[:, bass.ds(2 * r + t, 1)], None, ALU.mult).then_inc(y_set, 1)

            def results(k, kind, n, chunks):
                per = -(-len(chunks) // 4)
                for q in range(4):
                    for c in chunks[q * per:(q + 1) * per]:
                        w1_low(n, c)
                    result(k, q // 2, q % 2, kind)

            def group(k, u, n, i, kind, next_kind):
                w = width(kind)
                first = isinstance(i, int) and i == 0
                for j in range(FC):
                    gate_up(k, j, w)
                    if next_kind and j % 2 == 0:
                        split(k + 1, 1 - u, j // 2, next_kind)
                    low(k, u, j, w)
                    if first:
                        w2_low(n, j)
                if not first:
                    turnover = next_kind == "routed" and (kind == "shared" or i == GE - 1)
                    results(k - 1, kind, n + 1, list(range(C // 2)) if turnover else [])

            def after_shared():
                results(GS - 1, "shared", 1, list(range(C // 2, C)))
                dve.wait_ge(list_in, 16)
                nc.vector.tensor_scalar(scale[:, :], lists[:, :, 1].bitcast(F32), tg[0:M, 0:1], None,
                                        ALU.mult).then_inc(scaled, 1)
                dve.wait_ge(scaled, 1)

            def after(n, k, u, last):
                results(k, "routed", n + 1, [] if last else list(range(C // 2, C)))

            dve.wait_ge(gate, 1)
            for c in range(C):
                w1_low(0, c)
            split(0, 0, 0, "shared")
            split(0, 0, 1, "shared")
            schedule(dve, group, after_shared, after)

        @block.tensor
        def _(pe):
            def turn(k, t):
                pe.wait_ge(z_got[t], 16 * (k - GS) + 16)
                pe.wait_ge(zh_set, 2 * k + t)
                pe.wait_ge(zl_set, 2 * k + t)
                for c in range(C):
                    cc = c % (C // 2)
                    last = nc.tensor.transpose(psT[:, c // (C // 2), cc * M:(cc + 1) * M],
                                               zin[t][0:M, c * P:(c + 1) * P], ident[0:M, 0:M])
                last.then_inc(z_turned, 1)

            def first_product(k, u, j, w):
                wait(pe, gated, FC * k + (j - 1))
                for b in range(2):
                    acc = ps1[j % 2][:, b, 0:2 * w]
                    cols = slice(b * F + j * P, b * F + (j + 1) * P)
                    for c in range(C):
                        nc.tensor.matmul(acc, w1h[:, c, cols], zh[u][:, c, 0:2 * w], start=(c == 0), stop=False)
                        nc.tensor.matmul(acc, w1h[:, c, cols], zl[u][:, c, 0:2 * w], start=False, stop=False)
                        last = nc.tensor.matmul(acc, w1l[:, c, cols], zh[u][:, c, 0:2 * w],
                                                start=False, stop=(c == C - 1))
                last.then_inc(up, 1)

            def second_product(k, u, w):
                pe.wait_ge(hh_set, FC * k + FC)
                pe.wait_ge(hl_set, FC * k + FC)
                for t in range(2):
                    rows = slice(t * w, (t + 1) * w)
                    for half in range(2):
                        wait(pe, y_set, 4 * k - 4 + (2 * t + half + 1))
                        acc = ps2[t][0:w, half, 0:HALF]
                        cols = slice(half * HALF, (half + 1) * HALF)
                        for f in range(FC):
                            nc.tensor.matmul(acc, hh[u][:, f, rows], w2h[:, f, cols], start=(f == 0), stop=False)
                            nc.tensor.matmul(acc, hh[u][:, f, rows], w2l[:, f, cols], start=False, stop=False)
                            last = nc.tensor.matmul(acc, hl[u][:, f, rows], w2h[:, f, cols],
                                                    start=False, stop=(f == FC - 1))
                        last.then_inc(down, 1)

            def group(k, u, n, i, kind, next_kind):
                w = width(kind)
                if isinstance(i, int) and i == 0:
                    pe.wait_ge(w1h_set, C * n + C)
                    pe.wait_ge(w1l_set, C * n + C)
                pe.wait_ge(zh_set, 2 * k + 2)
                pe.wait_ge(zl_set, 2 * k + 2)
                for j in range(FC):
                    first_product(k, u, j, w)
                    if next_kind == "routed" and j % 2 == 0:
                        turn(k + 1, j // 2)
                if not (isinstance(i, int) and i == 0):
                    if i == 1:
                        pe.wait_ge(w2h_set, FC * n + FC)
                        pe.wait_ge(w2l_set, FC * n + FC)
                    second_product(k - 1, 1 - u, w)

            def after_shared():
                second_product(GS - 1, 1, P)

            def after(n, k, u, last):
                second_product(k, u, M)

            pe.wait_ge(made, 2)
            schedule(pe, group, after_shared, after)


def build(nc, x, ctx_rev, g_xattn, g_ffn, ssm_kernel, D, gate_w, expert_bias, shared_w1, shared_w2,
          routed_w1, routed_w2, out):
    B, S, L = x.shape
    H, T, E = S // HD, B * S, gate_w.shape[1]
    capacity = max(1, T // E)
    slots = -(-capacity // 10) * 10

    def scratch(name, shape, dt=F32):
        return nc.dram_tensor(name, shape, dt).ap()

    filt_hi, filt_lo = scratch("filt_hi", (H, PAD)), scratch("filt_lo", (H, PAD))
    z_d = scratch("z_d", (T + P, L))
    zT_d = scratch("zT_d", (H, P, L // P, P))
    logit_d = scratch("logit_d", (P, H, E))
    list_d = scratch("list_d", (E * slots + P, 2), I32)
    prepare_filters(nc, ssm_kernel, D, filt_hi, filt_lo, z_d, out)
    gated_conv(nc, x, ctx_rev, g_xattn, gate_w, expert_bias, filt_hi, filt_lo, z_d, zT_d, logit_d, out)
    with (nc.sbuf_tensor("slot_of", [P, H, 2], I32) as slot_of,
          nc.sbuf_tensor("pay", [P, H, 2, 2], I32) as pay):
        route(nc, logit_d, slot_of, pay, capacity, slots, H)
        experts(nc, zT_d, z_d, slot_of, pay, list_d, g_ffn, shared_w1, shared_w2, routed_w1, routed_w2,
                out, slots, H)


_INS = ["x", "ctx_2048", "g_xattn", "g_ffn", "L0_xattn_ssm_kernel", "L0_xattn_D", "L0_ffn_gate_w",
        "L0_ffn_expert_bias", "L0_ffn_shared_w1", "L0_ffn_shared_w2", "L0_ffn_routed_w1", "L0_ffn_routed_w2"]


def kernel(**inputs):
    import concourse.bacc as bacc
    from concourse.bass_utils import run_bass_kernel_spmd

    nc = bacc.Bacc("TRN2", target_bir_lowering=False, num_devices=1)
    arrays, args = {}, []
    for name in _INS:
        a = np.asarray(inputs[name])
        if name == "ctx_2048":
            a = a[:, :, ::-1]
        a = np.ascontiguousarray(a)
        arrays[f"in_{name}"] = a
        args.append(nc.dram_tensor(f"in_{name}", a.shape, mybir.dt.from_np(a.dtype), kind="ExternalInput").ap())
    B, S, L = inputs["x"].shape
    out = nc.dram_tensor("out_0", (B * S + P, L), F32, kind="ExternalOutput").ap()
    build(nc, *args, out)
    r = run_bass_kernel_spmd(nc, [arrays], core_ids=[0])
    return np.ascontiguousarray(r.results[0]["out_0"][:B * S].reshape(B, S, L))
```

```python
import math
import numpy as np
import concourse.bass as bass
from concourse import mybir
from contextlib import ExitStack

F32 = mybir.dt.float32
F32R = mybir.dt.float32r
I32 = mybir.dt.int32
ALU = mybir.AluOpType
ACT = mybir.ActivationFunctionType
AX = mybir.AxisListType

P = 128
BANK = 512
HD = 8
PAIRS = HD * (HD + 1) // 2
EPS = 1e-5
LN = slice(0, 2)
PAD = 1152


class Pool:

    def __init__(self, nc, ctx, tag):
        self.nc, self.ctx, self.tag = nc, ctx, tag

    def sb(self, name, shape, dt=F32):
        return self.ctx.enter_context(self.nc.sbuf_tensor(f"{self.tag}_{name}", shape, dt))

    def ps(self, name, shape, dt=F32):
        return self.ctx.enter_context(self.nc.psum_tensor(f"{self.tag}_{name}", shape, dt))

    def sem(self, name):
        return self.ctx.enter_context(self.nc.semaphore(f"{self.tag}_{name}"))


def identity_steps(nc, pool, ident, made):
    nc.gpsimd.memset(ident[:, :], 0.0).then_inc(made, 1)
    pool.wait_ge(made, 1)
    nc.gpsimd.affine_select(out=ident[:, :], in_=ident[:, :], compare_op=ALU.not_equal, fill=1.0,
                            base=0, pattern=[[-1, P]], channel_multiplier=1).then_inc(made, 1)


def prepare_filters(nc, ssm_kernel, D, filt_hi, filt_lo, z_d, out):
    H, L = ssm_kernel.shape
    T = z_d.shape[0] - P
    with ExitStack() as ctx:
        m = Pool(nc, ctx, "fil")
        full = m.sb("full", [H, PAD])
        hi = m.sb("hi", [H, PAD], F32R)
        lo = m.sb("lo", [H, PAD], F32R)
        d = m.sb("d", [H, 1])
        zero = m.sb("zero", [P, L])
        cleared, loaded, tapped, rounded, split, zeroed, stored = (
            m.sem(n) for n in ("cleared", "loaded", "tapped", "rounded", "split", "zeroed", "stored"))
        block = ctx.enter_context(nc.Block())

        @block.sync
        def _(sp):
            sp.wait_ge(cleared, 1)
            sp.dma_start(full[:, P - 1:P - 1 + L], ssm_kernel).then_inc(loaded, 16)
            sp.dma_start(d[:, :], D.rearrange("(h a) -> h a", a=1)).then_inc(loaded, 16)
            sp.wait_ge(zeroed, 1)
            sp.dma_start(z_d[T:T + P, :], zero[:, :]).then_inc(stored, 16)
            sp.dma_start(out[T:T + P, :], zero[:, :]).then_inc(stored, 16)
            sp.wait_ge(split, 1)
            sp.dma_start(filt_hi, hi[:, :].bitcast(F32)).then_inc(stored, 16)
            sp.dma_start(filt_lo, lo[:, :].bitcast(F32)).then_inc(stored, 16)
            sp.wait_ge(stored, 64)

        @block.vector
        def _(dve):
            nc.vector.memset(full[:, :], 0.0).then_inc(cleared, 1)
            nc.vector.memset(zero[:, :], 0.0).then_inc(zeroed, 1)
            dve.wait_ge(loaded, 32)
            nc.vector.tensor_tensor(full[:, P - 1:P], full[:, P - 1:P], d[:, :], ALU.add).then_inc(tapped, 1)
            dve.wait_ge(tapped, 1)
            nc.vector.tensor_copy(hi[:, :], full[:, :]).then_inc(rounded, 1)
            dve.wait_ge(rounded, 1)
            nc.vector.tensor_tensor(lo[:, :], full[:, :], hi[:, :].bitcast(F32), ALU.subtract).then_inc(split, 1)


def gated_conv(nc, x, xT, cT, g_xattn, gate_w, expert_bias, filt_hi, filt_lo, z_d, zT_d, logit_d, out):
    B, S, L = x.shape
    H = S // HD
    NT = L // P
    G = NT // 2
    E = gate_w.shape[1]
    NB = B // 2
    assert B * HD == P and H % 2 == 0 and H >= 6
    off = [sum(HD - r for r in range(i)) for i in range(HD)]

    x_rows = x.rearrange("b (h j) l -> h b j l", j=HD)
    z_rows = z_d[0:B * S, :].rearrange("(b h j) l -> h b j l", b=B, j=HD)
    o_rows = out[0:B * S, :].rearrange("(b h j) l -> h b j l", b=B, j=HD)

    def toeplitz(filt):
        return bass.AP(filt.tensor, 0, [[PAD, H], [1, P], [1, L]])

    t_hi, t_lo = toeplitz(filt_hi), toeplitz(filt_lo)

    with ExitStack() as ctx:
        m = Pool(nc, ctx, "att")
        xn = m.sb("xn", [P, L])
        kT = m.sb("kT", [P, NT, B, HD])
        qT = [m.sb(f"qT{u}", [P, NT, B, HD]) for u in range(2)]
        kv = m.sb("kv", [P, G, B, PAIRS])
        kv_hi = [m.sb(f"kv_hi{u}", [P, NT, B, PAIRS], F32R) for u in range(2)]
        kv_lo = [m.sb(f"kv_lo{u}", [P, NT, B, PAIRS], F32R) for u in range(2)]
        tz_hi = [m.sb(f"tz_hi{u}", [P, L], F32R) for u in range(2)]
        tz_lo = [m.sb(f"tz_lo{u}", [P, L], F32R) for u in range(2)]
        y = [m.sb(f"y{u}", [P, NT, B, PAIRS]) for u in range(2)]
        prod = m.sb("prod", [P, G * B, HD, HD])
        oT = m.sb("oT", [P, NT, B * HD])
        x1 = m.sb("x1", [P, L])
        z = m.sb("z", [P, L])
        zT = [m.sb(f"zT{u}", [P, NT, P]) for u in range(2)]
        ident = m.sb("ident", [P, P])
        ones = m.sb("ones", [P, P])
        gw = m.sb("gw", [P, NT, E])
        bias = m.sb("bias", [P, E])
        g = m.sb("g", [P, 1])
        tg = m.sb("tg", [P, 1])
        eps = m.sb("eps", [P, 1])
        minus_half = m.sb("minus_half", [P, 1])
        logit = m.sb("logit", [P, H, E])
        stats = [m.sb(f"stats{k}", [P, 2, 6]) for k in range(2)]
        mv = [m.sb(f"mv{k}", [P, 2]) for k in range(2)]
        root = [m.sb(f"root{k}", [P, 2]) for k in range(2)]
        diag = [m.sb(f"diag{k}", [P, 2, P]) for k in range(2)]
        spread = [m.sb(f"spread{k}", [P, 2, P]) for k in range(2)]
        minus = m.sb("minus", [P, 1])

        psY = [m.ps(f"psY{u}", [P, 2, BANK]) for u in range(2)]
        psO = m.ps("psO", [P, L])
        psB = m.ps("psB", [P, 2, 2 * P])
        psL = m.ps("psL", [P, E])

        const = m.sem("const")
        made = m.sem("made")
        oned = m.sem("oned")
        gate = m.sem("gate")
        passed = m.sem("passed")
        xn_in, kT_in = m.sem("xn_in"), m.sem("kT_in")
        xT_in = [m.sem(f"xT_in{u}") for u in range(2)]
        rT_in = [m.sem(f"rT_in{u}") for u in range(2)]
        tz_in = [m.sem(f"tz_in{u}") for u in range(2)]
        z_out, x1_out, l_out = m.sem("z_out"), m.sem("x1_out"), m.sem("l_out")
        zT_out = [m.sem(f"zT_out{u}") for u in range(2)]
        o_turned = m.sem("o_turned")
        y_done = m.sem("y_done")
        l_done = m.sem("l_done")
        spread_done = [m.sem(f"spread_done{k}") for k in range(2)]
        spread_set = [m.sem(f"spread_set{k}") for k in range(2)]
        y_set = m.sem("y_set")
        hi_set = m.sem("hi_set")
        z_set = m.sem("z_set")
        minus_set = m.sem("minus_set")
        kv_set = m.sem("kv_set")
        rooted = [m.sem(f"rooted{k}") for k in range(2)]
        diag_set = [m.sem(f"diag_set{k}") for k in range(2)]
        q_set = m.sem("q_set")
        zT_set = m.sem("zT_set")
        lo_set = m.sem("lo_set")
        told = [m.sem(f"told{k}") for k in range(2)]
        multiplied = m.sem("multiplied")
        first_set = m.sem("first_set")
        summed = m.sem("summed")
        x1_set = m.sem("x1_set")
        x1T_set = m.sem("x1T_set")
        l_set = m.sem("l_set")
        ROOT = 3

        block = ctx.enter_context(nc.Block())

        def keys_of(half):
            return slice((1 - half) * G, (2 - half) * G)

        def wait(eng, sem, value):
            if not (isinstance(value, int) and value <= 0):
                eng.wait_ge(sem, value)

        def steady(eng, step):
            for h in range(4):
                step(h, h % 2, True, h >= 1, h >= 2, h >= 3)
            with eng.Fori(2, H // 2 - 1) as pair:
                h = 2 * pair
                step(h, 0, True, True, True, True)
                step(h + 1, 1, True, True, True, True)
            step(H - 2, 0, True, True, True, True)
            step(H - 1, 1, False, True, True, True)

        def uses(n, u):
            return 8 * (n - u) + 16

        @block.sync
        def _(sp):
            sp.dma_start(gw[:, :, :], gate_w.rearrange("(c p) e -> p c e", p=P)).then_inc(const, 16)
            sp.dma_start(bias[:, :], expert_bias.rearrange("(a e) -> a e", a=1).to_broadcast([P, E])).then_inc(const, 16)
            sp.dma_start(g[:, :], g_xattn.rearrange("(a e) -> a e", a=1).to_broadcast([P, 1])).then_inc(const, 16)

            def load_stats(h):
                wait(sp, told[0], 3 * h - 1)
                sp.dma_start(xn[:, :], x_rows[h]).then_inc(xn_in, 16)

            def load_keys(h):
                wait(sp, kv_set, 2 * h)
                sp.dma_start(kT[:, :, :, :].rearrange("p t b i -> p t (b i)"), cT[h]).then_inc(kT_in, 16)

            def load_queries(h, u):
                wait(sp, summed, 2 * (h - 1))
                sp.dma_start(qT[u][:, :, :, :].rearrange("p t b i -> p t (b i)"), xT[h]).then_inc(xT_in[u], 16)

            def load_filter(h, u):
                wait(sp, y_done, NT * (h - 1))
                sp.dma_start(tz_hi[u][:, :].bitcast(F32), t_hi[h]).then_inc(tz_in[u], 16)
                sp.dma_start(tz_lo[u][:, :].bitcast(F32), t_lo[h]).then_inc(tz_in[u], 16)

            def load_residual_T(h, u):
                if not (isinstance(h, int) and h < 2):
                    sp.wait_ge(zT_out[u], uses(h - 2, u))
                    sp.sem_inc(passed, 1)
                    sp.wait_ge(l_done, h - 1)
                sp.dma_start(zT[u][:, :, :], xT[h]).then_inc(rT_in[u], 16)

            def store_x1(h):
                sp.wait_ge(x1_set, h + 1)
                sp.dma_start(o_rows[h], x1[:, :]).then_inc(x1_out, 16)

            def store_z(h):
                sp.wait_ge(z_set, h + 1)
                sp.dma_start(z_rows[h], z[:, :]).then_inc(z_out, 16)

            def store_zT(h, u):
                sp.wait_ge(zT_set, 2 * h + 2)
                sp.dma_start(zT_d[h], zT[u][:, :, :]).then_inc(zT_out[u], 16)

            load_keys(0)
            load_filter(0, 0)
            load_stats(0)
            load_keys(1)

            def step(h, u, ahead, back, back2, back3):
                if ahead:
                    load_filter(h + 1, 1 - u)
                load_queries(h, u)
                if ahead:
                    load_stats(h + 1)
                if back3:
                    store_zT(h - 3, 1 - u)
                if back:
                    load_residual_T(h - 1, 1 - u)
                if not (isinstance(h, int) and h >= H - 2):
                    load_keys(h + 2)
                if back2:
                    store_x1(h - 2)
                if back2:
                    store_z(h - 2)

            steady(sp, step)
            store_zT(H - 3, 1)
            load_residual_T(H - 1, 1)
            store_x1(H - 2)
            store_z(H - 2)
            store_zT(H - 2, 0)
            store_x1(H - 1)
            store_z(H - 1)
            store_zT(H - 1, 1)
            sp.wait_ge(l_set, H)
            sp.dma_start(logit_d, logit[:, :, :]).then_inc(l_out, 16)
            for u in range(2):
                sp.wait_ge(zT_out[u], 8 * H)
            sp.wait_ge(x1_out, 16 * H)
            sp.wait_ge(z_out, 16 * H)
            sp.wait_ge(l_out, 16)

        @block.gpsimd
        def _(pool):
            identity_steps(nc, pool, ident, made)
            nc.gpsimd.memset(eps[:, :], EPS).then_inc(made, 1)
            nc.gpsimd.memset(minus_half[:, :], -0.5).then_inc(made, 1)
            nc.gpsimd.memset(ones[:, :], 1.0).then_inc(oned, 1)
            pool.wait_ge(made, 4)

            def roots(k, h):
                def link(ins, n):
                    ins.then_inc(rooted[k], 1)
                    pool.wait_ge(rooted[k], ROOT * h + n)

                pool.wait_ge(told[k], 3 * h + 3)
                wait(pool, diag_set[k], 2 * h)
                if k == 1:
                    wait(pool, z_set, h)
                link(nc.gpsimd.tensor_tensor(root[k][:, 0:1], mv[k][:, 1:2], eps[:, :], ALU.add), 1)
                link(nc.gpsimd.tensor_tensor(root[k][:, 0:1], root[k][:, 0:1], minus_half[:, :], ALU.pow), 2)
                link(nc.gpsimd.tensor_tensor(root[k][:, 1:2], mv[k][:, 0:1], root[k][:, 0:1], ALU.mult), 3)

            def pairs(h, half):
                pool.wait_ge(kT_in, 16 * h + 16)
                wait(pool, lo_set, 2 * h + half)
                wait(pool, hi_set, 2 * h + half)
                ks = kT[:, keys_of(half)].rearrange("p t b i -> p (t b) i")
                dst = kv[:, :, :, :].rearrange("p t b i -> p (t b) i")
                for i in range(HD):
                    last = nc.gpsimd.tensor_tensor(dst[:, :, off[i]:off[i] + HD - i], ks[:, :, i:HD],
                                                   ks[:, :, i:i + 1].to_broadcast([P, G * B, HD - i]), ALU.mult)
                last.then_inc(kv_set, 1)

            def normalise(t, k, done, h):
                pool.wait_ge(spread_set[k], h + 1)
                for n, op in enumerate((ALU.mult, ALU.subtract)):
                    nc.gpsimd.tensor_tensor(t, t, spread[k][:, n:n + 1, :].to_broadcast([P, NT, P]), op).then_inc(done, 1)
                    pool.wait_ge(done, 2 * h + (n + 1))

            def queries(h, u):
                pool.wait_ge(xT_in[u], uses(h, u))
                normalise(qT[u][:, :, :, :].rearrange("p t b i -> p t (b i)"), 0, q_set, h)

            def first_terms(h, u, half):
                pool.wait_ge(y_set, NT * h + G * (half + 1))
                wait(pool, summed, 2 * h + half)
                ys = y[u][:, half * G:(half + 1) * G].rearrange("p t b i -> p (t b) i")
                qs = qT[u][:, half * G:(half + 1) * G].rearrange("p t b i -> p (t b) i")
                nc.gpsimd.tensor_tensor(prod[:, :, 0:HD, 0], ys[:, :, 0:HD],
                                        qs[:, :, 0:1].to_broadcast([P, G * B, HD]), ALU.mult)
                nc.gpsimd.tensor_tensor(prod[:, :, 0, 1:HD], ys[:, :, 1:HD], qs[:, :, 1:HD],
                                        ALU.mult).then_inc(first_set, 1)

            def z_turned(h, u):
                pool.wait_ge(o_turned, h + 1)
                normalise(zT[u][:, :, :], 1, zT_set, h)

            pairs(0, 0)
            pairs(0, 1)
            pairs(1, 0)

            def step(h, u, ahead, back, back2, back3):
                roots(0, h)
                if back:
                    first_terms(h - 1, 1 - u, 1)
                if ahead:
                    pairs(h + 1, 1)
                if back2:
                    roots(1, h - 2)
                queries(h, u)
                if back2:
                    z_turned(h - 2, u)
                if not (isinstance(h, int) and h >= H - 2):
                    pairs(h + 2, 0)
                first_terms(h, u, 0)

            steady(pool, step)
            first_terms(H - 1, 1, 1)
            for h in (H - 2, H - 1):
                roots(1, h)
                z_turned(h, h % 2)

        @block.scalar
        def _(act):
            act.wait_ge(const, 48)
            act.wait_ge(made, 2)
            nc.scalar.activation(tg[:, :], g[:, :], ACT.Tanh).then_inc(gate, 1)

            def spread_out(k, h):
                act.wait_ge(spread_done[k], h + 1)
                if k == 0:
                    wait(act, q_set, 2 * h)
                else:
                    wait(act, zT_set, 2 * h)
                nc.scalar.activation(spread[k][:, :, :], psB[:, k, :].rearrange("p (n r) -> p n r", n=2),
                                     ACT.Copy).then_inc(spread_set[k], 1)

            def diagonals(k, h):
                act.wait_ge(rooted[k], ROOT * h + ROOT)
                wait(act, spread_done[k], h)
                for n in range(2):
                    nc.scalar.activation(diag[k][:, n, :], ident[:, :], ACT.Identity,
                                         scale=root[k][:, n:n + 1]).then_inc(diag_set[k], 1)

            def normal(h):
                act.wait_ge(rooted[1], ROOT * h + 3)
                nc.scalar.activation(minus[:, :], root[1][:, 1:2], ACT.Copy, scale=-1.0).then_inc(minus_set, 1)
                act.wait_ge(minus_set, h + 1)
                wait(act, z_out, 16 * h)
                nc.scalar.activation(z[:, :], x1[:, :], ACT.Identity, bias=minus[:, 0:1],
                                     scale=root[1][:, 0:1]).then_inc(z_set, 1)

            def rows(h):
                act.wait_ge(o_turned, h + 1)
                wait(act, x1_out, 16 * h)
                nc.scalar.activation(x1[:, :], psO[:, :], ACT.Copy).then_inc(x1_set, 1)

            def high(h, u, half):
                act.wait_ge(kv_set, 2 * h + half + 1)
                wait(act, y_done, NT * (h - 1))
                nc.scalar.activation(kv_hi[u][:, keys_of(half)].rearrange("p t b i -> p (t b i)"),
                                     kv[:, :, :, :].rearrange("p t b i -> p (t b i)"), ACT.Copy).then_inc(hi_set, 1)

            def conv_out(h, u, a):
                act.wait_ge(y_done, NT * h + a + 1)
                if a == 0:
                    wait(act, multiplied, 2 * (h - 1))
                    wait(act, first_set, 2 * (h - 1))
                nc.scalar.activation(y[u][:, a].rearrange("p (c b) i -> p c (b i)", c=2),
                                     psY[a % 2][:, :, 0:NB * PAIRS], ACT.Copy).then_inc(y_set, 1)

            high(0, 0, 0)
            high(0, 0, 1)

            def step(h, u, ahead, back, back2, back3):
                conv_out(h, u, 0)
                conv_out(h, u, 1)
                if ahead:
                    high(h + 1, 1 - u, 0)
                conv_out(h, u, 2)
                if back2:
                    rows(h - 2)
                diagonals(0, h)
                conv_out(h, u, 3)
                spread_out(0, h)
                conv_out(h, u, 4)
                if back2:
                    diagonals(1, h - 2)
                    normal(h - 2)
                if ahead:
                    high(h + 1, 1 - u, 1)
                conv_out(h, u, 5)
                if back2:
                    spread_out(1, h - 2)
                for a in range(6, NT):
                    conv_out(h, u, a)

            steady(act, step)
            rows(H - 2)
            diagonals(1, H - 2)
            normal(H - 2)
            spread_out(1, H - 2)
            rows(H - 1)
            diagonals(1, H - 1)
            normal(H - 1)
            spread_out(1, H - 1)

        @block.vector
        def _(dve):
            def tell(k, h, src):
                wait(dve, rooted[k], ROOT * h)
                for c in range(2):
                    nc.vector.bn_stats(stats[k][:, c, :], src[:, c * (L // 2):(c + 1) * (L // 2)]).then_inc(told[k], 1)
                dve.wait_ge(told[k], 3 * h + 2)
                dve.sem_inc(passed, 1)
                nc.vector.bn_aggr(mv[k][:, :], stats[k][:, :, :].rearrange("p a b -> p (a b)")).then_inc(told[k], 1)

            def tell_x(h):
                dve.wait_ge(xn_in, 16 * h + 16)
                tell(0, h, xn)

            def low(h, u, half):
                dve.wait_ge(hi_set, 2 * h + half + 1)
                nc.vector.tensor_tensor(kv_lo[u][:, keys_of(half)].rearrange("p t b i -> p (t b i)"),
                                        kv[:, :, :, :].rearrange("p t b i -> p (t b i)"),
                                        kv_hi[u][:, keys_of(half)].rearrange("p t b i -> p (t b i)").bitcast(F32),
                                        ALU.subtract).then_inc(lo_set, 1)

            def combine(h, u, half):
                dve.wait_ge(y_set, NT * h + G * (half + 1))
                dve.wait_ge(q_set, 2 * h + 2)
                wait(dve, summed, 2 * h + half)
                ys = y[u][:, half * G:(half + 1) * G].rearrange("p t b i -> p (t b) i")
                qs = qT[u][:, half * G:(half + 1) * G].rearrange("p t b i -> p (t b) i")
                for i in range(1, HD):
                    n = HD - i
                    last = nc.vector.tensor_tensor(prod[:, :, i:HD, i], ys[:, :, off[i]:off[i] + n],
                                                   qs[:, :, i:i + 1].to_broadcast([P, G * B, n]), ALU.mult)
                    if n > 1:
                        last = nc.vector.tensor_tensor(prod[:, :, i, i + 1:HD], ys[:, :, off[i] + 1:off[i] + n],
                                                       qs[:, :, i + 1:HD], ALU.mult)
                last.then_inc(multiplied, 1)
                dve.wait_ge(multiplied, 2 * h + half + 1)
                dve.wait_ge(first_set, 2 * h + half + 1)
                wait(dve, x1T_set, h)
                nc.vector.tensor_reduce(oT[:, half * G:(half + 1) * G, :].rearrange("p t (b j) -> p (t b) j", j=HD),
                                        prod[:, :, :, :], AX.X, ALU.add).then_inc(summed, 1)

            def residual(h, u):
                dve.wait_ge(summed, 2 * h + 2)
                dve.wait_ge(rT_in[u], uses(h, u))
                nc.vector.scalar_tensor_tensor(out=zT[u][:, :, :].rearrange("p t n -> p (t n)"),
                                               in0=oT[:, :, :].rearrange("p t n -> p (t n)"), scalar=tg[:, 0:1],
                                               in1=zT[u][:, :, :].rearrange("p t n -> p (t n)"),
                                               op0=ALU.mult, op1=ALU.add).then_inc(x1T_set, 1)

            def tell_x1(h):
                dve.wait_ge(x1_set, h + 1)
                tell(1, h, x1)

            def logits(h):
                dve.wait_ge(l_done, h + 1)
                nc.vector.tensor_tensor(logit[:, h, :], psL[:, 0:E], bias[:, :], ALU.add).then_inc(l_set, 1)

            tell_x(0)
            low(0, 0, 0)
            low(0, 0, 1)
            dve.wait_ge(gate, 1)
            dve.wait_ge(const, 48)

            def step(h, u, ahead, back, back2, back3):
                if back:
                    combine(h - 1, 1 - u, 0)
                if ahead:
                    low(h + 1, 1 - u, 0)
                if back2:
                    tell_x1(h - 2)
                if back:
                    combine(h - 1, 1 - u, 1)
                if ahead:
                    low(h + 1, 1 - u, 1)
                if back3:
                    logits(h - 3)
                if ahead:
                    tell_x(h + 1)
                if back:
                    residual(h - 1, 1 - u)

            steady(dve, step)
            combine(H - 1, 1, 0)
            tell_x1(H - 2)
            combine(H - 1, 1, 1)
            logits(H - 3)
            residual(H - 1, 1)
            logits(H - 2)
            tell_x1(H - 1)
            logits(H - 1)

        @block.tensor
        def _(pe):
            def conv(h, u, tiles):
                for a in tiles:
                    if a == 0:
                        pe.wait_ge(hi_set, 2 * h + 1)
                        pe.wait_ge(lo_set, 2 * h + 1)
                        pe.wait_ge(tz_in[u], 2 * uses(h, u))
                    if a == G:
                        pe.wait_ge(hi_set, 2 * h + 2)
                        pe.wait_ge(lo_set, 2 * h + 2)
                    wait(pe, y_set, NT * h + a - 1)
                    for c in range(a + 1):
                        for half in range(2):
                            acc = psY[a % 2][:, half, 0:NB * PAIRS]
                            d = (a - c) * P
                            hi = kv_hi[u][:, NT - 1 - c, half * NB:(half + 1) * NB, :].rearrange("p b i -> p (b i)")
                            lo = kv_lo[u][:, NT - 1 - c, half * NB:(half + 1) * NB, :].rearrange("p b i -> p (b i)")
                            nc.tensor.matmul(acc, tz_hi[u][:, d:d + P], hi, start=(c == 0), stop=False)
                            nc.tensor.matmul(acc, tz_hi[u][:, d:d + P], lo, start=False, stop=False)
                            last = nc.tensor.matmul(acc, tz_lo[u][:, d:d + P], hi, start=False, stop=(c == a))
                    last.then_inc(y_done, 1)

            def spread_in(k, h, other=0):
                pe.wait_ge(diag_set[k], 2 * h + 2)
                wait(pe, spread_set[k], h)
                wait(pe, spread_set[1 - k], h - 2 if k == 0 else other or h + 3)
                nc.tensor.matmul(psB[:, k, :], ones[:, :], diag[k][:, :, :].rearrange("p n r -> p (n r)"),
                                 start=True, stop=True).then_inc(spread_done[k], 1)

            def turn_x1(h, u):
                pe.wait_ge(x1T_set, h + 1)
                wait(pe, x1_set, h)
                for t in range(NT):
                    last = nc.tensor.transpose(psO[:, t * P:(t + 1) * P], zT[u][:, t, :], ident[:, :])
                last.then_inc(o_turned, 1)

            def logits(h, u):
                pe.wait_ge(zT_set, 2 * h + 2)
                wait(pe, l_set, h)
                for t in range(NT):
                    last = nc.tensor.matmul(psL[:, 0:E], zT[u][:, t, :], gw[:, t, :], start=(t == 0), stop=(t == NT - 1))
                last.then_inc(l_done, 1)

            pe.wait_ge(made, 2)
            pe.wait_ge(oned, 1)
            pe.wait_ge(const, 48)

            def step(h, u, ahead, back, back2, back3):
                conv(h, u, range(0, 2))
                if back3:
                    logits(h - 3, 1 - u)
                conv(h, u, range(2, 3))
                if back2:
                    turn_x1(h - 2, u)
                conv(h, u, range(3, 4))
                spread_in(0, h)
                conv(h, u, range(4, 6))
                if back2:
                    spread_in(1, h - 2)
                conv(h, u, range(6, NT))

            steady(pe, step)
            logits(H - 3, 1)
            turn_x1(H - 2, 0)
            spread_in(1, H - 2, H)
            logits(H - 2, 0)
            turn_x1(H - 1, 1)
            spread_in(1, H - 1, H)
            logits(H - 1, 1)


def route(nc, logit_d, slot_of, pay, capacity, slots, H):
    E = logit_d.shape[2]
    S = H * HD
    BIG = float(1 << 22)
    with ExitStack() as ctx:
        m = Pool(nc, ctx, "rte")
        raw = m.sb("raw", [P, H, E])
        aff = m.sb("aff", [P, E, H])
        rank = m.sb("rank", [P, E, H])
        cmp = m.sb("cmp", [P, E, H])
        score = m.sb("score", [P, E, H])
        over = m.sb("over", [P, E, H])
        ties = m.sb("ties", [P, E, H])
        scan = [m.sb(f"scan{u}", [P, E, H]) for u in range(2)]
        slot = m.sb("slot", [P, E, H])
        a = m.sb("a", [P, E, H])
        b = m.sb("b", [P, E, H])
        first = m.sb("first", [P, H])
        second = m.sb("second", [P, H])
        none = m.sb("none", [P, H])
        spare = m.sb("spare", [P, H])
        gap = m.sb("gap", [P, H])
        token = m.sb("token", [P, H])
        weight = m.sb("weight", [P, H])
        thr = m.sb("thr", [P, E], I32)
        cand = m.sb("cand", [P, E], I32)
        bit = m.sb("bit", [P, E], I32)
        count = m.sb("count", [P, E])
        keep = m.sb("keep", [P, E])
        base = m.sb("base", [P, E])
        room = m.sb("room", [P, E])
        ones = m.sb("ones", [P, P])
        row = m.sb("row", [P, P])
        col = m.sb("col", [P, P])
        rb = m.sb("rb", [P, P])
        cb = m.sb("cb", [P, P])
        same = m.sb("same", [P, P])
        before = m.sb("before", [P, P])
        under = m.sb("under", [P, P])
        irow = m.sb("irow", [P, P], I32)
        icol = m.sb("icol", [P, P], I32)
        ibat = m.sb("ibat", [P, P], I32)
        itok = m.sb("itok", [P, H], I32)
        iexp = m.sb("iexp", [P, E], I32)
        psC = m.ps("psC", [P, E])
        psR = m.ps("psR", [P, E * H])

        loaded, numbered, negexp, counted, dch, tallied, ranked = (
            m.sem(n) for n in ("loaded", "numbered", "negexp", "counted", "dch", "tallied", "ranked"))
        block = ctx.enter_context(nc.Block())
        TALLIES = 30

        @block.sync
        def _(sp):
            sp.dma_start(raw[:, :, :], logit_d).then_inc(loaded, 16)

        @block.gpsimd
        def _(pool):
            nc.gpsimd.iota(irow[:, :], [[0, P]], base=0, channel_multiplier=1).then_inc(numbered, 1)
            nc.gpsimd.iota(icol[:, :], [[1, P]], base=0, channel_multiplier=0).then_inc(numbered, 1)
            nc.gpsimd.iota(itok[:, :], [[HD, H]], base=0, channel_multiplier=1).then_inc(numbered, 1)
            nc.gpsimd.iota(iexp[:, :], [[slots, E]], base=0, channel_multiplier=0).then_inc(numbered, 1)

        @block.scalar
        def _(act):
            act.wait_ge(loaded, 16)
            nc.scalar.activation(aff[:, :, :], raw[:, :, :].rearrange("p h e -> p e h"), ACT.Exp,
                                 scale=-1.0).then_inc(negexp, 1)

        @block.tensor
        def _(pe):
            with pe.Fori(0, TALLIES) as i:
                pe.wait_ge(counted, i + 1)
                nc.tensor.matmul(psC[:, :], ones[:, :], count[:, :], start=True, stop=True).then_inc(tallied, 1)
            pe.wait_ge(counted, TALLIES + 1)
            nc.tensor.matmul(psC[:, :], ones[:, :], count[:, :], start=True, stop=True).then_inc(tallied, 1)
            for n, what in enumerate((ties, slot)):
                pe.wait_ge(counted, TALLIES + 2 + n)
                flat = what[:, :, :].rearrange("p e h -> p (e h)")
                nc.tensor.matmul(psR[:, :], under[:, :], flat, start=True, stop=False)
                nc.tensor.matmul(psR[:, :], same[:, :], scan[0][:, :, :].rearrange("p e h -> p (e h)"),
                                 start=False, stop=False)
                nc.tensor.matmul(psR[:, :], before[:, :], scan[1][:, :, :].rearrange("p e h -> p (e h)"),
                                 start=False, stop=True).then_inc(ranked, 1)

        @block.vector
        def _(dve):
            done = [0]

            def link(ins):
                done[0] += 1
                ins.then_inc(dch, 1)
                dve.wait_ge(dch, done[0])

            v = nc.vector
            dve.wait_ge(numbered, 4)
            v.memset(ones[:, :], 1.0)
            v.memset(thr[:, :], 0)
            v.memset(bit[:, :], 1 << (TALLIES - 1))
            v.tensor_copy(row[:, :], irow[:, :])
            v.tensor_copy(col[:, :], icol[:, :])
            v.tensor_copy(token[:, :], itok[:, :])
            v.tensor_copy(base[:, :], iexp[:, :])
            v.tensor_scalar(spare[:, :], itok[:, 0:1].to_broadcast([P, H]), float(E * slots), None, ALU.add)
            link(v.tensor_scalar(ibat[:, :], irow[:, :], 3, None, ALU.logical_shift_right))
            link(v.tensor_copy(rb[:, :], ibat[:, :]))
            link(v.tensor_scalar(ibat[:, :], icol[:, :], 3, None, ALU.logical_shift_right))
            link(v.tensor_copy(cb[:, :], ibat[:, :]))
            link(v.scalar_tensor_tensor(out=token[:, :], in0=rb[:, 0:H], scalar=float(S - HD), in1=token[:, :],
                                        op0=ALU.mult, op1=ALU.add))
            v.tensor_tensor(same[:, :], rb[:, :], cb[:, :], ALU.is_equal)
            v.tensor_tensor(before[:, :], rb[:, :], cb[:, :], ALU.is_lt)
            link(v.tensor_tensor(under[:, :], row[:, :], col[:, :], ALU.is_lt))
            link(v.tensor_tensor(under[:, :], under[:, :], same[:, :], ALU.mult))

            dve.wait_ge(negexp, 1)
            link(v.tensor_scalar(aff[:, :, :], aff[:, :, :], 1.0, None, ALU.add))
            link(v.reciprocal(aff[:, :, :], aff[:, :, :]))

            link(v.memset(rank[:, :, :], 0.0))
            for d in range(1, E):
                lower, upper = slice(0, E - d), slice(d, E)
                link(v.tensor_tensor(cmp[:, lower, :], aff[:, lower, :], aff[:, upper, :], ALU.is_ge))
                link(v.tensor_tensor(rank[:, upper, :], rank[:, upper, :], cmp[:, lower, :], ALU.add))
                link(v.scalar_tensor_tensor(out=rank[:, lower, :].rearrange("p e h -> p (e h)"),
                                            in0=rank[:, lower, :].rearrange("p e h -> p (e h)"), scalar=1.0,
                                            in1=cmp[:, lower, :].rearrange("p e h -> p (e h)"),
                                            op0=ALU.add, op1=ALU.subtract))
            link(v.tensor_scalar(rank[:, :, :], rank[:, :, :], 2.0, None, ALU.is_lt))
            link(v.tensor_tensor(score[:, :, :], aff[:, :, :], rank[:, :, :], ALU.mult))
            link(v.scalar_tensor_tensor(out=score[:, :, :], in0=rank[:, :, :], scalar=-1.0, in1=score[:, :, :],
                                        op0=ALU.add, op1=ALU.add))

            linked = done[0]
            STEPS = 6
            with dve.Fori(0, TALLIES) as i:
                def step(ins, n):
                    ins.then_inc(dch, 1)
                    dve.wait_ge(dch, i * STEPS + (linked + n))

                step(v.tensor_tensor(cand[:, :], thr[:, :], bit[:, :], ALU.bitwise_or), 1)
                step(v.tensor_tensor(cmp[:, :, :], score[:, :, :],
                                     cand[:, :].bitcast(F32).unsqueeze(2).to_broadcast([P, E, H]), ALU.is_ge), 2)
                v.tensor_reduce(count[:, :], cmp[:, :, :], AX.X, ALU.add).then_inc(counted, 1)
                step(v.tensor_scalar(bit[:, :], bit[:, :], 1, None, ALU.logical_shift_right), 3)
                dve.wait_ge(tallied, i + 1)
                step(v.scalar_tensor_tensor(out=keep[:, :], in0=psC[:, :], scalar=float(capacity),
                                            in1=cand[:, :].bitcast(F32), op0=ALU.is_ge, op1=ALU.mult), 4)
                step(v.tensor_tensor(keep[:, :], keep[:, :], thr[:, :].bitcast(F32), ALU.max), 5)
                step(v.tensor_copy(thr[:, :].bitcast(F32), keep[:, :]), 6)
            done[0] = linked + STEPS * TALLIES

            limit = thr[:, :].bitcast(F32).unsqueeze(2).to_broadcast([P, E, H])
            v.tensor_tensor(ties[:, :, :], score[:, :, :], limit, ALU.is_equal)
            link(v.tensor_tensor(over[:, :, :], score[:, :, :], limit, ALU.is_gt))
            v.tensor_reduce(count[:, :], over[:, :, :], AX.X, ALU.add).then_inc(counted, 1)
            dve.wait_ge(tallied, TALLIES + 1)
            link(v.tensor_scalar(room[:, :], psC[:, :], -1.0, float(capacity), ALU.mult, ALU.add))

            def earlier(what, n):
                link(v.tensor_copy(scan[0][:, :, :], what[:, :, :]))
                d = 1
                while d < H:
                    link(v.tensor_copy(scan[1][:, :, :], scan[0][:, :, :]))
                    link(v.tensor_tensor(scan[0][:, :, d:H], scan[1][:, :, d:H], scan[1][:, :, 0:H - d], ALU.add))
                    d *= 2
                link(v.tensor_copy(scan[1][:, :, :], scan[0][:, :, H - 1:H].to_broadcast([P, E, H])))
                v.tensor_tensor(scan[0][:, :, :], scan[0][:, :, :], what[:, :, :], ALU.subtract).then_inc(counted, 1)
                dve.wait_ge(ranked, n + 1)

            earlier(ties, 0)
            rows = psR[:, :].rearrange("p (e h) -> p e h", e=E)
            link(v.tensor_tensor(cmp[:, :, :], rows, room[:, :].unsqueeze(2).to_broadcast([P, E, H]), ALU.is_lt))
            link(v.tensor_tensor(cmp[:, :, :], cmp[:, :, :], ties[:, :, :], ALU.mult))
            link(v.tensor_tensor(slot[:, :, :], cmp[:, :, :], over[:, :, :], ALU.add))
            earlier(slot, 1)
            link(v.tensor_tensor(a[:, :, :], rows, base[:, :].unsqueeze(2).to_broadcast([P, E, H]), ALU.add))
            link(v.tensor_scalar(b[:, :, :], a[:, :, :], -BIG, None, ALU.add))
            link(v.tensor_tensor(b[:, :, :], b[:, :, :], slot[:, :, :], ALU.mult))
            link(v.tensor_scalar(b[:, :, :], b[:, :, :], BIG, None, ALU.add))
            link(v.tensor_reduce(first[:, :], b[:, :, :].rearrange("p e h -> p h e"), AX.X, ALU.min))
            link(v.tensor_tensor(cmp[:, :, :], b[:, :, :], first[:, :].unsqueeze(1).to_broadcast([P, E, H]), ALU.is_equal))
            link(v.tensor_tensor(cmp[:, :, :], cmp[:, :, :], aff[:, :, :], ALU.mult))
            link(v.tensor_tensor(cmp[:, :, :], cmp[:, :, :], slot[:, :, :], ALU.mult))
            link(v.tensor_reduce(weight[:, :], cmp[:, :, :].rearrange("p e h -> p h e"), AX.X, ALU.add))
            link(v.tensor_copy(pay[:, :, 0, 1].bitcast(F32), weight[:, :]))
            link(v.tensor_scalar(a[:, :, :], a[:, :, :], 1.0, None, ALU.add))
            link(v.tensor_tensor(a[:, :, :], a[:, :, :], slot[:, :, :], ALU.mult))
            link(v.tensor_reduce(second[:, :], a[:, :, :].rearrange("p e h -> p h e"), AX.X, ALU.max))
            link(v.tensor_tensor(cmp[:, :, :], a[:, :, :], second[:, :].unsqueeze(1).to_broadcast([P, E, H]), ALU.is_equal))
            link(v.tensor_tensor(cmp[:, :, :], cmp[:, :, :], aff[:, :, :], ALU.mult))
            link(v.tensor_tensor(cmp[:, :, :], cmp[:, :, :], slot[:, :, :], ALU.mult))
            link(v.tensor_reduce(weight[:, :], cmp[:, :, :].rearrange("p e h -> p h e"), AX.X, ALU.add))
            link(v.tensor_copy(pay[:, :, 1, 1].bitcast(F32), weight[:, :]))
            link(v.tensor_scalar(second[:, :], second[:, :], -1.0, None, ALU.add))
            link(v.tensor_tensor(none[:, :], second[:, :], first[:, :], ALU.is_le))
            link(v.tensor_tensor(gap[:, :], spare[:, :], second[:, :], ALU.subtract))
            link(v.tensor_tensor(gap[:, :], gap[:, :], none[:, :], ALU.mult))
            link(v.tensor_tensor(second[:, :], second[:, :], gap[:, :], ALU.add))
            link(v.tensor_copy(slot_of[:, :, 1], second[:, :]))
            link(v.tensor_scalar(none[:, :], first[:, :], BIG, None, ALU.is_equal))
            link(v.tensor_tensor(gap[:, :], spare[:, :], first[:, :], ALU.subtract))
            link(v.tensor_tensor(gap[:, :], gap[:, :], none[:, :], ALU.mult))
            link(v.tensor_tensor(first[:, :], first[:, :], gap[:, :], ALU.add))
            link(v.tensor_copy(slot_of[:, :, 0], first[:, :]))
            for n in range(2):
                link(v.tensor_copy(pay[:, :, n, 0], token[:, :]))


def experts(nc, zT_d, z_d, slot_of, pay, list_d, g_ffn, shared_w1, shared_w2, routed_w1, routed_w2, out,
            slots, H):
    D, F2 = shared_w1.shape[1:]
    F = F2 // 2
    E = routed_w1.shape[0]
    C, FC = D // P, F // P
    GE = 5
    M = slots // (2 * GE)
    TILES = E * 2 * GE
    GS = H // 2
    HALF = D // 2
    B = P // HD
    T = B * H * HD
    assert slots == 2 * GE * M and M <= P and HALF <= BANK and GS % 2 == 0 and GS >= 6 and E % 2 == 1

    o_rows = out[0:T, :].rearrange("(b h j) l -> h b j l", b=B, j=HD)

    with ExitStack() as ctx:
        m = Pool(nc, ctx, "moe")
        w1h = m.sb("w1h", [P, C, F2], F32R)
        w1l = m.sb("w1l", [P, C, F2], F32R)
        w2h = m.sb("w2h", [P, FC, D], F32R)
        w2l = m.sb("w2l", [P, FC, D], F32R)
        raw = m.sb("raw", [P, C * F2])
        raw1 = raw[:, :].rearrange("p (c f) -> p c f", c=C)
        raw2 = raw[:, 0:FC * D].rearrange("p (c n) -> p c n", c=FC)
        zin = [m.sb(f"zin{t}", [P, D]) for t in range(2)]
        zh = [m.sb(f"zh{u}", [P, C, 2 * P], F32R) for u in range(2)]
        zl = [m.sb(f"zl{u}", [P, C, 2 * P], F32R) for u in range(2)]
        act_s = [m.sb(f"act_s{j}", [P, 2 * P]) for j in range(2)]
        hid = [m.sb(f"hid{j}", [P, 2 * P]) for j in range(2)]
        hh = [m.sb(f"hh{u}", [P, FC, 2 * P], F32R) for u in range(2)]
        hl = [m.sb(f"hl{u}", [P, FC, 2 * P], F32R) for u in range(2)]
        y = [m.sb(f"y{t}", [P, D]) for t in range(2)]
        ident = m.sb("ident", [P, P])
        g = m.sb("g", [P, 1])
        tg = m.sb("tg", [P, 1])
        lists = m.sb("lists", [M, TILES, 2], I32)
        scale = m.sb("scale", [M, TILES])
        stage_i = [m.sb(f"stage_i{n}", [P, 1], I32) for n in range(2)]
        stage_p = [m.sb(f"stage_p{n}", [P, 2], I32) for n in range(2)]
        get_i = [m.sb(f"get_i{t}", [M, 1], I32) for t in range(2)]
        add_i = [m.sb(f"add_i{t}", [M, 1], I32) for t in range(2)]

        ps1 = [m.ps(f"ps1_{j}", [P, 2, 2 * P]) for j in range(2)]
        ps2 = [m.ps(f"ps2_{t}", [P, 2, BANK]) for t in range(2)]
        psT = m.ps("psT", [P, 2, BANK])

        const = m.sem("const")
        made = m.sem("made")
        gate = m.sem("gate")
        passed = m.sem("passed")
        w1_in, w2_in = m.sem("w1_in"), m.sem("w2_in")
        w1h_set, w1l_set = m.sem("w1h_set"), m.sem("w1l_set")
        w2h_set, w2l_set = m.sem("w2h_set"), m.sem("w2l_set")
        z_in = [m.sem(f"z_in{t}") for t in range(2)]
        z_got = [m.sem(f"z_got{t}") for t in range(2)]
        z_turned = m.sem("z_turned")
        zh_set, zl_set = m.sem("zh_set"), m.sem("zl_set")
        up = m.sem("up")
        silu = m.sem("silu")
        gated = m.sem("gated")
        hh_set, hl_set = m.sem("hh_set"), m.sem("hl_set")
        down = m.sem("down")
        y_set = m.sem("y_set")
        res_in = [m.sem(f"res_in{t}") for t in range(2)]
        stored = [m.sem(f"stored{t}") for t in range(2)]
        list_made = m.sem("list_made")
        list_init = m.sem("list_init")
        staged = m.sem("staged")
        scattered = [m.sem(f"scattered{n}") for n in range(2)]
        list_in = m.sem("list_in")
        scaled = m.sem("scaled")
        got = m.sem("got")
        put = m.sem("put")
        added = m.sem("added")
        y_free = m.sem("y_free")

        block = ctx.enter_context(nc.Block())

        def wait(eng, sem, value):
            if not (isinstance(value, int) and value <= 0):
                eng.wait_ge(sem, value)

        LAST = GS + E * GE

        def schedule(eng, group, after_shared, after):
            group(0, 0, 0, 0, "shared", "shared")
            group(1, 1, 0, 1, "shared", "shared")
            group(2, 0, 0, 2, "shared", "shared")
            with eng.Fori(1, GS // 2 - 1) as p:
                group(2 * p + 1, 1, 0, 3, "shared", "shared")
                group(2 * p + 2, 0, 0, 4, "shared", "shared")
            group(GS - 1, 1, 0, GS - 1, "shared", "routed")
            after_shared()

            def expert(n, k0, u0, last):
                for i in range(GE):
                    group(k0 + i, (u0 + i) % 2, n, i, "routed", None if last and i == GE - 1 else "routed")
                after(n, k0 + GE - 1, (u0 + GE - 1) % 2, last)

            with eng.Fori(0, E // 2) as q:
                expert(2 * q + 1, 2 * GE * q + GS, 0, False)
                expert(2 * q + 2, 2 * GE * q + (GS + GE), 1, False)
            expert(E, GS + GE * (E - 1), 0, True)

        def width(kind):
            return P if kind == "shared" else M

        @block.sync
        def _(sp):
            def load_w1(n, src):
                wait(sp, w2h_set, FC * n)
                wait(sp, w2l_set, FC * n)
                sp.dma_start(raw1, src.rearrange("(c p) f -> p c f", p=P)).then_inc(w1_in, 16)

            def load_w2(n, src):
                sp.wait_ge(w1h_set, C * (n + 1))
                sp.wait_ge(w1l_set, C * (n + 1))
                sp.dma_start(raw2, src.rearrange("(c p) n -> p c n", p=P)).then_inc(w2_in, 16)

            def load_z(k):
                for t in range(2):
                    wait(sp, zh_set, 2 * k + t - 1)
                    wait(sp, zl_set, 2 * k + t - 1)
                    sp.dma_start(zin[t][:, :], zT_d[2 * k + t].rearrange("p c n -> p (c n)")).then_inc(z_in[t], 16)

            def residual(k):
                for t in range(2):
                    wait(sp, stored[t], 16 * k)
                    sp.dma_start(y[t][:, :], o_rows[2 * k + t]).then_inc(res_in[t], 16)

            def store(k):
                for t in range(2):
                    sp.wait_ge(y_set, 4 * k + 2 * t + 2)
                    sp.dma_start(o_rows[2 * k + t], y[t][:, :]).then_inc(stored[t], 16)

            sp.dma_start(g[:, :], g_ffn.rearrange("(a e) -> a e", a=1).to_broadcast([P, 1])).then_inc(const, 16)
            load_w1(0, shared_w1[0])
            load_z(0)
            sp.wait_ge(list_made, 2)
            sp.dma_start(list_d[0:E * slots, :].rearrange("(r q) c -> q r c", q=M), lists[:, :, :]).then_inc(list_init, 16)
            load_w2(0, shared_w2[0])
            load_z(1)
            residual(0)
            load_w1(1, routed_w1[0])
            with sp.Fori(1, GS - 1) as k:
                load_z(k + 1)
                store(k - 1)
                residual(k)
            store(GS - 2)
            residual(GS - 1)
            store(GS - 1)
            for t in range(2):
                sp.wait_ge(stored[t], 16 * GS)
                sp.sem_inc(y_free, 1)
            load_w2(1, routed_w2[0])
            with sp.Fori(2, E + 1) as n:
                load_w1(n, routed_w1[n - 1])
                load_w2(n, routed_w2[n - 1])

        @block.gpsimd
        def _(pool):
            identity_steps(nc, pool, ident, made)
            nc.gpsimd.iota(lists[:, :, 0], [[0, TILES]], base=T, channel_multiplier=1).then_inc(list_made, 1)
            nc.gpsimd.memset(lists[:, :, 1], 0).then_inc(list_made, 1)
            pool.wait_ge(list_init, 16)
            def scatter_column(h):
                for n in range(2):
                    wait(pool, scattered[1 - n], h * 16 + 16 * n)
                    nc.gpsimd.tensor_copy(stage_i[n][:, :], slot_of[:, bass.ds(h, 1), n:n + 1].rearrange("p a b -> p (a b)")).then_inc(staged, 1)
                    nc.gpsimd.tensor_copy(stage_p[n][:, :], pay[:, bass.ds(h, 1), n, :].rearrange("p a b -> p (a b)")).then_inc(staged, 1)
                    pool.wait_ge(staged, h * 4 + (2 * n + 2))
                    pool.sem_inc(passed, 1)
                    nc.gpsimd.indirect_dma_start(list_d, bass.IndirectOffsetOnAxis(stage_i[n][:, 0:1], 0),
                                                 stage_p[n][:, :], None).then_inc(scattered[n], 16)

            scatter_column(0)
            with pool.Fori(1, H) as h:
                scatter_column(h)
            pool.wait_ge(scattered[0], 16 * H)
            pool.wait_ge(scattered[1], 16 * H)
            pool.dma_start(lists[:, :, :], list_d[0:E * slots, :].rearrange("(r q) c -> q r c", q=M)).then_inc(list_in, 16)
            pool.wait_ge(list_in, 16)

            def gather(k):
                r = k - GS
                for t in range(2):
                    pool.wait_ge(zh_set, 2 * k + t - 1)
                    pool.wait_ge(zl_set, 2 * k + t - 1)
                    nc.gpsimd.tensor_copy(get_i[t][:, :], lists[:, bass.ds(2 * r + t, 1), 0]).then_inc(got, 1)
                    pool.wait_ge(got, 2 * r + (t + 1))
                    pool.sem_inc(passed, 1)
                    nc.gpsimd.indirect_dma_start(zin[t][0:M, :], None, z_d,
                                                 bass.IndirectOffsetOnAxis(get_i[t][:, 0:1], 0)).then_inc(z_got[t], 16)

            def scatter(k):
                r = k - GS
                for t in range(2):
                    pool.wait_ge(y_set, 4 * k + (2 * t + 2))
                    nc.gpsimd.tensor_copy(add_i[t][:, :], lists[:, bass.ds(2 * r + t, 1), 0]).then_inc(put, 1)
                    pool.wait_ge(put, 2 * r + (t + 1))
                    pool.sem_inc(passed, 1)
                    nc.gpsimd.indirect_dma_start(out, bass.IndirectOffsetOnAxis(add_i[t][:, 0:1], 0),
                                                 y[t][0:M, :], None, compute_op=ALU.add).then_inc(added, 16)
                    pool.wait_ge(added, 16 * (2 * r + (t + 1)))
                    pool.sem_inc(y_free, 1)

            for k in range(GS, GS + 4):
                gather(k)
                if k == GS + 2:
                    for t in range(2):
                        pool.wait_ge(stored[t], 16 * GS)
                if k == GS + 3:
                    scatter(GS)
            with pool.Fori(GS + 1, LAST - 3) as k:
                gather(k + 3)
                scatter(k)
            for k in range(LAST - 3, LAST):
                scatter(k)

        @block.scalar
        def _(act):
            act.wait_ge(const, 16)
            nc.scalar.activation(tg[:, :], g[:, :], ACT.Tanh).then_inc(gate, 1)

            def w1_high(n):
                act.wait_ge(w1_in, 16 * (n + 1))
                for c in range(C):
                    nc.scalar.activation(w1h[:, c, :], raw1[:, c, :], ACT.Copy).then_inc(w1h_set, 1)

            def w2_high(n, c, k):
                if c == 0:
                    act.wait_ge(w2_in, 16 * (n + 1))
                    wait(act, down, 4 * k)
                nc.scalar.activation(w2h[:, c, :], raw2[:, c, :], ACT.Copy).then_inc(w2h_set, 1)

            def split(k, u, t, kind):
                w = width(kind)
                wait(act, up, FC * (k - 1))
                if kind == "shared":
                    act.wait_ge(z_in[t], 16 * (k + 1))
                    nc.scalar.activation(zh[u][:, :, t * w:(t + 1) * w],
                                         zin[t][:, :].rearrange("p (c n) -> p c n", c=C), ACT.Copy).then_inc(zh_set, 1)
                else:
                    act.wait_ge(z_turned, 2 * (k - GS) + (t + 1))
                    nc.scalar.activation(zh[u][:, :, t * w:(t + 1) * w].rearrange("p (b c) n -> p b c n", b=2),
                                         psT[:, :, 0:C // 2 * w].rearrange("p b (c n) -> p b c n", n=w),
                                         ACT.Copy).then_inc(zh_set, 1)

            def swish(k, j, w):
                act.wait_ge(up, FC * k + (j + 1))
                wait(act, gated, FC * k + (j - 1))
                nc.scalar.activation(act_s[j % 2][:, 0:2 * w], ps1[j % 2][:, 1, 0:2 * w], ACT.Silu).then_inc(silu, 1)

            def high(k, u, j, w):
                act.wait_ge(gated, FC * k + (j + 1))
                wait(act, down, 4 * (k - 1))
                nc.scalar.activation(hh[u][:, j, 0:2 * w], hid[j % 2][:, 0:2 * w], ACT.Copy).then_inc(hh_set, 1)

            def group(k, u, n, i, kind, next_kind):
                w = width(kind)
                swish(k, 0, w)
                if next_kind:
                    split(k + 1, 1 - u, 0, next_kind)
                high(k, u, 0, w)
                first = isinstance(i, int) and i == 0
                if first:
                    w2_high(n, 0, k)
                swish(k, 1, w)
                high(k, u, 1, w)
                if first:
                    w2_high(n, 1, k)
                swish(k, 2, w)
                if next_kind:
                    split(k + 1, 1 - u, 1, next_kind)
                high(k, u, 2, w)
                if first:
                    w2_high(n, 2, k)
                swish(k, 3, w)
                high(k, u, 3, w)
                if first:
                    w2_high(n, 3, k)

            def after_shared():
                act.wait_ge(up, FC * GS)
                w1_high(1)

            def after(n, k, u, last):
                if not last:
                    act.wait_ge(up, FC * (k + 1))
                    w1_high(n + 1)

            w1_high(0)
            split(0, 0, 0, "shared")
            split(0, 0, 1, "shared")
            schedule(act, group, after_shared, after)

        @block.vector
        def _(dve):
            def w1_low(n, c):
                dve.wait_ge(w1h_set, C * n + (c + 1))
                nc.vector.tensor_tensor(w1l[:, c, :], raw1[:, c, :], w1h[:, c, :].bitcast(F32),
                                        ALU.subtract).then_inc(w1l_set, 1)

            def w2_low(n, c):
                dve.wait_ge(w2h_set, FC * n + (c + 1))
                nc.vector.tensor_tensor(w2l[:, c, :], raw2[:, c, :], w2h[:, c, :].bitcast(F32),
                                        ALU.subtract).then_inc(w2l_set, 1)

            def split(k, u, t, kind):
                w = width(kind)
                dve.wait_ge(zh_set, 2 * k + (t + 1))
                if kind == "shared":
                    nc.vector.tensor_tensor(zl[u][:, :, t * w:(t + 1) * w],
                                            zin[t][:, :].rearrange("p (c n) -> p c n", c=C),
                                            zh[u][:, :, t * w:(t + 1) * w].bitcast(F32),
                                            ALU.subtract).then_inc(zl_set, 1)
                else:
                    nc.vector.tensor_tensor(zl[u][:, :, t * w:(t + 1) * w].rearrange("p (b c) n -> p b c n", b=2),
                                            psT[:, :, 0:C // 2 * w].rearrange("p b (c n) -> p b c n", n=w),
                                            zh[u][:, :, t * w:(t + 1) * w].rearrange("p (b c) n -> p b c n", b=2).bitcast(F32),
                                            ALU.subtract).then_inc(zl_set, 1)

            def gate_up(k, j, w):
                dve.wait_ge(silu, FC * k + (j + 1))
                wait(dve, hl_set, FC * k + (j - 1))
                nc.vector.tensor_tensor(hid[j % 2][:, 0:2 * w], ps1[j % 2][:, 0, 0:2 * w],
                                        act_s[j % 2][:, 0:2 * w], ALU.mult).then_inc(gated, 1)

            def low(k, u, j, w):
                dve.wait_ge(hh_set, FC * k + (j + 1))
                nc.vector.tensor_tensor(hl[u][:, j, 0:2 * w], hid[j % 2][:, 0:2 * w],
                                        hh[u][:, j, 0:2 * w].bitcast(F32), ALU.subtract).then_inc(hl_set, 1)

            def result(k, t, half, kind):
                dve.wait_ge(down, 4 * k + (2 * t + half + 1))
                cols = slice(half * HALF, (half + 1) * HALF)
                if kind == "shared":
                    dve.wait_ge(res_in[t], 16 * k + 16)
                    nc.vector.scalar_tensor_tensor(out=y[t][:, cols], in0=ps2[t][:, half, 0:HALF], scalar=tg[:, 0:1],
                                                   in1=y[t][:, cols], op0=ALU.mult, op1=ALU.add).then_inc(y_set, 1)
                else:
                    r = k - GS
                    dve.wait_ge(y_free, 2 * r + (t + 1))
                    nc.vector.tensor_scalar(y[t][0:M, cols], ps2[t][0:M, half, 0:HALF],
                                            scale[:, bass.ds(2 * r + t, 1)], None, ALU.mult).then_inc(y_set, 1)

            def results(k, kind, n, chunks):
                per = -(-len(chunks) // 4)
                for q in range(4):
                    for c in chunks[q * per:(q + 1) * per]:
                        w1_low(n, c)
                    result(k, q // 2, q % 2, kind)

            def group(k, u, n, i, kind, next_kind):
                w = width(kind)
                first = isinstance(i, int) and i == 0
                for j in range(FC):
                    gate_up(k, j, w)
                    if next_kind and j % 2 == 0:
                        split(k + 1, 1 - u, j // 2, next_kind)
                    low(k, u, j, w)
                    if first:
                        w2_low(n, j)
                if not first:
                    turnover = next_kind == "routed" and (kind == "shared" or i == GE - 1)
                    results(k - 1, kind, n + 1, list(range(C // 2)) if turnover else [])

            def after_shared():
                results(GS - 1, "shared", 1, list(range(C // 2, C)))
                dve.wait_ge(list_in, 16)
                nc.vector.tensor_scalar(scale[:, :], lists[:, :, 1].bitcast(F32), tg[0:M, 0:1], None,
                                        ALU.mult).then_inc(scaled, 1)
                dve.wait_ge(scaled, 1)

            def after(n, k, u, last):
                results(k, "routed", n + 1, [] if last else list(range(C // 2, C)))

            dve.wait_ge(gate, 1)
            for c in range(C):
                w1_low(0, c)
            split(0, 0, 0, "shared")
            split(0, 0, 1, "shared")
            schedule(dve, group, after_shared, after)

        @block.tensor
        def _(pe):
            def turn(k, t):
                pe.wait_ge(z_got[t], 16 * (k - GS) + 16)
                pe.wait_ge(zh_set, 2 * k + t)
                pe.wait_ge(zl_set, 2 * k + t)
                for c in range(C):
                    cc = c % (C // 2)
                    last = nc.tensor.transpose(psT[:, c // (C // 2), cc * M:(cc + 1) * M],
                                               zin[t][0:M, c * P:(c + 1) * P], ident[0:M, 0:M])
                last.then_inc(z_turned, 1)

            def first_product(k, u, j, w):
                wait(pe, gated, FC * k + (j - 1))
                for b in range(2):
                    acc = ps1[j % 2][:, b, 0:2 * w]
                    cols = slice(b * F + j * P, b * F + (j + 1) * P)
                    for c in range(C):
                        nc.tensor.matmul(acc, w1h[:, c, cols], zh[u][:, c, 0:2 * w], start=(c == 0), stop=False)
                        nc.tensor.matmul(acc, w1h[:, c, cols], zl[u][:, c, 0:2 * w], start=False, stop=False)
                        last = nc.tensor.matmul(acc, w1l[:, c, cols], zh[u][:, c, 0:2 * w],
                                                start=False, stop=(c == C - 1))
                last.then_inc(up, 1)

            def second_product(k, u, w):
                pe.wait_ge(hh_set, FC * k + FC)
                pe.wait_ge(hl_set, FC * k + FC)
                for t in range(2):
                    rows = slice(t * w, (t + 1) * w)
                    for half in range(2):
                        wait(pe, y_set, 4 * k - 4 + (2 * t + half + 1))
                        acc = ps2[t][0:w, half, 0:HALF]
                        cols = slice(half * HALF, (half + 1) * HALF)
                        for f in range(FC):
                            nc.tensor.matmul(acc, hh[u][:, f, rows], w2h[:, f, cols], start=(f == 0), stop=False)
                            nc.tensor.matmul(acc, hh[u][:, f, rows], w2l[:, f, cols], start=False, stop=False)
                            last = nc.tensor.matmul(acc, hl[u][:, f, rows], w2h[:, f, cols],
                                                    start=False, stop=(f == FC - 1))
                        last.then_inc(down, 1)

            def group(k, u, n, i, kind, next_kind):
                w = width(kind)
                if isinstance(i, int) and i == 0:
                    pe.wait_ge(w1h_set, C * n + C)
                    pe.wait_ge(w1l_set, C * n + C)
                pe.wait_ge(zh_set, 2 * k + 2)
                pe.wait_ge(zl_set, 2 * k + 2)
                for j in range(FC):
                    first_product(k, u, j, w)
                    if next_kind == "routed" and j % 2 == 0:
                        turn(k + 1, j // 2)
                if not (isinstance(i, int) and i == 0):
                    if i == 1:
                        pe.wait_ge(w2h_set, FC * n + FC)
                        pe.wait_ge(w2l_set, FC * n + FC)
                    second_product(k - 1, 1 - u, w)

            def after_shared():
                second_product(GS - 1, 1, P)

            def after(n, k, u, last):
                second_product(k, u, M)

            pe.wait_ge(made, 2)
            schedule(pe, group, after_shared, after)


def build(nc, x, xT, cT, g_xattn, g_ffn, ssm_kernel, D, gate_w, expert_bias, shared_w1, shared_w2,
          routed_w1, routed_w2, out):
    B, S, L = x.shape
    H, T, E = S // HD, B * S, gate_w.shape[1]
    capacity = max(1, T // E)
    slots = -(-capacity // 10) * 10

    def scratch(name, shape, dt=F32):
        return nc.dram_tensor(name, shape, dt).ap()

    filt_hi, filt_lo = scratch("filt_hi", (H, PAD)), scratch("filt_lo", (H, PAD))
    z_d = scratch("z_d", (T + P, L))
    zT_d = scratch("zT_d", (H, P, L // P, P))
    logit_d = scratch("logit_d", (P, H, E))
    list_d = scratch("list_d", (E * slots + P, 2), I32)
    prepare_filters(nc, ssm_kernel, D, filt_hi, filt_lo, z_d, out)
    gated_conv(nc, x, xT, cT, g_xattn, gate_w, expert_bias, filt_hi, filt_lo, z_d, zT_d, logit_d, out)
    with (nc.sbuf_tensor("slot_of", [P, H, 2], I32) as slot_of,
          nc.sbuf_tensor("pay", [P, H, 2, 2], I32) as pay):
        route(nc, logit_d, slot_of, pay, capacity, slots, H)
        experts(nc, zT_d, z_d, slot_of, pay, list_d, g_ffn, shared_w1, shared_w2, routed_w1, routed_w2,
                out, slots, H)


_INS = ["x", "xT", "cT", "g_xattn", "g_ffn", "L0_xattn_ssm_kernel", "L0_xattn_D", "L0_ffn_gate_w",
        "L0_ffn_expert_bias", "L0_ffn_shared_w1", "L0_ffn_shared_w2", "L0_ffn_routed_w1", "L0_ffn_routed_w2"]


def head_tiles(a):
    B, S, L = a.shape
    return a.reshape(B, S // HD, HD, L // P, P).transpose(1, 4, 3, 0, 2).reshape(S // HD, P, L // P, B * HD)


def kernel(**inputs):
    import concourse.bacc as bacc
    from concourse.bass_utils import run_bass_kernel_spmd

    nc = bacc.Bacc("TRN2", target_bir_lowering=False, num_devices=1)
    laid = {name: np.asarray(a) for name, a in inputs.items()}
    laid["xT"] = head_tiles(laid["x"])
    laid["cT"] = head_tiles(laid["ctx_2048"][:, :, ::-1])
    arrays, args = {}, []
    for name in _INS:
        a = np.ascontiguousarray(laid[name])
        arrays[f"in_{name}"] = a
        args.append(nc.dram_tensor(f"in_{name}", a.shape, mybir.dt.from_np(a.dtype), kind="ExternalInput").ap())
    B, S, L = laid["x"].shape
    out = nc.dram_tensor("out_0", (B * S + P, L), F32, kind="ExternalOutput").ap()
    build(nc, *args, out)
    r = run_bass_kernel_spmd(nc, [arrays], core_ids=[0])
    return np.ascontiguousarray(r.results[0]["out_0"][:B * S].reshape(B, S, L))
```

```python
import math
import numpy as np
import concourse.bass as bass
from concourse import mybir
from contextlib import ExitStack

F32 = mybir.dt.float32
F32R = mybir.dt.float32r
I32 = mybir.dt.int32
ALU = mybir.AluOpType
ACT = mybir.ActivationFunctionType
AX = mybir.AxisListType

P = 128
BANK = 512
HD = 8
PAIRS = HD * (HD + 1) // 2
EPS = 1e-5
PAD = 1152


class Pool:

    def __init__(self, nc, ctx, tag):
        self.nc, self.ctx, self.tag = nc, ctx, tag

    def sb(self, name, shape, dt=F32):
        return self.ctx.enter_context(self.nc.sbuf_tensor(f"{self.tag}_{name}", shape, dt))

    def ps(self, name, shape, dt=F32):
        return self.ctx.enter_context(self.nc.psum_tensor(f"{self.tag}_{name}", shape, dt))

    def sem(self, name):
        return self.ctx.enter_context(self.nc.semaphore(f"{self.tag}_{name}"))


def identity_steps(nc, pool, ident, made):
    nc.gpsimd.memset(ident[:, :], 0.0).then_inc(made, 1)
    pool.wait_ge(made, 1)
    nc.gpsimd.affine_select(out=ident[:, :], in_=ident[:, :], compare_op=ALU.not_equal, fill=1.0,
                            base=0, pattern=[[-1, P]], channel_multiplier=1).then_inc(made, 1)


def prepare_filters(nc, ssm_kernel, D, filt_hi, filt_lo, z_d, out):
    H, L = ssm_kernel.shape
    T = z_d.shape[0] - P
    with ExitStack() as ctx:
        m = Pool(nc, ctx, "fil")
        full = m.sb("full", [H, PAD])
        hi = m.sb("hi", [H, PAD], F32R)
        lo = m.sb("lo", [H, PAD], F32R)
        d = m.sb("d", [H, 1])
        zero = m.sb("zero", [P, L])
        cleared, loaded, tapped, rounded, split, zeroed, stored = (
            m.sem(n) for n in ("cleared", "loaded", "tapped", "rounded", "split", "zeroed", "stored"))
        block = ctx.enter_context(nc.Block())

        @block.sync
        def _(sp):
            sp.wait_ge(cleared, 1)
            sp.dma_start(full[:, P - 1:P - 1 + L], ssm_kernel).then_inc(loaded, 16)
            sp.dma_start(d[:, :], D.rearrange("(h a) -> h a", a=1)).then_inc(loaded, 16)
            sp.wait_ge(zeroed, 1)
            sp.dma_start(z_d[T:T + P, :], zero[:, :]).then_inc(stored, 16)
            sp.dma_start(out[T:T + P, :], zero[:, :]).then_inc(stored, 16)
            sp.wait_ge(split, 1)
            sp.dma_start(filt_hi, hi[:, :].bitcast(F32)).then_inc(stored, 16)
            sp.dma_start(filt_lo, lo[:, :].bitcast(F32)).then_inc(stored, 16)
            sp.wait_ge(stored, 64)

        @block.vector
        def _(dve):
            nc.vector.memset(full[:, :], 0.0).then_inc(cleared, 1)
            nc.vector.memset(zero[:, :], 0.0).then_inc(zeroed, 1)
            dve.wait_ge(loaded, 32)
            nc.vector.tensor_tensor(full[:, P - 1:P], full[:, P - 1:P], d[:, :], ALU.add).then_inc(tapped, 1)
            dve.wait_ge(tapped, 1)
            nc.vector.tensor_copy(hi[:, :], full[:, :]).then_inc(rounded, 1)
            dve.wait_ge(rounded, 1)
            nc.vector.tensor_tensor(lo[:, :], full[:, :], hi[:, :].bitcast(F32), ALU.subtract).then_inc(split, 1)


def gated_conv(nc, x, xT, cT, g_xattn, gate_w, expert_bias, filt_hi, filt_lo, z_d, zT_d, logit_d, out):
    B, S, L = x.shape
    H = S // HD
    NT = L // P
    G = NT // 2
    E = gate_w.shape[1]
    NB = B // 2
    W = P + E
    TB = BANK // W
    FB, RT = NT // TB, NT % TB
    assert RT > 1 and FB <= 2 and B * HD == P and H % 2 == 0 and H >= 6
    off = [HD + sum(HD - 1 - r for r in range(i)) for i in range(HD)]

    x_rows = x.rearrange("b (h j) l -> h b j l", j=HD)
    z_rows = z_d[0:B * S, :].rearrange("(b h j) l -> h b j l", b=B, j=HD)
    o_rows = out[0:B * S, :].rearrange("(b h j) l -> h b j l", b=B, j=HD)

    def toeplitz(filt):
        return bass.AP(filt.tensor, 0, [[PAD, H], [1, P], [1, L]])

    t_hi, t_lo = toeplitz(filt_hi), toeplitz(filt_lo)

    with ExitStack() as ctx:
        m = Pool(nc, ctx, "att")
        xn = m.sb("xn", [P, L])
        kT = m.sb("kT", [P, NT, B, HD])
        qT = [m.sb(f"qT{u}", [P, NT, B, HD]) for u in range(2)]
        kv = m.sb("kv", [P, G, B, PAIRS])
        kv_hi = [m.sb(f"kv_hi{u}", [P, NT, B, PAIRS], F32R) for u in range(2)]
        kv_lo = [m.sb(f"kv_lo{u}", [P, NT, B, PAIRS], F32R) for u in range(2)]
        tz_hi = [m.sb(f"tz_hi{u}", [P, L], F32R) for u in range(2)]
        tz_lo = [m.sb(f"tz_lo{u}", [P, L], F32R) for u in range(2)]
        y = [m.sb(f"y{u}", [P, NT, B, PAIRS]) for u in range(2)]
        prod = m.sb("prod", [P, G * B, HD, HD])
        oT = m.sb("oT", [P, NT, B * HD])
        x1 = m.sb("x1", [P, L])
        z = m.sb("z", [P, L])
        zT = [m.sb(f"zT{u}", [P, NT, P]) for u in range(2)]
        ident = m.sb("ident", [P, P])
        ones = m.sb("ones", [P, P])
        turn = m.sb("turn", [P, NT, W])
        sums = m.sb("sums", [P, E])
        part = m.sb("part", [P, E, FB + 1])
        whole = m.sb("whole", [P, E])
        shift = m.sb("shift", [P, E])
        bias = m.sb("bias", [P, E])
        g = m.sb("g", [P, 1])
        tg = m.sb("tg", [P, 1])
        eps = m.sb("eps", [P, 1])
        minus_half = m.sb("minus_half", [P, 1])
        logit = m.sb("logit", [P, H, E])
        stats = [m.sb(f"stats{k}", [P, 2, 6]) for k in range(2)]
        mv = [m.sb(f"mv{k}", [P, 2]) for k in range(2)]
        root = [m.sb(f"root{k}", [P, 2]) for k in range(2)]
        diag = [m.sb(f"diag{k}", [P, 2, P]) for k in range(2)]
        spread = [m.sb(f"spread{k}", [P, 2, P]) for k in range(2)]
        minus = m.sb("minus", [P, 1])

        psY = [m.ps(f"psY{u}", [P, 2, BANK]) for u in range(2)]
        psO = m.ps("psO", [P, FB + 1, BANK])
        psB = m.ps("psB", [P, 2, 2 * P])

        const = m.sem("const")
        made = m.sem("made")
        oned = m.sem("oned")
        gate = m.sem("gate")
        passed = m.sem("passed")
        xn_in, kT_in = m.sem("xn_in"), m.sem("kT_in")
        xT_in = [m.sem(f"xT_in{u}") for u in range(2)]
        rT_in = [m.sem(f"rT_in{u}") for u in range(2)]
        tz_in = [m.sem(f"tz_in{u}") for u in range(2)]
        z_out, x1_out, l_out = m.sem("z_out"), m.sem("x1_out"), m.sem("l_out")
        zT_out = [m.sem(f"zT_out{u}") for u in range(2)]
        o_turned = m.sem("o_turned")
        y_done = m.sem("y_done")
        l_step = m.sem("l_step")
        added_up = m.sem("added_up")
        turn_set = m.sem("turn_set")
        spread_done = [m.sem(f"spread_done{k}") for k in range(2)]
        spread_set = [m.sem(f"spread_set{k}") for k in range(2)]
        y_set = m.sem("y_set")
        hi_set = m.sem("hi_set")
        z_set = m.sem("z_set")
        minus_set = m.sem("minus_set")
        kv_set = m.sem("kv_set")
        sq_set = m.sem("sq_set")
        rooted = [m.sem(f"rooted{k}") for k in range(2)]
        diag_set = [m.sem(f"diag_set{k}") for k in range(2)]
        q_set = m.sem("q_set")
        zT_set = m.sem("zT_set")
        lo_set = m.sem("lo_set")
        told = [m.sem(f"told{k}") for k in range(2)]
        multiplied = m.sem("multiplied")
        first_set = m.sem("first_set")
        summed = m.sem("summed")
        x1_set = m.sem("x1_set")
        x1T_set = m.sem("x1T_set")
        l_set = m.sem("l_set")
        ROOT = 3

        block = ctx.enter_context(nc.Block())

        def keys_of(half):
            return slice((1 - half) * G, (2 - half) * G)

        def wait(eng, sem, value):
            if not (isinstance(value, int) and value <= 0):
                eng.wait_ge(sem, value)

        def steady(eng, step):
            for h in range(4):
                step(h, h % 2, True, h >= 1, h >= 2, h >= 3)
            with eng.Fori(2, H // 2 - 1) as pair:
                h = 2 * pair
                step(h, 0, True, True, True, True)
                step(h + 1, 1, True, True, True, True)
            step(H - 2, 0, True, True, True, True)
            step(H - 1, 1, False, True, True, True)

        def uses(n, u):
            return 8 * (n - u) + 16

        @block.sync
        def _(sp):
            sp.dma_start(turn[:, :, P:W], gate_w.rearrange("(c p) e -> p c e", p=P)).then_inc(const, 16)
            sp.dma_start(bias[:, :], expert_bias.rearrange("(a e) -> a e", a=1).to_broadcast([P, E])).then_inc(const, 16)
            sp.dma_start(g[:, :], g_xattn.rearrange("(a e) -> a e", a=1).to_broadcast([P, 1])).then_inc(const, 16)

            def load_stats(h):
                wait(sp, told[0], 3 * h - 1)
                sp.dma_start(xn[:, :], x_rows[h]).then_inc(xn_in, 16)

            def load_keys(h):
                wait(sp, hi_set, 2 * h)
                sp.dma_start(kT[:, :, :, :].rearrange("p t b i -> p t (b i)"), cT[h]).then_inc(kT_in, 16)

            def load_queries(h, u):
                wait(sp, summed, 2 * (h - 1))
                sp.dma_start(qT[u][:, :, :, :].rearrange("p t b i -> p t (b i)"), xT[h]).then_inc(xT_in[u], 16)

            def load_filter(h, u):
                wait(sp, y_done, NT * (h - 1))
                sp.dma_start(tz_hi[u][:, :].bitcast(F32), t_hi[h]).then_inc(tz_in[u], 16)
                sp.dma_start(tz_lo[u][:, :].bitcast(F32), t_lo[h]).then_inc(tz_in[u], 16)

            def load_residual_T(h, u):
                if not (isinstance(h, int) and h < 2):
                    sp.wait_ge(zT_out[u], uses(h - 2, u))
                sp.dma_start(zT[u][:, :, :], xT[h]).then_inc(rT_in[u], 16)

            def store_x1(h):
                sp.wait_ge(x1_set, 2 * h + 2)
                sp.dma_start(o_rows[h], x1[:, :]).then_inc(x1_out, 16)

            def store_z(h):
                sp.wait_ge(z_set, h + 1)
                sp.dma_start(z_rows[h], z[:, :]).then_inc(z_out, 16)

            def store_zT(h, u):
                sp.wait_ge(zT_set, 2 * h + 2)
                sp.dma_start(zT_d[h], zT[u][:, :, :]).then_inc(zT_out[u], 16)

            load_keys(0)
            load_filter(0, 0)
            load_stats(0)
            load_keys(1)

            def step(h, u, ahead, back, back2, back3):
                if ahead:
                    load_filter(h + 1, 1 - u)
                load_queries(h, u)
                if ahead:
                    load_stats(h + 1)
                if back3:
                    store_zT(h - 3, 1 - u)
                if back:
                    load_residual_T(h - 1, 1 - u)
                if not (isinstance(h, int) and h >= H - 2):
                    load_keys(h + 2)
                if back2:
                    store_x1(h - 2)
                if back2:
                    store_z(h - 2)

            steady(sp, step)
            store_zT(H - 3, 1)
            load_residual_T(H - 1, 1)
            store_x1(H - 2)
            store_z(H - 2)
            store_zT(H - 2, 0)
            store_x1(H - 1)
            store_z(H - 1)
            store_zT(H - 1, 1)
            sp.wait_ge(l_set, H)
            sp.dma_start(logit_d, logit[:, :, :]).then_inc(l_out, 16)
            for u in range(2):
                sp.wait_ge(zT_out[u], 8 * H)
            sp.wait_ge(x1_out, 16 * H)
            sp.wait_ge(z_out, 16 * H)
            sp.wait_ge(l_out, 16)

        @block.gpsimd
        def _(pool):
            identity_steps(nc, pool, ident, made)
            nc.gpsimd.memset(eps[:, :], EPS).then_inc(made, 1)
            nc.gpsimd.memset(minus_half[:, :], -0.5).then_inc(made, 1)
            nc.gpsimd.memset(ones[:, :], 1.0).then_inc(oned, 1)
            pool.wait_ge(made, 4)

            def roots(k, h):
                def link(ins, n):
                    ins.then_inc(rooted[k], 1)
                    pool.wait_ge(rooted[k], ROOT * h + n)

                pool.wait_ge(told[k], 3 * h + 3)
                wait(pool, diag_set[k], 2 * h)
                if k == 1:
                    wait(pool, z_set, h)
                    wait(pool, l_set, h)
                link(nc.gpsimd.tensor_tensor(root[k][:, 0:1], mv[k][:, 1:2], eps[:, :], ALU.add), 1)
                link(nc.gpsimd.tensor_tensor(root[k][:, 0:1], root[k][:, 0:1], minus_half[:, :], ALU.pow), 2)
                link(nc.gpsimd.tensor_tensor(root[k][:, 1:2], mv[k][:, 0:1], root[k][:, 0:1], ALU.mult), 3)

            def pairs(h, half):
                pool.wait_ge(kT_in, 16 * h + 16)
                wait(pool, lo_set, 2 * h + half)
                wait(pool, hi_set, 2 * h + half)
                ks = kT[:, keys_of(half)].rearrange("p t b i -> p (t b) i")
                dst = kv[:, :, :, :].rearrange("p t b i -> p (t b) i")
                for i in range(HD - 1):
                    n = HD - 1 - i
                    last = nc.gpsimd.tensor_tensor(dst[:, :, off[i]:off[i] + n], ks[:, :, i + 1:HD],
                                                   ks[:, :, i:i + 1].to_broadcast([P, G * B, n]), ALU.mult)
                last.then_inc(kv_set, 1)

            def normalise(t, k, done, h):
                pool.wait_ge(spread_set[k], h + 1)
                for n, op in enumerate((ALU.mult, ALU.subtract)):
                    nc.gpsimd.tensor_tensor(t, t, spread[k][:, n:n + 1, :].to_broadcast([P, NT, P]), op).then_inc(done, 1)
                    pool.wait_ge(done, 2 * h + (n + 1))

            def queries(h, u):
                pool.wait_ge(xT_in[u], uses(h, u))
                normalise(qT[u][:, :, :, :].rearrange("p t b i -> p t (b i)"), 0, q_set, h)

            def first_terms(h, u, half):
                pool.wait_ge(y_set, NT * h + G * (half + 1))
                wait(pool, summed, 2 * h + half)
                ys = y[u][:, half * G:(half + 1) * G].rearrange("p t b i -> p (t b) i")
                qs = qT[u][:, half * G:(half + 1) * G].rearrange("p t b i -> p (t b) i")
                n = HD - 1
                nc.gpsimd.tensor_tensor(prod[:, :, 1:HD, 0], ys[:, :, off[0]:off[0] + n],
                                        qs[:, :, 0:1].to_broadcast([P, G * B, n]), ALU.mult)
                nc.gpsimd.tensor_tensor(prod[:, :, 0, 1:HD], ys[:, :, off[0]:off[0] + n], qs[:, :, 1:HD],
                                        ALU.mult).then_inc(first_set, 1)

            def z_turned(h, u):
                pool.wait_ge(o_turned, h + 1)
                normalise(zT[u][:, :, :], 1, zT_set, h)

            pairs(0, 0)
            pairs(0, 1)
            pairs(1, 0)

            def step(h, u, ahead, back, back2, back3):
                roots(0, h)
                if back:
                    first_terms(h - 1, 1 - u, 1)
                if ahead:
                    pairs(h + 1, 1)
                if back2:
                    roots(1, h - 2)
                queries(h, u)
                if back2:
                    z_turned(h - 2, u)
                if not (isinstance(h, int) and h >= H - 2):
                    pairs(h + 2, 0)
                first_terms(h, u, 0)

            steady(pool, step)
            first_terms(H - 1, 1, 1)
            for h in (H - 2, H - 1):
                roots(1, h)
                z_turned(h, h % 2)

        @block.scalar
        def _(act):
            act.wait_ge(const, 48)
            act.wait_ge(made, 2)
            nc.scalar.activation(tg[:, :], g[:, :], ACT.Tanh).then_inc(gate, 1)

            def spread_out(k, h):
                act.wait_ge(spread_done[k], h + 1)
                if k == 0:
                    wait(act, q_set, 2 * h)
                else:
                    wait(act, zT_set, 2 * h)
                nc.scalar.activation(spread[k][:, :, :], psB[:, k, :].rearrange("p (n r) -> p n r", n=2),
                                     ACT.Copy).then_inc(spread_set[k], 1)

            def diagonals(k, h):
                act.wait_ge(rooted[k], ROOT * h + ROOT)
                wait(act, spread_done[k], h)
                for n in range(2):
                    nc.scalar.activation(diag[k][:, n, :], ident[:, :], ACT.Identity,
                                         scale=root[k][:, n:n + 1]).then_inc(diag_set[k], 1)

            def normal(h):
                act.wait_ge(rooted[1], ROOT * h + 3)
                nc.scalar.activation(minus[:, :], root[1][:, 1:2], ACT.Copy, scale=-1.0).then_inc(minus_set, 1)
                act.wait_ge(minus_set, h + 1)
                wait(act, z_out, 16 * h)
                nc.scalar.activation(z[:, :], x1[:, :], ACT.Identity, bias=minus[:, 0:1],
                                     scale=root[1][:, 0:1]).then_inc(z_set, 1)

            def rows(h):
                act.wait_ge(o_turned, h + 1)
                wait(act, x1_out, 16 * h)
                wait(act, z_set, h)
                full = FB * TB * P
                nc.scalar.activation(x1[:, 0:full].rearrange("p (f t r) -> p f t r", f=FB, t=TB),
                                     psO[:, 0:FB, 0:TB * W].rearrange("p f (t w) -> p f t w", w=W)[:, :, :, 0:P],
                                     ACT.Copy).then_inc(x1_set, 1)
                nc.scalar.activation(x1[:, full:L].rearrange("p (t r) -> p t r", r=P),
                                     psO[:, FB, 0:RT * W].rearrange("p (t w) -> p t w", w=W)[:, :, 0:P],
                                     ACT.Copy).then_inc(x1_set, 1)

            def squares(h, half):
                act.wait_ge(kT_in, 16 * h + 16)
                wait(act, lo_set, 2 * h + half)
                wait(act, hi_set, 2 * h + half)
                nc.scalar.activation(kv[:, :, :, 0:HD], kT[:, keys_of(half)], ACT.Square).then_inc(sq_set, 1)

            def high(h, u, half):
                act.wait_ge(kv_set, 2 * h + half + 1)
                act.wait_ge(sq_set, 2 * h + half + 1)
                wait(act, y_done, NT * (h - 1))
                nc.scalar.activation(kv_hi[u][:, keys_of(half)].rearrange("p t b i -> p (t b i)"),
                                     kv[:, :, :, :].rearrange("p t b i -> p (t b i)"), ACT.Copy).then_inc(hi_set, 1)

            def conv_out(h, u, a):
                act.wait_ge(y_done, NT * h + a + 1)
                if a == 0:
                    wait(act, multiplied, 2 * (h - 1))
                    wait(act, first_set, 2 * (h - 1))
                nc.scalar.activation(y[u][:, a].rearrange("p (c b) i -> p c (b i)", c=2),
                                     psY[a % 2][:, :, 0:NB * PAIRS], ACT.Copy).then_inc(y_set, 1)

            squares(0, 0)
            high(0, 0, 0)
            squares(0, 1)
            high(0, 0, 1)

            def step(h, u, ahead, back, back2, back3):
                if ahead:
                    squares(h + 1, 0)
                conv_out(h, u, 0)
                conv_out(h, u, 1)
                if ahead:
                    high(h + 1, 1 - u, 0)
                conv_out(h, u, 2)
                if back2:
                    rows(h - 2)
                diagonals(0, h)
                conv_out(h, u, 3)
                spread_out(0, h)
                if ahead:
                    squares(h + 1, 1)
                conv_out(h, u, 4)
                if back2:
                    diagonals(1, h - 2)
                    normal(h - 2)
                if ahead:
                    high(h + 1, 1 - u, 1)
                conv_out(h, u, 5)
                if back2:
                    spread_out(1, h - 2)
                for a in range(6, NT):
                    conv_out(h, u, a)

            steady(act, step)
            rows(H - 2)
            diagonals(1, H - 2)
            normal(H - 2)
            spread_out(1, H - 2)
            rows(H - 1)
            diagonals(1, H - 1)
            normal(H - 1)
            spread_out(1, H - 1)

        @block.vector
        def _(dve):
            def tell(k, h, src):
                wait(dve, rooted[k], ROOT * h)
                for c in range(2):
                    nc.vector.bn_stats(stats[k][:, c, :], src[:, c * (L // 2):(c + 1) * (L // 2)]).then_inc(told[k], 1)
                dve.wait_ge(told[k], 3 * h + 2)
                dve.sem_inc(passed, 1)
                nc.vector.bn_aggr(mv[k][:, :], stats[k][:, :, :].rearrange("p a b -> p (a b)")).then_inc(told[k], 1)

            def tell_x(h):
                dve.wait_ge(xn_in, 16 * h + 16)
                tell(0, h, xn)

            def low(h, u, half):
                dve.wait_ge(hi_set, 2 * h + half + 1)
                nc.vector.tensor_tensor(kv_lo[u][:, keys_of(half)].rearrange("p t b i -> p (t b i)"),
                                        kv[:, :, :, :].rearrange("p t b i -> p (t b i)"),
                                        kv_hi[u][:, keys_of(half)].rearrange("p t b i -> p (t b i)").bitcast(F32),
                                        ALU.subtract).then_inc(lo_set, 1)

            def combine(h, u, half):
                dve.wait_ge(y_set, NT * h + G * (half + 1))
                dve.wait_ge(q_set, 2 * h + 2)
                wait(dve, summed, 2 * h + half)
                ys = y[u][:, half * G:(half + 1) * G].rearrange("p t b i -> p (t b) i")
                qs = qT[u][:, half * G:(half + 1) * G].rearrange("p t b i -> p (t b) i")
                flat = prod[:, :, :, :].rearrange("p m j i -> p m (j i)")
                nc.vector.tensor_tensor(flat[:, :, 0:HD * HD:HD + 1], ys[:, :, 0:HD], qs, ALU.mult)
                for i in range(1, HD - 1):
                    n = HD - 1 - i
                    nc.vector.tensor_tensor(prod[:, :, i + 1:HD, i], ys[:, :, off[i]:off[i] + n],
                                            qs[:, :, i:i + 1].to_broadcast([P, G * B, n]), ALU.mult)
                    last = nc.vector.tensor_tensor(prod[:, :, i, i + 1:HD], ys[:, :, off[i]:off[i] + n],
                                                   qs[:, :, i + 1:HD], ALU.mult)
                last.then_inc(multiplied, 1)
                dve.wait_ge(multiplied, 2 * h + half + 1)
                dve.wait_ge(first_set, 2 * h + half + 1)
                wait(dve, x1T_set, h)
                nc.vector.tensor_reduce(oT[:, half * G:(half + 1) * G, :].rearrange("p t (b j) -> p (t b) j", j=HD),
                                        prod[:, :, :, :], AX.X, ALU.add).then_inc(summed, 1)

            def residual(h, u):
                dve.wait_ge(summed, 2 * h + 2)
                dve.wait_ge(rT_in[u], uses(h, u))
                nc.vector.scalar_tensor_tensor(out=zT[u][:, :, :].rearrange("p t n -> p (t n)"),
                                               in0=oT[:, :, :].rearrange("p t n -> p (t n)"), scalar=tg[:, 0:1],
                                               in1=zT[u][:, :, :].rearrange("p t n -> p (t n)"),
                                               op0=ALU.mult, op1=ALU.add).then_inc(x1T_set, 1)

            def tell_x1(h):
                dve.wait_ge(x1_set, 2 * h + 2)
                tell(1, h, x1)

            def logits(h):
                def of_bank(f, tiles):
                    return psO[:, f, 0:tiles * W].rearrange("p (t w) -> p w t", w=W)[:, P:W, :]

                dve.wait_ge(rooted[1], ROOT * h + ROOT)
                nc.vector.scalar_tensor_tensor(out=shift[:, :], in0=sums[:, :], scalar=root[1][:, 1:2], in1=bias[:, :],
                                               op0=ALU.mult, op1=ALU.add)
                for f in range(FB + 1):
                    nc.vector.tensor_reduce(part[:, :, f:f + 1], of_bank(f, TB if f < FB else RT), AX.X,
                                            ALU.add).then_inc(l_step, 1)
                dve.wait_ge(l_step, (FB + 2) * h + (FB + 1))
                nc.vector.tensor_reduce(whole[:, :], part[:, :, :], AX.X, ALU.add).then_inc(l_step, 1)
                dve.wait_ge(l_step, (FB + 2) * h + (FB + 2))
                nc.vector.scalar_tensor_tensor(out=logit[:, h, :], in0=whole[:, :], scalar=root[1][:, 0:1],
                                               in1=shift[:, :], op0=ALU.mult, op1=ALU.add).then_inc(l_set, 1)

            dve.wait_ge(made, 2)
            nc.vector.tensor_copy(turn[:, :, 0:P], ident[:, :].unsqueeze(1).to_broadcast([P, NT, P])).then_inc(turn_set, 1)
            tell_x(0)
            low(0, 0, 0)
            low(0, 0, 1)
            dve.wait_ge(gate, 1)
            dve.wait_ge(const, 48)
            dve.wait_ge(added_up, 1)
            nc.vector.tensor_scalar(sums[:, :], psB[:, 0, 0:E], -1.0, None, ALU.mult).then_inc(turn_set, 1)
            dve.wait_ge(turn_set, 2)

            def step(h, u, ahead, back, back2, back3):
                if back:
                    combine(h - 1, 1 - u, 0)
                if ahead:
                    low(h + 1, 1 - u, 0)
                if back2:
                    tell_x1(h - 2)
                if back:
                    combine(h - 1, 1 - u, 1)
                if ahead:
                    low(h + 1, 1 - u, 1)
                if back2:
                    logits(h - 2)
                if ahead:
                    tell_x(h + 1)
                if back:
                    residual(h - 1, 1 - u)

            steady(dve, step)
            combine(H - 1, 1, 0)
            tell_x1(H - 2)
            combine(H - 1, 1, 1)
            residual(H - 1, 1)
            logits(H - 2)
            tell_x1(H - 1)
            logits(H - 1)

        @block.tensor
        def _(pe):
            def conv(h, u, tiles):
                for a in tiles:
                    if a == 0:
                        pe.wait_ge(hi_set, 2 * h + 1)
                        pe.wait_ge(lo_set, 2 * h + 1)
                        pe.wait_ge(tz_in[u], 2 * uses(h, u))
                    if a == G:
                        pe.wait_ge(hi_set, 2 * h + 2)
                        pe.wait_ge(lo_set, 2 * h + 2)
                    wait(pe, y_set, NT * h + a - 1)
                    for c in range(a + 1):
                        for half in range(2):
                            acc = psY[a % 2][:, half, 0:NB * PAIRS]
                            d = (a - c) * P
                            hi = kv_hi[u][:, NT - 1 - c, half * NB:(half + 1) * NB, :].rearrange("p b i -> p (b i)")
                            lo = kv_lo[u][:, NT - 1 - c, half * NB:(half + 1) * NB, :].rearrange("p b i -> p (b i)")
                            nc.tensor.matmul(acc, tz_hi[u][:, d:d + P], hi, start=(c == 0), stop=False)
                            nc.tensor.matmul(acc, tz_hi[u][:, d:d + P], lo, start=False, stop=False)
                            last = nc.tensor.matmul(acc, tz_lo[u][:, d:d + P], hi, start=False, stop=(c == a))
                    last.then_inc(y_done, 1)

            def spread_in(k, h, other=0):
                pe.wait_ge(diag_set[k], 2 * h + 2)
                if isinstance(h, int) and h == 0:
                    pe.wait_ge(turn_set, 2)
                wait(pe, spread_set[k], h)
                wait(pe, spread_set[1 - k], h - 2 if k == 0 else other or h + 3)
                nc.tensor.matmul(psB[:, k, :], ones[:, :], diag[k][:, :, :].rearrange("p n r -> p (n r)"),
                                 start=True, stop=True).then_inc(spread_done[k], 1)

            def turn_x1(h, u):
                pe.wait_ge(x1T_set, h + 1)
                wait(pe, x1_set, 2 * h)
                wait(pe, l_set, h)
                for t in range(NT):
                    last = nc.tensor.matmul(psO[:, t // TB, t % TB * W:(t % TB + 1) * W], zT[u][:, t, :],
                                            turn[:, t, :], start=True, stop=True)
                last.then_inc(o_turned, 1)

            pe.wait_ge(made, 2)
            pe.wait_ge(oned, 1)
            pe.wait_ge(const, 48)
            for t in range(NT):
                last = nc.tensor.matmul(psB[:, 0, 0:E], ones[:, :], turn[:, t, P:W], start=(t == 0), stop=(t == NT - 1))
            last.then_inc(added_up, 1)

            def step(h, u, ahead, back, back2, back3):
                conv(h, u, range(0, 3))
                if back2:
                    turn_x1(h - 2, u)
                conv(h, u, range(3, 4))
                spread_in(0, h)
                conv(h, u, range(4, 6))
                if back2:
                    spread_in(1, h - 2)
                conv(h, u, range(6, NT))

            steady(pe, step)
            turn_x1(H - 2, 0)
            spread_in(1, H - 2, H)
            turn_x1(H - 1, 1)
            spread_in(1, H - 1, H)


def experts(nc, zT_d, z_d, logit_d, list_d, g_ffn, shared_w1, shared_w2, routed_w1, routed_w2, out,
            capacity, slots, H):
    D, F2 = shared_w1.shape[1:]
    F = F2 // 2
    E = routed_w1.shape[0]
    C, FC = D // P, F // P
    GE = 5
    M = slots // (2 * GE)
    TILES = E * 2 * GE
    GS = H // 2
    HALF = D // 2
    B = P // HD
    T = B * H * HD
    S = H * HD
    BITS = 30
    FIRST = 2 + 4
    SEARCH = 1 + (BITS - FIRST) // 8
    GR = 2 * SEARCH + 1
    assert slots == 2 * GE * M and M <= P and HALF <= BANK and GS % 2 == 0 and GS > GR + 8 and E % 2 == 1
    assert (BITS - FIRST) % 8 == 0 and E * H <= BANK

    o_rows = out[0:T, :].rearrange("(b h j) l -> h b j l", b=B, j=HD)

    with ExitStack() as ctx:
        m = Pool(nc, ctx, "moe")
        w1h = m.sb("w1h", [P, C, F2], F32R)
        w1l = m.sb("w1l", [P, C, F2], F32R)
        w2h = m.sb("w2h", [P, FC, D], F32R)
        w2l = m.sb("w2l", [P, FC, D], F32R)
        raw = m.sb("raw", [P, C * F2])
        raw1 = raw[:, :].rearrange("p (c f) -> p c f", c=C)
        raw2 = raw[:, 0:FC * D].rearrange("p (c n) -> p c n", c=FC)
        zin = [m.sb(f"zin{t}", [P, D]) for t in range(2)]
        zh = [m.sb(f"zh{u}", [P, C, 2 * P], F32R) for u in range(2)]
        zl = [m.sb(f"zl{u}", [P, C, 2 * P], F32R) for u in range(2)]
        act_s = [m.sb(f"act_s{j}", [P, 2 * P]) for j in range(2)]
        hid = [m.sb(f"hid{j}", [P, 2 * P]) for j in range(2)]
        hh = [m.sb(f"hh{u}", [P, FC, 2 * P], F32R) for u in range(2)]
        hl = [m.sb(f"hl{u}", [P, FC, 2 * P], F32R) for u in range(2)]
        y = [m.sb(f"y{t}", [P, D]) for t in range(2)]
        ident = m.sb("ident", [P, P])
        g = m.sb("g", [P, 1])
        tg = m.sb("tg", [P, 1])
        lists = m.sb("lists", [M, TILES, 2], I32)
        scale = m.sb("scale", [M, TILES])
        stage_i = [m.sb(f"stage_i{n}", [P, 1], I32) for n in range(2)]
        stage_p = [m.sb(f"stage_p{n}", [P, 2], I32) for n in range(2)]
        get_i = [m.sb(f"get_i{t}", [M, 1], I32) for t in range(2)]
        add_i = [m.sb(f"add_i{t}", [M, 1], I32) for t in range(2)]

        ps1 = [m.ps(f"ps1_{j}", [P, 2, 2 * P]) for j in range(2)]
        ps2 = [m.ps(f"ps2_{t}", [P, 2, BANK]) for t in range(2)]
        psT = m.ps("psT", [P, 2, BANK])

        aff = m.sb("aff", [P, E, H])
        score = m.sb("score", [P, E, H])
        token = m.sb("token", [P, H])
        spare = m.sb("spare", [P, H])
        base = m.sb("base", [P, E])
        thr = m.sb("thr", [P, E], I32)
        cand = m.sb("cand", [P, E], I32)
        bit = m.sb("bit", [P, E], I32)
        count = m.sb("count", [P, E])
        keep = m.sb("keep", [P, E])
        room = m.sb("room", [P, E])
        ones = m.sb("ones", [P, P])
        same = m.sb("same", [P, P])
        before = m.sb("before", [P, P])
        under = m.sb("under", [P, P])
        slot_of = m.sb("slot_of", [P, H, 2], I32)
        pay = m.sb("pay", [P, H, 2, 2], I32)

        def carve(area):
            at = [0]

            def piece(*shape):
                n = int(np.prod(shape))
                at[0] += n
                assert at[0] <= area.shape[1]
                flat = area[:, at[0] - n:at[0]]
                return flat if len(shape) == 1 else flat.rearrange("p (a b) -> p a b", a=shape[0])
            return piece

        early = [carve(a) for a in (y[0], y[1], act_s[0], act_s[1], hid[0])]
        logit, beat, itok, iexp = early[0](H, E), early[0](E, H), early[0](H), early[0](E)
        rank, row, col, rb, cb = early[1](E, H), *(early[1](P) for _ in range(4))
        irow, icol, ibat = (piece(P).bitcast(I32) for piece in early[2:])
        itok, iexp = itok.bitcast(I32), iexp.bitcast(I32)
        late = carve(raw[:, FC * D:])
        cmp = late(E, H)
        over = late(E, H)
        ties = late(E, H)
        scan = [late(E, H) for _ in range(2)]
        slot, slot_a, slot_b = (late(E, H) for _ in range(3))
        first, second, none, gap, weight = (late(H) for _ in range(5))
        psC = psT[:, 0, 0:E]
        psR = psT[:, 1, 0:E * H]

        const = m.sem("const")
        made = m.sem("made")
        gate = m.sem("gate")
        passed = m.sem("passed")
        logit_in = m.sem("logit_in")
        numbered = m.sem("numbered")
        negexp = m.sem("negexp")
        counted = m.sem("counted")
        rdone = m.sem("rdone")
        tallied = m.sem("tallied")
        ranked = m.sem("ranked")
        routed = m.sem("routed")
        w1_in = [m.sem(f"w1_in{j}") for j in range(FC)]
        w2_in = m.sem("w2_in")
        w1h_set, w1l_set = m.sem("w1h_set"), m.sem("w1l_set")
        w2h_set, w2l_set = m.sem("w2h_set"), m.sem("w2l_set")
        z_in = [m.sem(f"z_in{t}") for t in range(2)]
        z_got = [m.sem(f"z_got{t}") for t in range(2)]
        z_turned = m.sem("z_turned")
        zh_set, zl_set = m.sem("zh_set"), m.sem("zl_set")
        up = m.sem("up")
        silu = m.sem("silu")
        gated = m.sem("gated")
        hh_set, hl_set = m.sem("hh_set"), m.sem("hl_set")
        down = m.sem("down")
        y_set = m.sem("y_set")
        res_in = [m.sem(f"res_in{t}") for t in range(2)]
        stored = [m.sem(f"stored{t}") for t in range(2)]
        list_made = m.sem("list_made")
        list_init = m.sem("list_init")
        staged = m.sem("staged")
        scattered = [m.sem(f"scattered{n}") for n in range(2)]
        list_in = m.sem("list_in")
        scaled = m.sem("scaled")
        got = m.sem("got")
        put = m.sem("put")
        added = m.sem("added")
        y_free = m.sem("y_free")

        block = ctx.enter_context(nc.Block())

        def wait(eng, sem, value):
            if not (isinstance(value, int) and value <= 0):
                eng.wait_ge(sem, value)

        LAST = GS + E * GE
        BIG = float(1 << 22)
        SCORE_STEPS = 13 + 3 * (E - 1)
        BIT_STEPS = 6

        def schedule(eng, group, after_shared, after):
            group(0, 0, 0, 0, "shared", "shared")
            group(1, 1, 0, 1, "shared", "shared", [None, None, 0, 1])
            group(2, 0, 0, 2, "shared", "shared", [2, 3, 4, 5])
            with eng.Fori(1, SEARCH) as p:
                bit0 = (p - 1) * 8 + FIRST
                group(2 * p + 1, 1, 0, 3, "shared", "shared", [bit0 + j for j in range(4)])
                group(2 * p + 2, 0, 0, 4, "shared", "shared", [bit0 + (4 + j) for j in range(4)])
            group(GR, 1, 0, 3, "shared", "shared", ["compare", "scan ties", "scan ties on", "keep"])
            group(GR + 1, 0, 0, 4, "shared", "shared", ["scan kept", "scan kept on", "number", "first"])
            group(GR + 2, 1, 0, 3, "shared", "shared", ["second", "weigh", "no second", "no first"])
            group(GR + 3, 0, 0, 4, "shared", "shared")
            with eng.Fori(GR // 2 + 2, GS // 2 - 1) as p:
                group(2 * p + 1, 1, 0, 3, "shared", "shared")
                group(2 * p + 2, 0, 0, 4, "shared", "shared")
            group(GS - 1, 1, 0, GS - 1, "shared", "routed")
            after_shared()

            def expert(n, k0, u0, last):
                for i in range(GE):
                    group(k0 + i, (u0 + i) % 2, n, i, "routed", None if last and i == GE - 1 else "routed")
                after(n, k0 + GE - 1, (u0 + GE - 1) % 2, last)

            with eng.Fori(0, E // 2) as q:
                expert(2 * q + 1, 2 * GE * q + GS, 0, False)
                expert(2 * q + 2, 2 * GE * q + (GS + GE), 1, False)
            expert(E, GS + GE * (E - 1), 0, True)

        def block_cols(j, b):
            return slice(b * F + j * P, b * F + (j + 1) * P)

        def width(kind):
            return P if kind == "shared" else M

        @block.sync
        def _(sp):
            def load_w1(n, src):
                wait(sp, w2h_set, FC * n)
                wait(sp, w2l_set, FC * n)
                for j in range(FC):
                    load_pair(j, src)

            def load_pair(j, src):
                for b in range(2):
                    sp.dma_start(raw1[:, :, block_cols(j, b)],
                                 src[:, block_cols(j, b)].rearrange("(c p) f -> p c f", p=P)).then_inc(w1_in[j], 16)

            def load_w2(n, src):
                sp.wait_ge(w1h_set, 2 * FC * (n + 1))
                sp.wait_ge(w1l_set, 2 * FC * (n + 1))
                sp.dma_start(raw2, src.rearrange("(c p) n -> p c n", p=P)).then_inc(w2_in, 16)

            def load_z(k):
                for t in range(2):
                    wait(sp, zh_set, 2 * k + t - 1)
                    wait(sp, zl_set, 2 * k + t - 1)
                    sp.dma_start(zin[t][:, :], zT_d[2 * k + t].rearrange("p c n -> p (c n)")).then_inc(z_in[t], 16)

            def residual(k):
                for t in range(2):
                    wait(sp, stored[t], 16 * k)
                    sp.dma_start(y[t][:, :], o_rows[2 * k + t]).then_inc(res_in[t], 16)

            def store(k):
                for t in range(2):
                    sp.wait_ge(y_set, 4 * k + 2 * t + 2)
                    sp.dma_start(o_rows[2 * k + t], y[t][:, :]).then_inc(stored[t], 16)

            sp.dma_start(logit, logit_d).then_inc(logit_in, 16)
            sp.dma_start(g[:, :], g_ffn.rearrange("(a e) -> a e", a=1).to_broadcast([P, 1])).then_inc(const, 16)
            load_z(0)
            load_w1(0, shared_w1[0])
            sp.wait_ge(list_made, 2)
            sp.dma_start(list_d[0:E * slots, :].rearrange("(r q) c -> q r c", q=M), lists[:, :, :]).then_inc(list_init, 16)
            load_w2(0, shared_w2[0])
            load_z(1)
            sp.wait_ge(rdone, SCORE_STEPS)
            residual(0)
            load_z(2)

            def shared_rows(k):
                load_z(k + 2)
                store(k - 1)
                residual(k)

            with sp.Fori(1, GR + 4) as k:
                shared_rows(k)
            sp.wait_ge(routed, 1)
            for j in range(FC):
                load_pair(j, routed_w1[0])
                shared_rows(GR + 4 + j)
            with sp.Fori(GR + 4 + FC, GS - 2) as k:
                shared_rows(k)
            store(GS - 3)
            residual(GS - 2)
            store(GS - 2)
            residual(GS - 1)
            store(GS - 1)
            for t in range(2):
                sp.wait_ge(stored[t], 16 * GS)
                sp.sem_inc(y_free, 1)
            load_w2(1, routed_w2[0])
            with sp.Fori(2, E + 1) as n:
                load_w1(n, routed_w1[n - 1])
                load_w2(n, routed_w2[n - 1])

        @block.gpsimd
        def _(pool):
            for number, pattern, base_, up_ in ((irow, [[0, P]], 0, 1), (icol, [[1, P]], 0, 0),
                                               (itok, [[HD, H]], 0, 1), (iexp, [[slots, E]], 0, 0)):
                nc.gpsimd.iota(number, pattern, base=base_, channel_multiplier=up_).then_inc(numbered, 1)
            identity_steps(nc, pool, ident, made)
            nc.gpsimd.iota(lists[:, :, 0], [[0, TILES]], base=T, channel_multiplier=1).then_inc(list_made, 1)
            nc.gpsimd.memset(lists[:, :, 1], 0).then_inc(list_made, 1)
            pool.wait_ge(list_init, 16)
            pool.wait_ge(routed, 1)

            def scatter_column(h):
                for n in range(2):
                    nc.gpsimd.tensor_copy(stage_i[n][:, :], slot_of[:, bass.ds(h, 1), n:n + 1].rearrange("p a b -> p (a b)")).then_inc(staged, 1)
                    nc.gpsimd.tensor_copy(stage_p[n][:, :], pay[:, bass.ds(h, 1), n, :].rearrange("p a b -> p (a b)")).then_inc(staged, 1)
                    pool.wait_ge(staged, h * 4 + (2 * n + 2))
                    pool.sem_inc(passed, 1)
                    wait(pool, scattered[1 - n], h * 16 + 16 * n)
                    pool.sem_inc(passed, 1)
                    nc.gpsimd.indirect_dma_start(list_d, bass.IndirectOffsetOnAxis(stage_i[n][:, 0:1], 0),
                                                 stage_p[n][:, :], None).then_inc(scattered[n], 16)

            scatter_column(0)
            with pool.Fori(1, H) as h:
                scatter_column(h)
            pool.wait_ge(scattered[0], 16 * H)
            pool.wait_ge(scattered[1], 16 * H)
            pool.dma_start(lists[:, :, :], list_d[0:E * slots, :].rearrange("(r q) c -> q r c", q=M)).then_inc(list_in, 16)
            pool.wait_ge(list_in, 16)

            def gather(k):
                r = k - GS
                for t in range(2):
                    pool.wait_ge(zh_set, 2 * k + t - 1)
                    pool.wait_ge(zl_set, 2 * k + t - 1)
                    nc.gpsimd.tensor_copy(get_i[t][:, :], lists[:, bass.ds(2 * r + t, 1), 0]).then_inc(got, 1)
                    pool.wait_ge(got, 2 * r + (t + 1))
                    pool.sem_inc(passed, 1)
                    nc.gpsimd.indirect_dma_start(zin[t][0:M, :], None, z_d,
                                                 bass.IndirectOffsetOnAxis(get_i[t][:, 0:1], 0)).then_inc(z_got[t], 16)

            def scatter(k):
                r = k - GS
                for t in range(2):
                    pool.wait_ge(y_set, 4 * k + (2 * t + 2))
                    nc.gpsimd.tensor_copy(add_i[t][:, :], lists[:, bass.ds(2 * r + t, 1), 0]).then_inc(put, 1)
                    pool.wait_ge(put, 2 * r + (t + 1))
                    pool.sem_inc(passed, 1)
                    nc.gpsimd.indirect_dma_start(out, bass.IndirectOffsetOnAxis(add_i[t][:, 0:1], 0),
                                                 y[t][0:M, :], None, compute_op=ALU.add).then_inc(added, 16)
                    pool.wait_ge(added, 16 * (2 * r + (t + 1)))
                    pool.sem_inc(y_free, 1)

            for k in range(GS, GS + 4):
                gather(k)
                if k == GS + 2:
                    for t in range(2):
                        pool.wait_ge(stored[t], 16 * GS)
                if k == GS + 3:
                    scatter(GS)
            with pool.Fori(GS + 1, LAST - 3) as k:
                gather(k + 3)
                scatter(k)
            for k in range(LAST - 3, LAST):
                scatter(k)

        @block.scalar
        def _(act):
            act.wait_ge(const, 16)
            nc.scalar.activation(tg[:, :], g[:, :], ACT.Tanh).then_inc(gate, 1)
            act.wait_ge(logit_in, 16)
            nc.scalar.activation(aff[:, :, :], logit.rearrange("p h e -> p e h"), ACT.Exp,
                                 scale=-1.0).then_inc(negexp, 1)

            def w1_high(n):
                for j in range(FC):
                    act.wait_ge(w1_in[j], 32 * (n + 1))
                    for b in range(2):
                        nc.scalar.activation(w1h[:, :, block_cols(j, b)], raw1[:, :, block_cols(j, b)],
                                             ACT.Copy).then_inc(w1h_set, 1)

            def w2_high(n, c, k):
                if c == 0:
                    act.wait_ge(w2_in, 16 * (n + 1))
                    wait(act, down, 4 * k)
                nc.scalar.activation(w2h[:, c, :], raw2[:, c, :], ACT.Copy).then_inc(w2h_set, 1)

            def split(k, u, t, kind):
                w = width(kind)
                wait(act, up, FC * (k - 1))
                if kind == "shared":
                    act.wait_ge(z_in[t], 16 * (k + 1))
                    nc.scalar.activation(zh[u][:, :, t * w:(t + 1) * w],
                                         zin[t][:, :].rearrange("p (c n) -> p c n", c=C), ACT.Copy).then_inc(zh_set, 1)
                else:
                    act.wait_ge(z_turned, 2 * (k - GS) + (t + 1))
                    nc.scalar.activation(zh[u][:, :, t * w:(t + 1) * w].rearrange("p (b c) n -> p b c n", b=2),
                                         psT[:, :, 0:C // 2 * w].rearrange("p b (c n) -> p b c n", n=w),
                                         ACT.Copy).then_inc(zh_set, 1)

            def swish(k, j, w):
                act.wait_ge(up, FC * k + (j + 1))
                wait(act, gated, FC * k + (j - 1))
                nc.scalar.activation(act_s[j % 2][:, 0:2 * w], ps1[j % 2][:, 1, 0:2 * w], ACT.Silu).then_inc(silu, 1)

            def high(k, u, j, w):
                act.wait_ge(gated, FC * k + (j + 1))
                wait(act, down, 4 * (k - 1))
                nc.scalar.activation(hh[u][:, j, 0:2 * w], hid[j % 2][:, 0:2 * w], ACT.Copy).then_inc(hh_set, 1)

            def group(k, u, n, i, kind, next_kind, places=()):
                w = width(kind)
                swish(k, 0, w)
                if next_kind:
                    split(k + 1, 1 - u, 0, next_kind)
                high(k, u, 0, w)
                first = isinstance(i, int) and i == 0
                if first:
                    w2_high(n, 0, k)
                swish(k, 1, w)
                high(k, u, 1, w)
                if first:
                    w2_high(n, 1, k)
                swish(k, 2, w)
                if next_kind:
                    split(k + 1, 1 - u, 1, next_kind)
                high(k, u, 2, w)
                if first:
                    w2_high(n, 2, k)
                swish(k, 3, w)
                high(k, u, 3, w)
                if first:
                    w2_high(n, 3, k)

            def after_shared():
                act.wait_ge(up, FC * GS)
                w1_high(1)

            def after(n, k, u, last):
                if not last:
                    act.wait_ge(up, FC * (k + 1))
                    w1_high(n + 1)

            split(0, 0, 0, "shared")
            split(0, 0, 1, "shared")
            w1_high(0)
            schedule(act, group, after_shared, after)

        @block.vector
        def _(dve):
            v = nc.vector
            done = [0]

            def link(ins):
                done[0] += 1
                ins.then_inc(rdone, 1)
                dve.wait_ge(rdone, done[0])

            def make_scores():
                dve.wait_ge(numbered, 4)
                v.memset(ones[:, :], 1.0)
                v.memset(thr[:, :], 0)
                v.memset(bit[:, :], 1 << (BITS - 1))
                v.tensor_copy(row, irow)
                v.tensor_copy(col, icol)
                v.tensor_copy(token[:, :], itok)
                v.tensor_copy(base[:, :], iexp)
                v.tensor_scalar(spare[:, :], itok[:, 0:1].to_broadcast([P, H]), float(E * slots), None, ALU.add)
                link(v.tensor_scalar(ibat, irow, 3, None, ALU.logical_shift_right))
                link(v.tensor_copy(rb, ibat))
                link(v.tensor_scalar(ibat, icol, 3, None, ALU.logical_shift_right))
                link(v.tensor_copy(cb, ibat))
                link(v.scalar_tensor_tensor(out=token[:, :], in0=rb[:, 0:H], scalar=float(S - HD),
                                            in1=token[:, :], op0=ALU.mult, op1=ALU.add))
                v.tensor_tensor(same[:, :], rb, cb, ALU.is_equal)
                v.tensor_tensor(before[:, :], rb, cb, ALU.is_lt)
                link(v.tensor_tensor(under[:, :], row, col, ALU.is_lt))
                link(v.tensor_tensor(under[:, :], under[:, :], same[:, :], ALU.mult))
                dve.wait_ge(negexp, 1)
                link(v.tensor_scalar(aff[:, :, :], aff[:, :, :], 1.0, None, ALU.add))
                link(v.reciprocal(aff[:, :, :], aff[:, :, :]))
                link(v.memset(rank, 0.0))
                for d in range(1, E):
                    lower, upper = slice(0, E - d), slice(d, E)
                    link(v.tensor_tensor(beat[:, lower, :], aff[:, lower, :], aff[:, upper, :], ALU.is_ge))
                    link(v.tensor_tensor(rank[:, upper, :], rank[:, upper, :], beat[:, lower, :], ALU.add))
                    link(v.scalar_tensor_tensor(out=rank[:, lower, :].rearrange("p e h -> p (e h)"),
                                                in0=rank[:, lower, :].rearrange("p e h -> p (e h)"), scalar=1.0,
                                                in1=beat[:, lower, :].rearrange("p e h -> p (e h)"),
                                                op0=ALU.add, op1=ALU.subtract))
                link(v.tensor_scalar(rank, rank, 2.0, None, ALU.is_lt))
                link(v.tensor_tensor(score[:, :, :], aff[:, :, :], rank, ALU.mult))
                link(v.scalar_tensor_tensor(out=score[:, :, :], in0=rank, scalar=-1.0, in1=score[:, :, :],
                                            op0=ALU.add, op1=ALU.add))
                assert done[0] == SCORE_STEPS

            def find_bit(i):
                def step(ins, n):
                    ins.then_inc(rdone, 1)
                    dve.wait_ge(rdone, i * BIT_STEPS + (SCORE_STEPS + n))

                step(v.tensor_tensor(cand[:, :], thr[:, :], bit[:, :], ALU.bitwise_or), 1)
                step(v.tensor_tensor(cmp, score[:, :, :],
                                     cand[:, :].bitcast(F32).unsqueeze(2).to_broadcast([P, E, H]), ALU.is_ge), 2)
                v.tensor_reduce(count[:, :], cmp, AX.X, ALU.add).then_inc(counted, 1)
                step(v.tensor_scalar(bit[:, :], bit[:, :], 1, None, ALU.logical_shift_right), 3)
                dve.wait_ge(tallied, i + 1)
                step(v.scalar_tensor_tensor(out=keep[:, :], in0=psC, scalar=float(capacity),
                                            in1=cand[:, :].bitcast(F32), op0=ALU.is_ge, op1=ALU.mult), 4)
                step(v.tensor_tensor(keep[:, :], keep[:, :], thr[:, :].bitcast(F32), ALU.max), 5)
                step(v.tensor_copy(thr[:, :].bitcast(F32), keep[:, :]), BIT_STEPS)

            def scan_columns(what, strides):
                if strides[0] == 1:
                    link(v.tensor_copy(scan[0], what))
                for d in strides:
                    link(v.tensor_copy(scan[1], scan[0]))
                    link(v.tensor_tensor(scan[0][:, :, d:H], scan[1][:, :, d:H], scan[1][:, :, 0:H - d], ALU.add))

            def scan_ends(what):
                link(v.tensor_copy(scan[1], scan[0][:, :, H - 1:H].to_broadcast([P, E, H])))
                v.tensor_tensor(scan[0], scan[0], what, ALU.subtract).then_inc(counted, 1)

            def weigh(which, of, n):
                link(v.tensor_tensor(cmp, of, which.unsqueeze(1).to_broadcast([P, E, H]), ALU.is_equal))
                link(v.tensor_tensor(cmp, cmp, aff[:, :, :], ALU.mult))
                link(v.tensor_tensor(cmp, cmp, slot, ALU.mult))
                link(v.tensor_reduce(weight, cmp.rearrange("p e h -> p h e"), AX.X, ALU.add))
                link(v.tensor_copy(pay[:, :, n, 1].bitcast(F32), weight))

            def replace(which, n):
                link(v.tensor_tensor(gap, spare[:, :], which, ALU.subtract))
                link(v.tensor_tensor(gap, gap, none, ALU.mult))
                link(v.tensor_tensor(which, which, gap, ALU.add))
                link(v.tensor_copy(slot_of[:, :, n], which))
                link(v.tensor_copy(pay[:, :, n, 0], token[:, :]))

            rows = psR.rearrange("p (e h) -> p e h", e=E)
            strides = [1 << n for n in range((H - 1).bit_length())]
            split_at = len(strides) // 2

            def route(step):
                if step is None:
                    return
                if not isinstance(step, str):
                    find_bit(step)
                elif step == "compare":
                    done[0] = SCORE_STEPS + BIT_STEPS * BITS
                    limit = thr[:, :].bitcast(F32).unsqueeze(2).to_broadcast([P, E, H])
                    link(v.tensor_tensor(ties, score[:, :, :], limit, ALU.is_equal))
                    link(v.tensor_tensor(over, score[:, :, :], limit, ALU.is_gt))
                    v.tensor_reduce(count[:, :], over, AX.X, ALU.add).then_inc(counted, 1)
                elif step == "scan ties":
                    scan_columns(ties, strides[:split_at])
                elif step == "scan ties on":
                    dve.wait_ge(tallied, BITS + 1)
                    link(v.tensor_scalar(room[:, :], psC, -1.0, float(capacity), ALU.mult, ALU.add))
                    scan_columns(ties, strides[split_at:])
                    scan_ends(ties)
                elif step == "keep":
                    dve.wait_ge(ranked, 1)
                    link(v.tensor_tensor(cmp, rows, room[:, :].unsqueeze(2).to_broadcast([P, E, H]), ALU.is_lt))
                    link(v.tensor_tensor(cmp, cmp, ties, ALU.mult))
                    link(v.tensor_tensor(slot, cmp, over, ALU.add))
                elif step == "scan kept":
                    scan_columns(slot, strides[:split_at])
                elif step == "scan kept on":
                    scan_columns(slot, strides[split_at:])
                    scan_ends(slot)
                elif step == "number":
                    dve.wait_ge(ranked, 2)
                    link(v.tensor_tensor(slot_a, rows, base[:, :].unsqueeze(2).to_broadcast([P, E, H]), ALU.add))
                    link(v.tensor_scalar(slot_b, slot_a, -BIG, None, ALU.add))
                    link(v.tensor_tensor(slot_b, slot_b, slot, ALU.mult))
                    link(v.tensor_scalar(slot_b, slot_b, BIG, None, ALU.add))
                    link(v.tensor_reduce(first, slot_b.rearrange("p e h -> p h e"), AX.X, ALU.min))
                elif step == "first":
                    weigh(first, slot_b, 0)
                elif step == "second":
                    link(v.tensor_scalar(slot_a, slot_a, 1.0, None, ALU.add))
                    link(v.tensor_tensor(slot_a, slot_a, slot, ALU.mult))
                    link(v.tensor_reduce(second, slot_a.rearrange("p e h -> p h e"), AX.X, ALU.max))
                elif step == "weigh":
                    weigh(second, slot_a, 1)
                    link(v.tensor_scalar(second, second, -1.0, None, ALU.add))
                elif step == "no second":
                    link(v.tensor_tensor(none, second, first, ALU.is_le))
                    replace(second, 1)
                elif step == "no first":
                    link(v.tensor_scalar(none, first, BIG, None, ALU.is_equal))
                    replace(first, 0)
                    dve.sem_inc(routed, 1)

            def w1_low(n, q):
                dve.wait_ge(w1h_set, 2 * FC * n + (q + 1))
                cols = block_cols(q // 2, q % 2)
                nc.vector.tensor_tensor(w1l[:, :, cols], raw1[:, :, cols], w1h[:, :, cols].bitcast(F32),
                                        ALU.subtract).then_inc(w1l_set, 1)

            def w2_low(n, c):
                dve.wait_ge(w2h_set, FC * n + (c + 1))
                nc.vector.tensor_tensor(w2l[:, c, :], raw2[:, c, :], w2h[:, c, :].bitcast(F32),
                                        ALU.subtract).then_inc(w2l_set, 1)

            def split(k, u, t, kind):
                w = width(kind)
                dve.wait_ge(zh_set, 2 * k + (t + 1))
                if kind == "shared":
                    nc.vector.tensor_tensor(zl[u][:, :, t * w:(t + 1) * w],
                                            zin[t][:, :].rearrange("p (c n) -> p c n", c=C),
                                            zh[u][:, :, t * w:(t + 1) * w].bitcast(F32),
                                            ALU.subtract).then_inc(zl_set, 1)
                else:
                    nc.vector.tensor_tensor(zl[u][:, :, t * w:(t + 1) * w].rearrange("p (b c) n -> p b c n", b=2),
                                            psT[:, :, 0:C // 2 * w].rearrange("p b (c n) -> p b c n", n=w),
                                            zh[u][:, :, t * w:(t + 1) * w].rearrange("p (b c) n -> p b c n", b=2).bitcast(F32),
                                            ALU.subtract).then_inc(zl_set, 1)

            def gate_up(k, j, w):
                dve.wait_ge(silu, FC * k + (j + 1))
                wait(dve, hl_set, FC * k + (j - 1))
                nc.vector.tensor_tensor(hid[j % 2][:, 0:2 * w], ps1[j % 2][:, 0, 0:2 * w],
                                        act_s[j % 2][:, 0:2 * w], ALU.mult).then_inc(gated, 1)

            def low(k, u, j, w):
                dve.wait_ge(hh_set, FC * k + (j + 1))
                nc.vector.tensor_tensor(hl[u][:, j, 0:2 * w], hid[j % 2][:, 0:2 * w],
                                        hh[u][:, j, 0:2 * w].bitcast(F32), ALU.subtract).then_inc(hl_set, 1)

            def result(k, t, half, kind):
                dve.wait_ge(down, 4 * k + (2 * t + half + 1))
                cols = slice(half * HALF, (half + 1) * HALF)
                if kind == "shared":
                    dve.wait_ge(res_in[t], 16 * k + 16)
                    nc.vector.scalar_tensor_tensor(out=y[t][:, cols], in0=ps2[t][:, half, 0:HALF], scalar=tg[:, 0:1],
                                                   in1=y[t][:, cols], op0=ALU.mult, op1=ALU.add).then_inc(y_set, 1)
                else:
                    r = k - GS
                    dve.wait_ge(y_free, 2 * r + (t + 1))
                    nc.vector.tensor_scalar(y[t][0:M, cols], ps2[t][0:M, half, 0:HALF],
                                            scale[:, bass.ds(2 * r + t, 1)], None, ALU.mult).then_inc(y_set, 1)

            def results(k, kind, n, blocks):
                per = -(-len(blocks) // 4)
                for q in range(4):
                    for b in blocks[q * per:(q + 1) * per]:
                        w1_low(n, b)
                    result(k, q // 2, q % 2, kind)

            def group(k, u, n, i, kind, next_kind, places=()):
                w = width(kind)
                first = isinstance(i, int) and i == 0
                for j in range(FC):
                    gate_up(k, j, w)
                    if next_kind and j % 2 == 0:
                        split(k + 1, 1 - u, j // 2, next_kind)
                    low(k, u, j, w)
                    if first:
                        w2_low(n, j)
                    if places:
                        route(places[j])
                if not first:
                    turnover = next_kind == "routed" and (kind == "shared" or i == GE - 1)
                    results(k - 1, kind, n + 1, list(range(FC)) if turnover else [])

            def after_shared():
                results(GS - 1, "shared", 1, list(range(FC, 2 * FC)))
                dve.wait_ge(list_in, 16)
                nc.vector.tensor_scalar(scale[:, :], lists[:, :, 1].bitcast(F32), tg[0:M, 0:1], None,
                                        ALU.mult).then_inc(scaled, 1)
                dve.wait_ge(scaled, 1)

            def after(n, k, u, last):
                results(k, "routed", n + 1, [] if last else list(range(FC, 2 * FC)))

            make_scores()
            dve.wait_ge(gate, 1)
            w1_low(0, 0)
            w1_low(0, 1)
            split(0, 0, 0, "shared")
            split(0, 0, 1, "shared")
            for q in range(2, 2 * FC):
                w1_low(0, q)
            schedule(dve, group, after_shared, after)

        @block.tensor
        def _(pe):
            def turn(k, t):
                pe.wait_ge(z_got[t], 16 * (k - GS) + 16)
                pe.wait_ge(zh_set, 2 * k + t)
                pe.wait_ge(zl_set, 2 * k + t)
                for c in range(C):
                    cc = c % (C // 2)
                    last = nc.tensor.transpose(psT[:, c // (C // 2), cc * M:(cc + 1) * M],
                                               zin[t][0:M, c * P:(c + 1) * P], ident[0:M, 0:M])
                last.then_inc(z_turned, 1)

            def first_product(k, u, j, w):
                wait(pe, gated, FC * k + (j - 1))
                for b in range(2):
                    acc = ps1[j % 2][:, b, 0:2 * w]
                    cols = block_cols(j, b)
                    for c in range(C):
                        nc.tensor.matmul(acc, w1h[:, c, cols], zh[u][:, c, 0:2 * w], start=(c == 0), stop=False)
                        nc.tensor.matmul(acc, w1h[:, c, cols], zl[u][:, c, 0:2 * w], start=False, stop=False)
                        last = nc.tensor.matmul(acc, w1l[:, c, cols], zh[u][:, c, 0:2 * w],
                                                start=False, stop=(c == C - 1))
                last.then_inc(up, 1)

            def second_product(k, u, w, place=None):
                pe.wait_ge(hh_set, FC * k + FC)
                pe.wait_ge(hl_set, FC * k + FC)
                for t in range(2):
                    rows = slice(t * w, (t + 1) * w)
                    for half in range(2):
                        wait(pe, y_set, 4 * k - 4 + (2 * t + half + 1))
                        acc = ps2[t][0:w, half, 0:HALF]
                        cols = slice(half * HALF, (half + 1) * HALF)
                        for f in range(FC):
                            nc.tensor.matmul(acc, hh[u][:, f, rows], w2h[:, f, cols], start=(f == 0), stop=False)
                            nc.tensor.matmul(acc, hh[u][:, f, rows], w2l[:, f, cols], start=False, stop=False)
                            last = nc.tensor.matmul(acc, hl[u][:, f, rows], w2h[:, f, cols],
                                                    start=False, stop=(f == FC - 1))
                        last.then_inc(down, 1)
                    if t == 0:
                        sum_partitions(place)

            def tally():
                nc.tensor.matmul(psC, ones[:, :], count[:, :], start=True, stop=True).then_inc(tallied, 1)

            def rank_tokens(what):
                def flat(a):
                    return a.rearrange("p e h -> p (e h)")

                nc.tensor.matmul(psR, under[:, :], flat(what), start=True, stop=False)
                nc.tensor.matmul(psR, same[:, :], flat(scan[0]), start=False, stop=False)
                nc.tensor.matmul(psR, before[:, :], flat(scan[1]), start=False, stop=True).then_inc(ranked, 1)

            def sum_partitions(step):
                if step is not None and not isinstance(step, str):
                    pe.wait_ge(counted, step + 1)
                    tally()
                elif step == "compare":
                    pe.wait_ge(counted, BITS + 1)
                    tally()
                elif step == "scan ties on":
                    pe.wait_ge(counted, BITS + 2)
                    rank_tokens(ties)
                elif step == "scan kept on":
                    pe.wait_ge(counted, BITS + 3)
                    rank_tokens(slot)

            def group(k, u, n, i, kind, next_kind, places=()):
                w = width(kind)
                if next_kind == "routed" and kind == "shared":
                    pe.wait_ge(routed, 1)
                pe.wait_ge(zh_set, 2 * k + 2)
                pe.wait_ge(zl_set, 2 * k + 2)
                for j in range(FC):
                    if isinstance(i, int) and i == 0:
                        pe.wait_ge(w1h_set, 2 * FC * n + 2 * (j + 1))
                        pe.wait_ge(w1l_set, 2 * FC * n + 2 * (j + 1))
                    first_product(k, u, j, w)
                    if places and j > 0:
                        sum_partitions(places[j - 1])
                    if next_kind == "routed" and j % 2 == 0:
                        turn(k + 1, j // 2)
                if not (isinstance(i, int) and i == 0):
                    if i == 1:
                        pe.wait_ge(w2h_set, FC * n + FC)
                        pe.wait_ge(w2l_set, FC * n + FC)
                    second_product(k - 1, 1 - u, w, places[FC - 1] if places else None)

            def after_shared():
                second_product(GS - 1, 1, P)

            def after(n, k, u, last):
                second_product(k, u, M)

            pe.wait_ge(made, 2)
            schedule(pe, group, after_shared, after)


def build(nc, x, xT, cT, g_xattn, g_ffn, ssm_kernel, D, gate_w, expert_bias, shared_w1, shared_w2,
          routed_w1, routed_w2, out):
    B, S, L = x.shape
    H, T, E = S // HD, B * S, gate_w.shape[1]
    capacity = max(1, T // E)
    slots = -(-capacity // 10) * 10

    def scratch(name, shape, dt=F32):
        return nc.dram_tensor(name, shape, dt).ap()

    filt_hi, filt_lo = scratch("filt_hi", (H, PAD)), scratch("filt_lo", (H, PAD))
    z_d = scratch("z_d", (T + P, L))
    zT_d = scratch("zT_d", (H, P, L // P, P))
    logit_d = scratch("logit_d", (P, H, E))
    list_d = scratch("list_d", (E * slots + P, 2), I32)
    prepare_filters(nc, ssm_kernel, D, filt_hi, filt_lo, z_d, out)
    gated_conv(nc, x, xT, cT, g_xattn, gate_w, expert_bias, filt_hi, filt_lo, z_d, zT_d, logit_d, out)
    experts(nc, zT_d, z_d, logit_d, list_d, g_ffn, shared_w1, shared_w2, routed_w1, routed_w2,
            out, capacity, slots, H)


_INS = ["x", "xT", "cT", "g_xattn", "g_ffn", "L0_xattn_ssm_kernel", "L0_xattn_D", "L0_ffn_gate_w",
        "L0_ffn_expert_bias", "L0_ffn_shared_w1", "L0_ffn_shared_w2", "L0_ffn_routed_w1", "L0_ffn_routed_w2"]


def head_tiles(a):
    B, S, L = a.shape
    return a.reshape(B, S // HD, HD, L // P, P).transpose(1, 4, 3, 0, 2).reshape(S // HD, P, L // P, B * HD)


def kernel(**inputs):
    import concourse.bacc as bacc
    from concourse.bass_utils import run_bass_kernel_spmd

    nc = bacc.Bacc("TRN2", target_bir_lowering=False, num_devices=1)
    laid = {name: np.asarray(a) for name, a in inputs.items()}
    laid["xT"] = head_tiles(laid["x"])
    laid["cT"] = head_tiles(laid["ctx_2048"][:, :, ::-1])
    arrays, args = {}, []
    for name in _INS:
        a = np.ascontiguousarray(laid[name])
        arrays[f"in_{name}"] = a
        args.append(nc.dram_tensor(f"in_{name}", a.shape, mybir.dt.from_np(a.dtype), kind="ExternalInput").ap())
    B, S, L = laid["x"].shape
    out = nc.dram_tensor("out_0", (B * S + P, L), F32, kind="ExternalOutput").ap()
    build(nc, *args, out)
    r = run_bass_kernel_spmd(nc, [arrays], core_ids=[0])
    return np.ascontiguousarray(r.results[0]["out_0"][:B * S].reshape(B, S, L))
```
